# Optimizing a Trainium2 kernel written in Bass

```python
import numpy as np
import jax
import jax.numpy as jnp

def _softmax(x, axis=-1):
    return jax.nn.softmax(x, axis=axis)

def _gelu(x):
    return jax.nn.gelu(x, approximate=True)

def _silu(x):
    return jax.nn.silu(x)

def _sigmoid(x):
    return jax.nn.sigmoid(x)

def _layernorm(x, axis=-1, eps=1e-05):
    m = jnp.mean(x, axis=axis, keepdims=True)
    v = jnp.var(x, axis=axis, keepdims=True)
    return (x - m) / jnp.sqrt(v + eps)

def _scatter_add(tgt, idx, src, axis=0):
    return tgt.at[idx].add(src)

def _segment_sum(src, seg, n):
    return jax.ops.segment_sum(src, seg, n)
kernel_name = 'mk_early_fusion_d1_tok_img1024_r4_3ee89f'

def setup_inputs(seed: int=0):
    np.random.seed(seed)
    _w = jnp.asarray

    def _rec_inputs():
        import jax
        import jax.numpy as jnp
        _rk = jax.random.key(seed)
        x = -0.00016672 + 0.999947 * jax.random.normal(jax.random.fold_in(_rk, 1), (32, 3, 96, 96), jnp.float32)
        txt = 0.435037 + 1.14557 * jax.random.normal(jax.random.fold_in(_rk, 2), (32, 128, 256), jnp.float32)
        return (x, txt)
    x, txt = _rec_inputs()

    def _L0_tok_setup():
        import jax, jax.numpy as jnp
        import numpy as np
        PATCH = 16
        EPS = 1e-05

        def _patchify(img, p):
            B, C, H, W = img.shape
            h, w = (H // p, W // p)
            x = img.reshape(B, C, h, p, w, p)
            x = x.transpose(0, 2, 4, 1, 3, 5)
            return x.reshape(B, h, w, C * p * p)

        def _layernorm(x, gamma):
            mu = x.mean(axis=-1, keepdims=True)
            var = ((x - mu) ** 2).mean(axis=-1, keepdims=True)
            return (x - mu) * jax.lax.rsqrt(var + EPS) * gamma

        def _posemb_sincos_2d(h, w, dim, temperature=10000.0, dtype=jnp.float32):
            y, x = jnp.meshgrid(jnp.arange(h, dtype=dtype), jnp.arange(w, dtype=dtype), indexing='ij')
            omega = jnp.arange(dim // 4, dtype=dtype) / (dim // 4 - 1)
            omega = 1.0 / temperature ** omega
            y = y.reshape(-1)[:, None] * omega[None, :]
            x = x.reshape(-1)[:, None] * omega[None, :]
            return jnp.concatenate([jnp.sin(x), jnp.cos(x), jnp.sin(y), jnp.cos(y)], axis=1)
        key = jax.random.key(seed)
        k1, k2, k3, k4 = jax.random.split(key, 4)
        patch_dim = 3 * PATCH * PATCH
        dim = 256
        img = jax.random.normal(k1, (64, 3, 96, 96), dtype=jnp.float32)
        ln1_w = jax.random.uniform(k2, (patch_dim,), dtype=jnp.float32, minval=0.9, maxval=1.1)
        W = jax.random.normal(k3, (dim, patch_dim), dtype=jnp.float32) * 0.02
        ln2_w = jax.random.uniform(k4, (dim,), dtype=jnp.float32, minval=0.9, maxval=1.1)
        return {'img': img, 'ln1_w': ln1_w, 'W': W, 'ln2_w': ln2_w}
    _L0_tok_all = _L0_tok_setup()
    _L0_tok_in = {k: v for k, v in _L0_tok_all.items() if k in ('ln1_w', 'W', 'ln2_w')}
    del _L0_tok_all

    def _L0_attn_setup():
        import jax, jax.numpy as jnp
        import numpy as np
        EMB = 256
        HEADS = 16
        HEAD_DIM = EMB // HEADS
        MAX_LEN = 250
        key = jax.random.key(seed)
        ks = jax.random.split(key, 11)
        s = 0.02
        x = jax.random.normal(ks[0], (4, 256, EMB), dtype=jnp.float32)
        Wq = jax.random.normal(ks[1], (EMB, EMB), dtype=jnp.float32) * s
        bq = jnp.zeros((EMB,), dtype=jnp.float32)
        Wk = jax.random.normal(ks[2], (EMB, EMB), dtype=jnp.float32) * s
        bk = jnp.zeros((EMB,), dtype=jnp.float32)
        Wv = jax.random.normal(ks[3], (EMB, EMB), dtype=jnp.float32) * s
        bv = jnp.zeros((EMB,), dtype=jnp.float32)
        Wp = jax.random.normal(ks[4], (EMB, EMB), dtype=jnp.float32) * s
        bp = jnp.zeros((EMB,), dtype=jnp.float32)
        bias_table = jax.random.normal(ks[5], (2 * MAX_LEN - 1, HEADS), dtype=jnp.float32) * 0.02
        temperature = jnp.ones((1,), dtype=jnp.float32)
        return {'x': x, 'Wq': Wq, 'bq': bq, 'Wk': Wk, 'bk': bk, 'Wv': Wv, 'bv': bv, 'Wp': Wp, 'bp': bp, 'bias_table': bias_table, 'temperature': temperature}
    _L0_attn_all = _L0_attn_setup()
    _L0_attn_in = {k: v for k, v in _L0_attn_all.items() if k in ('Wq', 'bq', 'Wk', 'bk', 'Wv', 'bv', 'Wp', 'bp', 'bias_table', 'temperature')}
    del _L0_attn_all

    def _L0_ffn_setup():
        import jax, jax.numpy as jnp
        import numpy as np
        E, K = (8, 2)
        DM, DE = (256, 704)
        B, S = (1, 512)
        EPS = 1e-06

        def _rmsnorm(x, w):
            var = jnp.mean(jnp.square(x), axis=-1, keepdims=True)
            return x * jax.lax.rsqrt(var + EPS) * w
        key = jax.random.key(seed)
        kx, kg, k1, k2, k3 = jax.random.split(key, 5)

        def kaiming_uniform(k, shape, fan_in):
            bound = 1.0 / np.sqrt(fan_in)
            return jax.random.uniform(k, shape, jnp.float32, -bound, bound)
        return {'x': jax.random.normal(kx, (B, S, DM), jnp.float32), 'gate_w': kaiming_uniform(kg, (E, DM), DM), 'rms_w': jnp.ones((DM,), jnp.float32), 'W1': kaiming_uniform(k1, (E, DE, DM), DE * DM), 'W2': kaiming_uniform(k2, (E, DE, DM), DE * DM), 'W3': kaiming_uniform(k3, (E, DM, DE), DM * DE)}
    _L0_ffn_all = _L0_ffn_setup()
    _L0_ffn_in = {k: v for k, v in _L0_ffn_all.items() if k in ('gate_w', 'rms_w', 'W1', 'W2', 'W3')}
    del _L0_ffn_all
    return {'x': x, 'txt': txt, 'L0_tok_ln1_w': _L0_tok_in['ln1_w'], 'L0_tok_W': _L0_tok_in['W'], 'L0_tok_ln2_w': _L0_tok_in['ln2_w'], 'L0_attn_Wq': _L0_attn_in['Wq'], 'L0_attn_bq': _L0_attn_in['bq'], 'L0_attn_Wk': _L0_attn_in['Wk'], 'L0_attn_bk': _L0_attn_in['bk'], 'L0_attn_Wv': _L0_attn_in['Wv'], 'L0_attn_bv': _L0_attn_in['bv'], 'L0_attn_Wp': _L0_attn_in['Wp'], 'L0_attn_bp': _L0_attn_in['bp'], 'L0_attn_bias_table': _L0_attn_in['bias_table'], 'L0_attn_temperature': _L0_attn_in['temperature'], 'L0_ffn_gate_w': _L0_ffn_in['gate_w'], 'L0_ffn_rms_w': _L0_ffn_in['rms_w'], 'L0_ffn_W1': _L0_ffn_in['W1'], 'L0_ffn_W2': _L0_ffn_in['W2'], 'L0_ffn_W3': _L0_ffn_in['W3']}

def reference(x, txt, L0_tok_ln1_w, L0_tok_W, L0_tok_ln2_w, L0_attn_Wq, L0_attn_bq, L0_attn_Wk, L0_attn_bk, L0_attn_Wv, L0_attn_bv, L0_attn_Wp, L0_attn_bp, L0_attn_bias_table, L0_attn_temperature, L0_ffn_gate_w, L0_ffn_rms_w, L0_ffn_W1, L0_ffn_W2, L0_ffn_W3):
    import jax
    import jax.numpy as jnp

    def _L0_tok_ref(img, ln1_w, W, ln2_w):
        import jax, jax.numpy as jnp
        import numpy as np
        PATCH = 16
        EPS = 1e-05

        def _patchify(img, p):
            B, C, H, W = img.shape
            h, w = (H // p, W // p)
            x = img.reshape(B, C, h, p, w, p)
            x = x.transpose(0, 2, 4, 1, 3, 5)
            return x.reshape(B, h, w, C * p * p)

        def _layernorm(x, gamma):
            mu = x.mean(axis=-1, keepdims=True)
            var = ((x - mu) ** 2).mean(axis=-1, keepdims=True)
            return (x - mu) * jax.lax.rsqrt(var + EPS) * gamma

        def _posemb_sincos_2d(h, w, dim, temperature=10000.0, dtype=jnp.float32):
            y, x = jnp.meshgrid(jnp.arange(h, dtype=dtype), jnp.arange(w, dtype=dtype), indexing='ij')
            omega = jnp.arange(dim // 4, dtype=dtype) / (dim // 4 - 1)
            omega = 1.0 / temperature ** omega
            y = y.reshape(-1)[:, None] * omega[None, :]
            x = x.reshape(-1)[:, None] * omega[None, :]
            return jnp.concatenate([jnp.sin(x), jnp.cos(x), jnp.sin(y), jnp.cos(y)], axis=1)
        patches = _patchify(img, PATCH)
        B, h, w, d = patches.shape
        x = patches.reshape(B, h * w, d)
        x = _layernorm(x, ln1_w)
        x = jnp.einsum('bnd,ed->bne', x, W)
        x = _layernorm(x, ln2_w)
        pe = _posemb_sincos_2d(h, w, x.shape[-1], dtype=x.dtype)
        return x + pe[None, :, :]

    def _L0_attn_ref(x, Wq, bq, Wk, bk, Wv, bv, Wp, bp, bias_table, temperature):
        import jax, jax.numpy as jnp
        import numpy as np
        EMB = 256
        HEADS = 16
        HEAD_DIM = EMB // HEADS
        MAX_LEN = 250
        B, N, C = x.shape
        H, D = (HEADS, C // HEADS)

        def split_heads(t):
            return t.reshape(B, N, H, D).transpose(0, 2, 1, 3)
        q = split_heads(x @ Wq + bq)
        k = split_heads(x @ Wk + bk)
        v = split_heads(x @ Wv + bv)
        energy = jnp.einsum('bhqd,bhkd->bhqk', q, k)
        pos = jnp.arange(N)
        rel = pos[:, None] - pos[None, :] + (N - 1)
        rel = jnp.clip(rel, 0, bias_table.shape[0] - 1)
        bias = bias_table[rel].transpose(2, 0, 1)
        energy = energy + bias[None]
        scaling = jnp.sqrt(jnp.float32(C))
        temp = jnp.clip(temperature[0], 0.1, 10.0)
        att = jax.nn.softmax(energy / (scaling * temp), axis=-1)
        out = jnp.einsum('bhqk,bhkd->bhqd', att, v)
        out = out.transpose(0, 2, 1, 3).reshape(B, N, C)
        return out @ Wp + bp

    def _L0_ffn_ref(x, gate_w, rms_w, W1, W2, W3):
        import jax, jax.numpy as jnp
        import numpy as np
        E, K = (8, 2)
        DM, DE = (256, 704)
        B, S = (1, 512)
        EPS = 1e-06

        def _rmsnorm(x, w):
            var = jnp.mean(jnp.square(x), axis=-1, keepdims=True)
            return x * jax.lax.rsqrt(var + EPS) * w
        y = _rmsnorm(x, rms_w)
        logits = jnp.einsum('bsd,ed->bse', y, gate_w)
        vals, idx = jax.lax.top_k(logits, K)
        w = jax.nn.softmax(vals, axis=-1)
        w_full = jnp.einsum('bsk,bske->bse', w, jax.nn.one_hot(idx, E, dtype=x.dtype))
        up = jnp.einsum('bsd,end->bsen', y, W1)
        gate = jnp.einsum('bsd,end->bsen', y, W2)
        h = jax.nn.silu(up) * gate
        out = jnp.einsum('bsen,emn->bsem', h, W3)
        comb = jnp.einsum('bsem,bse->bsm', out, w_full)
        return x + comb
    h = _L0_tok_ref(x, L0_tok_ln1_w, L0_tok_W, L0_tok_ln2_w)
    h = jnp.concatenate([h, txt], axis=1)
    h = h + _L0_attn_ref(_layernorm(h, axis=-1), L0_attn_Wq, L0_attn_bq, L0_attn_Wk, L0_attn_bk, L0_attn_Wv, L0_attn_bv, L0_attn_Wp, L0_attn_bp, L0_attn_bias_table, L0_attn_temperature)
    h = h + _L0_ffn_ref(_layernorm(h, axis=-1), L0_ffn_gate_w, L0_ffn_rms_w, L0_ffn_W1, L0_ffn_W2, L0_ffn_W3)
    return h

_drawn_inputs = setup_inputs


def setup_inputs(seed=0):
    import zlib

    import numpy as np

    out = dict(_drawn_inputs(seed))
    spreads = {'L0_attn_bq': (0.0, 0.8),
     'L0_attn_bk': (0.0, 2.0),
     'L0_attn_bv': (0.0, 0.288),
     'L0_attn_bp': (0.0, 0.1),
     'L0_ffn_rms_w': (1.0, 0.6)}
    factors = {'L0_attn_Wq': 8.0,
     'L0_attn_Wk': 8.0,
     'L0_attn_Wv': 5.888,
     'L0_attn_bias_table': 64.0,
     'L0_ffn_gate_w': 64.0,
     'L0_ffn_W1': 64.0,
     'L0_ffn_W2': 64.0,
     'L0_ffn_W3': 64.0}
    for name, (base, spread) in spreads.items():
        noise = np.random.default_rng([zlib.crc32(name.encode()), seed]).standard_normal(out[name].shape)
        drawn = base * np.exp(spread * noise) if base else spread * noise
        out[name] = jnp.asarray(drawn.astype(out[name].dtype))
    for name, factor in factors.items():
        out[name] = (out[name] * factor).astype(out[name].dtype)
    return out
```

```python
import numpy as np
import concourse.bass as bass
from concourse import mybir
from contextlib import ExitStack

BATCH, CHANS, IMG, PATCH = 32, 3, 96, 16
SIDE = IMG // PATCH
NI = SIDE * SIDE
NT = 128
SEQ = NI + NT
TOK = BATCH * SEQ
DM = 256
FEAT = CHANS * PATCH * PATCH
HEADS, HD = 16, 16
PAIRS = HEADS // 2
P = 128
KC = DM // P
FC = FEAT // P
IT = BATCH * NI // P
TT = TOK // P
EXPERTS, DE = 8, 704
TABLE = 499
QS = NT + 64
VW = 3 * HD + 1

FT = 512
ETILES = (2 * TOK + EXPERTS * (FT - 1)) // FT
SLOTS = ETILES * FT
MC = DE // P
MR = DE - MC * P
UPC = 2 * MC + 1

ISLANDS = 4


def build(nc, A, stop=9):
    f32, bf16, fp16, i32 = mybir.dt.float32, mybir.dt.bfloat16, mybir.dt.float16, mybir.dt.int32
    ALU, ACT, AX = mybir.AluOpType, mybir.ActivationFunctionType, mybir.AxisListType

    outer = ExitStack()
    with outer:
        def dram(name, shape, dt=f32):
            return nc.dram_tensor(name, shape, dt, kind="Internal").ap()

        h0_img = dram("h0_img", (BATCH * NI, DM))
        xn_img = dram("xn_img", (BATCH * NI, DM))
        xn_txt = dram("xn_txt", (BATCH * NT, DM))
        h1_d = dram("h1_d", (TOK, DM))
        y_slots = dram("y_slots", (SLOTS, DM))
        o_slots = dram("o_slots", (SLOTS, DM))

        def tools(ctx):
            def sb(name, shape, dt=f32):
                return ctx.enter_context(nc.sbuf_tensor(name, shape, dt))

            def bank(name):
                return ctx.enter_context(nc.psum_tensor(name, [P, 512], f32))

            def sem(name):
                return ctx.enter_context(nc.semaphore(name))
            return sb, bank, sem

        sbo, _, semo = tools(outer)
        ident = sbo("ident", [P, P])

        tokenise(nc, A, locals())
        if stop < 2:
            return
        attention(nc, A, locals())
        if stop < 3:
            return
        experts(nc, A, locals(), stop)


def tokenise(nc, A, G):
    f32, ALU, ACT = mybir.dt.float32, mybir.AluOpType, mybir.ActivationFunctionType
    ident, h0_img, xn_img, xn_txt, y_slots = (G[k] for k in ("ident", "h0_img", "xn_img", "xn_txt", "y_slots"))
    eps = 1e-5
    with ExitStack() as ctx:
        sb, bank, sem = G["tools"](ctx)
        px = sb("px", [P, IT, FEAT])
        wt = sb("wt", [P, FC, DM])
        ln1 = sb("ln1", [P, FC])
        ln2 = sb("ln2", [P, DM])
        pe_t = sb("pe_t", [P, IT, DM])
        xT = sb("xT", [P, 2, FC, P])
        z = sb("z", [P, IT, DM])
        xo = sb("xo", [P, IT, DM])
        st1 = sb("st1", [P, IT, 2, 6])
        mv1 = sb("mv1", [P, IT, 2])
        st2 = sb("st2", [P, IT, 6])
        mv2 = sb("mv2", [P, IT, 2])
        st3 = sb("st3", [P, IT, 6])
        mv3 = sb("mv3", [P, IT, 2])
        rs = sb("rs", [P, 4, IT])
        tx = sb("tx", [P, 2, ISLANDS, DM])
        tst = sb("tst", [P, 2, ISLANDS, 6])
        tmv = sb("tmv", [P, 2, ISLANDS, 2])
        trs = sb("trs", [P, 2, 2, ISLANDS])
        zeros = sb("zeros", [P, 1024])
        bt = [bank(f"bt{i}") for i in range(4)]
        bz = [bank(f"bz{i}") for i in range(2)]

        s_zero, s_ident = sem("s_zero"), sem("s_ident")
        s_fill = sem("s_fill")
        s_px = [sem(f"s_px{t}") for t in range(IT)]
        s_w, s_wl = sem("s_w"), sem("s_wl")
        s_mv1, s_std1, s_rs1, s_n1 = sem("s_mv1"), sem("s_std1"), sem("s_rs1"), sem("s_n1")
        s_xTp, s_xTs, s_z = sem("s_xTp"), sem("s_xTs"), sem("s_z")
        s_zc, s_st = sem("s_zc"), sem("s_st")
        s_v2, s_std2, s_rs2, s_n2, s_n2b, s_h0 = (sem(x) for x in ("s_v2", "s_std2", "s_rs2", "s_n2", "s_n2b", "s_h0"))
        s_v3, s_std3, s_rs3, s_n3 = (sem(x) for x in ("s_v3", "s_std3", "s_rs3", "s_n3"))
        s_out = sem("s_out1")
        s_tx = [sem("s_tx0"), sem("s_tx1")]
        s_tst, s_tmv, s_tv, s_tstd, s_trs, s_tn = (sem(x) for x in ("s_tst", "s_tmv", "s_tv", "s_tstd", "s_trs", "s_tn"))
        s_tout = [sem("s_tout0"), sem("s_tout1")]
        s_t1, s_teps = sem("s_t1"), sem("s_teps")
        GROUPS = BATCH // ISLANDS
        x_txt = A["txt"].rearrange("b t c -> (b t) c")
        FILLS = SLOTS * DM // (P * 1024)
        fill_rows = y_slots.rearrange("(p r) c -> p (r c)", p=P)

        with nc.Block() as block:
            @block.sync
            def _(sp):
                for t in range(IT):
                    sp.dma_start(px[:, t, :], A["patches"][t * P:(t + 1) * P, :]).then_inc(s_px[t], 16)
                sp.dma_start(ln1[:, :], A["ln1_w"]).then_inc(s_w, 16)
                sp.dma_start(wt[:, :, :], A["tokW"].rearrange("(c p) n -> p c n", p=P)).then_inc(s_w, 16)
                sp.dma_start(ln2[:, :], A["ln2_w"]).then_inc(s_w, 16)
                sp.dma_start(pe_t[:, :, :], A["pos"].rearrange("(t p) n -> p t n", p=P)).then_inc(s_w, 16)
                for j in range(2):
                    sp.sem_inc(s_tout[j], 16)
                with sp.Fori(0, GROUPS // 2) as i:
                    for j in range(2):
                        rows = bass.ds((2 * i + j) * ISLANDS * P, ISLANDS * P)
                        wait_alone(sp, s_tout[j], 16 + i * 16, s_zero)
                        sp.dma_start(tx[:, j, :, :], x_txt[rows, :].rearrange("(t p) n -> p t n", p=P))\
                            .then_inc(s_tx[j], 16)
                    for j in range(2):
                        rows = bass.ds((2 * i + j) * ISLANDS * P, ISLANDS * P)
                        wait_alone(sp, s_tn, 2 * i + j + 1, s_zero)
                        sp.dma_start(xn_txt[rows, :].rearrange("(t p) n -> p t n", p=P), tx[:, j, :, :])\
                            .then_inc(s_tout[j], 16)
                sp.wait_ge(s_zero, 1)
                with sp.Fori(0, FILLS) as i:
                    sp.dma_start(fill_rows[:, bass.ds(i * 1024, 1024)], zeros[:, :]).then_inc(s_fill, 16)
                for t in range(IT):
                    sp.wait_ge(s_h0, t + 1)
                    sp.dma_start(h0_img[t * P:(t + 1) * P, :], z[:, t, :]).then_inc(s_out, 16)
                for t in range(IT):
                    sp.wait_ge(s_n3, t + 1)
                    sp.dma_start(xn_img[t * P:(t + 1) * P, :], xo[:, t, :]).then_inc(s_out, 16)
                sp.wait_ge(s_out, 2 * IT * 16)
                sp.wait_ge(s_fill, FILLS * 16)
                for j in range(2):
                    sp.wait_ge(s_tout[j], 16 + GROUPS // 2 * 16)

            @block.gpsimd
            def _(pool):
                pool.memset(ident[:, :], 0.0).then_inc(s_ident, 1)
                pool.memset(zeros[:, :], 0.0).then_inc(s_zero, 1)
                pool.wait_ge(s_ident, 1)
                pool.affine_select(out=ident[:, :], in_=ident[:, :], compare_op=ALU.not_equal, fill=1.0, base=0,
                                   pattern=[[-1, P]], channel_multiplier=1).then_inc(s_ident, 1)

            @block.scalar
            def _(act):
                with act.Fori(0, GROUPS // 2) as i:
                    for j in range(2):
                        act.wait_ge(s_tv, 2 * i + j + 1)
                        nc.scalar.activation(trs[:, j, 1, :], trs[:, j, 0, :], ACT.Sqrt).then_inc(s_tstd, 1)
                act.wait_ge(s_mv1, 1)
                nc.scalar.activation(rs[:, 0, :], rs[:, 3, :], ACT.Sqrt).then_inc(s_std1, 1)
                for t in range(IT):
                    act.wait_ge(s_xTp, t + 1)
                    if t >= 2:
                        act.wait_ge(s_z, t - 1)
                    nc.scalar.activation(xT[:, t % 2, 0:4, :], bt[2 * (t % 2)][:, 0:512].rearrange("p (c n) -> p c n", c=4), ACT.Copy)
                    nc.scalar.activation(xT[:, t % 2, 4:6, :], bt[2 * (t % 2) + 1][:, 0:256].rearrange("p (c n) -> p c n", c=2), ACT.Copy)\
                        .then_inc(s_xTs, 1)
                act.wait_ge(s_v2, 1)
                nc.scalar.activation(rs[:, 1, :], rs[:, 3, :], ACT.Sqrt).then_inc(s_std2, 1)
                act.wait_ge(s_v3, 1)
                nc.scalar.activation(rs[:, 2, :], rs[:, 3, :], ACT.Sqrt).then_inc(s_std3, 1)

            @block.tensor
            def _(pe):
                pe.wait_ge(s_ident, 2)
                for t in range(IT + 1):
                    if t < IT:
                        pe.wait_ge(s_n1, t + 1)
                        if t >= 2:
                            pe.wait_ge(s_xTs, t - 1)
                        for c in range(FC):
                            last = nc.tensor.transpose(bt[2 * (t % 2) + c // 4][:, (c % 4) * P:(c % 4 + 1) * P],
                                                       px[:, t, c * P:(c + 1) * P], ident[:, :])
                        last.then_inc(s_xTp, 1)
                    if t >= 1:
                        u = t - 1
                        pe.wait_ge(s_xTs, u + 1)
                        if u == 0:
                            pe.wait_ge(s_wl, 1)
                        if u >= 2:
                            pe.wait_ge(s_zc, u - 1)
                        for c in range(FC):
                            last = nc.tensor.matmul(bz[u % 2][:, 0:DM], xT[:, u % 2, c, :], wt[:, c, :],
                                                    start=(c == 0), stop=(c == FC - 1))
                        last.then_inc(s_z, 1)

            @block.vector
            def _(dve):
                v = nc.vector

                def variance(mv, s_mv_n, s_after):
                    v.tensor_scalar(rs[:, 3, :], mv[:, :, 1], eps, None, ALU.add).then_inc(s_after, 1)

                with dve.Fori(0, GROUPS // 2) as i:
                    for j in range(2):
                        g = 2 * i + j
                        dve.wait_ge(s_tx[j], (i + 1) * 16)
                        for t in range(ISLANDS):
                            v.bn_stats(tst[:, j, t, :], tx[:, j, t, :]).then_inc(s_tst, 1)
                        dve.wait_ge(s_tst, (g + 1) * ISLANDS)
                        v.memset(trs[:, j, 0, :], eps).then_inc(s_teps, 1)
                        for t in range(ISLANDS):
                            v.bn_aggr(tmv[:, j, t, :], tst[:, j, t, :]).then_inc(s_tmv, 1)
                        dve.wait_ge(s_teps, g + 1)
                        dve.wait_ge(s_tmv, (g + 1) * ISLANDS)
                        v.tensor_tensor(trs[:, j, 0, :], trs[:, j, 0, :], tmv[:, j, :, 1], ALU.add).then_inc(s_tv, 1)
                        dve.wait_ge(s_tstd, g + 1)
                        v.reciprocal(trs[:, j, 1, :], trs[:, j, 1, :]).then_inc(s_trs, 1)
                        dve.wait_ge(s_trs, g + 1)
                        for t in range(ISLANDS):
                            last = v.tensor_scalar(tx[:, j, t, :], tx[:, j, t, :], tmv[:, j, t, 0:1],
                                                   trs[:, j, 1, t:t + 1], ALU.subtract, ALU.mult)
                        last.then_inc(s_tn, 1)
                for t in range(IT):
                    dve.wait_ge(s_px[t], 16)
                    for k in range(2):
                        v.bn_stats(st1[:, t, k, :], px[:, t, k * 384:(k + 1) * 384]).then_inc(s_st, 1)
                    dve.wait_ge(s_st, 2 * (t + 1))
                    v.bn_aggr(mv1[:, t, :], st1[:, t, :, :]).then_inc(s_t1, 1)
                dve.wait_ge(s_t1, IT)
                variance(mv1, None, s_mv1)
                dve.wait_ge(s_w, 64)
                for c in range(FC):
                    last = v.tensor_scalar(wt[:, c, :], wt[:, c, :], ln1[:, c:c + 1], None, ALU.mult)
                last.then_inc(s_wl, 1)
                dve.wait_ge(s_std1, 1)
                v.reciprocal(rs[:, 0, :], rs[:, 0, :]).then_inc(s_rs1, 1)
                dve.wait_ge(s_rs1, 1)
                for t in range(IT):
                    v.tensor_scalar(px[:, t, :], px[:, t, :], mv1[:, t, 0:1], rs[:, 0, t:t + 1],
                                    ALU.subtract, ALU.mult).then_inc(s_n1, 1)
                for t in range(IT):
                    dve.wait_ge(s_z, t + 1)
                    v.bn_stats(st2[:, t, :], bz[t % 2][:, 0:DM]).then_inc(s_st, 1)
                    v.tensor_copy(z[:, t, :], bz[t % 2][:, 0:DM]).then_inc(s_zc, 1)
                    dve.wait_ge(s_st, 2 * IT + t + 1)
                    v.bn_aggr(mv2[:, t, :], st2[:, t, :]).then_inc(s_t1, 1)
                dve.wait_ge(s_t1, 2 * IT)
                dve.wait_ge(s_std1, 1)
                variance(mv2, None, s_v2)
                dve.wait_ge(s_std2, 1)
                v.reciprocal(rs[:, 1, :], rs[:, 1, :]).then_inc(s_rs2, 1)
                dve.wait_ge(s_rs2, 1)
                dve.wait_ge(s_zc, IT)
                for t in range(IT):
                    v.tensor_scalar(z[:, t, :], z[:, t, :], mv2[:, t, 0:1], rs[:, 1, t:t + 1],
                                    ALU.subtract, ALU.mult).then_inc(s_n2, 1)
                for t in range(IT):
                    dve.wait_ge(s_n2, t + 1)
                    v.tensor_tensor(z[:, t, :], z[:, t, :], ln2[:, :], ALU.mult).then_inc(s_n2b, 1)
                for t in range(IT):
                    dve.wait_ge(s_n2b, t + 1)
                    v.tensor_tensor(z[:, t, :], z[:, t, :], pe_t[:, t, :], ALU.add).then_inc(s_h0, 1)
                for t in range(IT):
                    dve.wait_ge(s_h0, t + 1)
                    v.bn_stats(st3[:, t, :], z[:, t, :]).then_inc(s_st, 1)
                for t in range(IT):
                    dve.wait_ge(s_st, 3 * IT + t + 1)
                    v.bn_aggr(mv3[:, t, :], st3[:, t, :]).then_inc(s_t1, 1)
                dve.wait_ge(s_t1, 3 * IT)
                variance(mv3, None, s_v3)
                dve.wait_ge(s_std3, 1)
                v.reciprocal(rs[:, 2, :], rs[:, 2, :]).then_inc(s_rs3, 1)
                dve.wait_ge(s_rs3, 1)
                for t in range(IT):
                    v.tensor_scalar(xo[:, t, :], z[:, t, :], mv3[:, t, 0:1], rs[:, 2, t:t + 1],
                                    ALU.subtract, ALU.mult).then_inc(s_n3, 1)


class Turn:

    def __init__(self, i, k):
        self.i, self.k = i, k
        self.b, self.par, self.half = 2 * i + k, k % 2, i + k // 2

    def at(self, d):
        return Turn(self.i, self.k + d)

    def pair(self, p):
        return 8 * self.i * 2 + (8 * self.k + p)


def turns(engine):
    yield Turn(0, 0), True, False
    yield Turn(0, 1), False, False
    with engine.Fori(1, BATCH // 2 - 1) as i:
        yield Turn(i, 0), False, False
        yield Turn(i, 1), False, False
    yield Turn(BATCH // 2 - 1, 0), False, False
    yield Turn(BATCH // 2 - 1, 1), False, True


def wait(engine, sem, value):
    if not isinstance(value, int) or value > 0:
        engine.wait_ge(sem, value)


def wait_alone(engine, sem, value, ready):
    engine.wait_ge(ready, 1)
    wait(engine, sem, value)


def attention(nc, A, G):
    f32, bf16, fp16 = mybir.dt.float32, mybir.dt.bfloat16, mybir.dt.float16
    ALU, ACT, AX = mybir.AluOpType, mybir.ActivationFunctionType, mybir.AxisListType
    ident, h0_img, xn_img, xn_txt, h1_d = (G[k] for k in ("ident", "h0_img", "xn_img", "xn_txt", "h1_d"))
    txt_rows = A["txt"].rearrange("b t c -> (b t) c")
    with ExitStack() as ctx:
        sb, bank, sem = G["tools"](ctx)
        w_in = [sb(f"w_{n}", [P, KC, DM]) for n in "qkvp"]
        wq, wk, wv, wp = w_in
        bq, bk = sb("bq", [P, KC]), sb("bk", [P, KC])
        bv, bp = sb("bv", [P, 2 * DM]), sb("bp", [P, DM])
        bias = sb("bias", [P, PAIRS, 3, SEQ])
        temp = sb("temp", [P, 1])
        scale = sb("scale", [P, 1])
        x_in = sb("x_in", [P, 2, 2, DM])
        xT = sb("xT_a", [P, KC, 2 * P])
        qs = sb("qs", [P, KC, SEQ])
        qm = sb("qm", [P, 2, PAIRS, 3 * P])
        ks = sb("ks", [P, 2, KC, SEQ])
        vf = sb("vf", [P, 2, HEADS, HD])
        vr = sb("vr", [P, 2, HEADS, HD])
        v3 = sb("v3", [P, 2, 2, HEADS, VW], bf16)
        vm = sb("vm", [P, 2, PAIRS, 4, VW], bf16)
        score = sb("score", [P, 2, 3, SEQ])
        prob = sb("prob", [P, 2, 3 * SEQ])
        rmax = sb("rmax", [P, 2, 3])
        pth = sb("pth", [P, 2, 512], fp16)
        ptl = sb("ptl", [P, 2, 512], fp16)
        osum = sb("osum", [P, 2, PAIRS, 4, HD])
        rden = sb("rden", [P, 2, PAIRS, 4])
        on = sb("on", [P, 2, DM])
        oT = sb("oT", [P, KC, SEQ])
        res = sb("res", [P, 2, 2, DM])
        ps_s = [bank(f"ps_s{i}") for i in range(2)]
        ps_t = [bank(f"ps_t{i}") for i in range(2)]
        ps_o = [bank(f"ps_o{i}") for i in range(2)]
        ps_x, ps_y = bank("ps_x"), bank("ps_y")

        s_const, s_init, s_scale, s_bias = sem("s_const"), sem("s_init"), sem("s_scale"), sem("s_bias")
        two = lambda n: [sem(f"{n}{i}") for i in range(2)]
        s_x, s_qm, s_vm, s_res, s_store = two("s_x"), two("s_qm"), two("s_vm"), two("s_res"), two("s_store")
        (s_xT_ps, s_xT, s_q_ps, s_q, s_k_ps, s_k, s_v_ps, s_vf, s_v1, s_vr, s_v2, s_v3) = (
            sem(n) for n in ("a_xT_ps", "a_xT", "a_q_ps", "a_q", "a_k_ps", "a_k", "a_v_ps", "a_vf", "a_v1",
                             "a_vr", "a_v2", "a_v3"))
        (s_S, s_Sb, s_mx, s_shift, s_P, s_PT, s_Ph, s_Pl, s_O, s_Ored) = (
            sem(n) for n in ("a_S", "a_Sb", "a_mx", "a_shift", "a_P", "a_PT", "a_Ph", "a_Pl", "a_O", "a_Ored"))
        s_On, s_oT_ps, s_oT, s_Y, s_rb, s_h1 = (sem(n) for n in ("a_On", "a_oT_ps", "a_oT", "a_Y", "a_rb", "a_h1"))
        QM, VM = HEADS * 16, 3 * 16

        def rows(T, part):
            return bass.ds(T.b * (NT if part == 0 else NI), NT if part == 0 else NI)

        with nc.Block() as block:
            @block.sync
            def _(sp):
                for w, name in zip(w_in, ("Wq", "Wk", "Wv", "Wp")):
                    sp.dma_start(w[:, :, :], A[name].rearrange("(c p) n -> p c n", p=P)).then_inc(s_const, 16)
                for t, name in ((temp, "temp"), (bq, "bq"), (bk, "bk"), (bv, "bv"), (bp, "bp")):
                    sp.dma_start(t[:, :], A[name]).then_inc(s_const, 16)
                sp.dma_start(bias[:, :, :, :], A["bias"]).then_inc(s_const, 16)

                def load_x(T):
                    wait_alone(sp, s_xT_ps, T.b - 1, s_scale)
                    sp.dma_start(x_in[:, T.par, 0, :], xn_txt[rows(T, 0), :]).then_inc(s_x[T.par], 16)
                    sp.dma_start(x_in[0:NI, T.par, 1, :], xn_img[rows(T, 1), :]).then_inc(s_x[T.par], 16)

                def spread(T):
                    sp.wait_ge(s_q, T.b + 1)
                    for h in range(HEADS // KC):
                        r, q, o = h * HD, h // 2, h % 2
                        to = qm[r:r + HD, T.par, :, :].rearrange("p (c q) n -> p c q n", c=KC)[:, :, q, :]
                        sp.dma_start(to[:, :, o * P:(o + 1) * P], qs[r:r + HD, :, 0:NT]).then_inc(s_qm[T.par], 16)
                        sp.dma_start(to[:, :, 2 * P + o * 64:2 * P + o * 64 + NI], qs[r:r + HD, :, NT:SEQ])\
                            .then_inc(s_qm[T.par], 16)
                    sp.wait_ge(s_v3, T.b + 1)
                    src = v3[0:NI, T.par, 1, :, :].rearrange("p (a b) w -> p a b w", b=2)
                    sp.dma_start(vm[0:NI, T.par, :, 0, :], src[:, :, 0, :]).then_inc(s_vm[T.par], 16)
                    sp.dma_start(vm[NI:2 * NI, T.par, :, 1, :], src[:, :, 1, :]).then_inc(s_vm[T.par], 16)
                    sp.dma_start(vm[2 * NI:3 * NI, T.par, :, 2:4, :], src).then_inc(s_vm[T.par], 16)

                def load_res(T):
                    wait_alone(sp, s_store[T.par], T.half * 32, s_scale)
                    sp.dma_start(res[:, T.par, 0, :], txt_rows[rows(T, 0), :]).then_inc(s_res[T.par], 16)
                    sp.dma_start(res[0:NI, T.par, 1, :], h0_img[rows(T, 1), :]).then_inc(s_res[T.par], 16)

                def store(T):
                    wait_alone(sp, s_h1, T.b + 1, s_scale)
                    sp.dma_start(h1_d[bass.ds(T.b * SEQ + NI, NT), :], res[:, T.par, 0, :]).then_inc(s_store[T.par], 16)
                    sp.dma_start(h1_d[bass.ds(T.b * SEQ, NI), :], res[0:NI, T.par, 1, :]).then_inc(s_store[T.par], 16)

                load_x(Turn(0, 0))
                sp.wait_ge(s_init, 6)
                spread(Turn(0, 0))
                for T, first, last in turns(sp):
                    if not last:
                        load_x(T.at(1))
                    load_res(T)
                    if not last:
                        spread(T.at(1))
                    if not first:
                        store(T.at(-1))
                store(Turn(BATCH // 2 - 1, 1))
                for j in range(2):
                    sp.wait_ge(s_store[j], BATCH * 16)

            @block.gpsimd
            def _(pool):
                pool.memset(qm[:, :, :, :], 0.0).then_inc(s_init, 1)
                pool.memset(vm[:, :, :, :, :], 0.0).then_inc(s_init, 1)
                pool.memset(v3[:, :, :, :, VW - 1:VW], 1.0).then_inc(s_init, 1)
                pool.memset(xT[:, :, :], 0.0).then_inc(s_init, 1)

                def front(T):
                    pool.wait_ge(s_v1, T.b + 1)
                    wait(pool, s_v3, T.b)
                    pool.tensor_tensor(vr[:, :, :, :], vf[:, :, :, :], v3[:, T.par, :, :, 0:HD], ALU.subtract).then_inc(s_vr, 1)
                    pool.tensor_tensor(v3[:, T.par, :, :, HD:2 * HD], vf[:, :, :, :], v3[:, T.par, :, :, 0:HD],
                                       ALU.subtract).then_inc(s_v2, 1)
                    pool.wait_ge(s_v2, T.b + 1)
                    pool.tensor_tensor(v3[:, T.par, :, :, 2 * HD:3 * HD], vr[:, :, :, :], v3[:, T.par, :, :, HD:2 * HD],
                                       ALU.subtract).then_inc(s_v3, 1)

                def shift(T, p):
                    n = T.pair(p)
                    pool.wait_ge(s_mx, n + 1)
                    wait(pool, s_PT, n - 1)
                    for lo, k, src in ((0, P, score[:, p % 2, :, 0:P]), (3 * P, NI, score[:, p % 2, :, P:SEQ])):
                        last = pool.tensor_tensor(prob[:, p % 2, lo:lo + 3 * k].rearrange("p (t n) -> p t n", t=3), src,
                                                  rmax[:, p % 2, :].unsqueeze(2).to_broadcast([P, 3, k]), ALU.subtract)
                    last.then_inc(s_shift, 1)

                front(Turn(0, 0))
                shift(Turn(0, 0), 0)
                pool.wait_ge(s_const, 160)
                for T, first, last in turns(pool):
                    pool.wait_ge(s_res[T.par], (T.half + 1) * 32)
                    pool.tensor_tensor(res[:, T.par, 0, :], res[:, T.par, 0, :], bp[:, :], ALU.add)
                    pool.tensor_tensor(res[0:NI, T.par, 1, :], res[0:NI, T.par, 1, :], bp[0:NI, :], ALU.add).then_inc(s_rb, 1)
                    for p in range(PAIRS):
                        if p < PAIRS - 1:
                            shift(T, p + 1)
                        elif not last:
                            shift(T.at(1), 0)
                        if not last and p == 4:
                            front(T.at(1))

            @block.tensor
            def _(pe):
                def xT_(T):
                    pe.wait_ge(s_x[T.par], (T.half + 1) * 32)
                    wait(pe, s_oT, T.b - 2)
                    for c in range(KC):
                        nc.tensor.transpose(ps_x[:, c * 256:c * 256 + NT], x_in[:, T.par, 0, c * P:(c + 1) * P], ident[:, :])
                        last = nc.tensor.transpose(ps_x[:, c * 256 + NT:c * 256 + SEQ], x_in[0:NI, T.par, 1, c * P:(c + 1) * P],
                                                   ident[0:NI, 0:NI])
                    last.then_inc(s_xT_ps, 1)

                def project(out, w):
                    for m in range(KC):
                        for c in range(KC):
                            last = nc.tensor.matmul(out[:, m * SEQ:(m + 1) * SEQ], w[:, c, m * P:(m + 1) * P], xT[:, c, 0:SEQ],
                                                    start=(c == 0), stop=(c == KC - 1))
                    return last

                def q_(T):
                    pe.wait_ge(s_xT, T.b + 1)
                    wait(pe, s_h1, T.b - 2)
                    project(ps_y, wq).then_inc(s_q_ps, 1)

                def k_(T):
                    project(ps_x, wk).then_inc(s_k_ps, 1)

                def v_(T):
                    pe.wait_ge(s_q, T.b + 1)
                    for m in range(2):
                        for c in range(KC):
                            last = nc.tensor.matmul(ps_y[:, m * DM:(m + 1) * DM], xT[:, c, m * P:(m + 1) * P], wv[:, c, :],
                                                    start=(c == 0), stop=(c == KC - 1))
                    last.then_inc(s_v_ps, 1)

                def oT_(T, follows):
                    pe.wait_ge(s_On, T.b + 1)
                    if follows:
                        pe.wait_ge(s_k, T.b + 3)
                    for c in range(KC):
                        nc.tensor.transpose(ps_x[:, c * 256:c * 256 + NT], on[:, 0, c * P:(c + 1) * P], ident[:, :])
                        last = nc.tensor.transpose(ps_x[:, c * 256 + NT:c * 256 + SEQ], on[0:NI, 1, c * P:(c + 1) * P],
                                                   ident[0:NI, 0:NI])
                    last.then_inc(s_oT_ps, 1)

                def out_(T, follows):
                    pe.wait_ge(s_oT, T.b + 1)
                    if follows:
                        pe.wait_ge(s_vf, T.b + 3)
                    for m, (lo, n) in enumerate(((0, NT), (NT, NI))):
                        for c in range(KC):
                            last = nc.tensor.matmul(ps_y[0:n, m * DM:(m + 1) * DM], oT[:, c, lo:lo + n], wp[:, c, :],
                                                    start=(c == 0), stop=(c == KC - 1))
                    last.then_inc(s_Y, 1)

                def scores(T, p):
                    n = T.pair(p)
                    if p == 0:
                        pe.wait_ge(s_qm[T.par], (T.half + 1) * QM)
                        pe.wait_ge(s_k, T.b + 1)
                    wait(pe, s_Sb, n - 1)
                    c = p // 4
                    out = ps_s[p % 2]
                    for t in range(3):
                        last = nc.tensor.matmul(out[:, t * SEQ:(t + 1) * SEQ], qm[:, T.par, p, t * P:(t + 1) * P], ks[:, T.par, c, :], start=True, stop=True)
                    last.then_inc(s_S, 1)

                def turn_probs(T, p):
                    n = T.pair(p)
                    pe.wait_ge(s_P, n + 1)
                    wait(pe, s_Pl, n - 1)
                    out = ps_t[p % 2]
                    for t in range(3):
                        nc.tensor.transpose(out[:, t * P:(t + 1) * P], prob[:, p % 2, t * P:(t + 1) * P], ident[:, :])
                    nc.tensor.transpose(out[0:3 * NI, 3 * P:4 * P], prob[:, p % 2, 3 * P:3 * SEQ], ident[:, :]).then_inc(s_PT, 1)

                def values(T, p):
                    n = T.pair(p)
                    if p == 0:
                        pe.wait_ge(s_vm[T.par], (T.half + 1) * VM)
                    pe.wait_ge(s_Pl, n + 1)
                    wait(pe, s_Ored, n - 1)
                    out = ps_o[p % 2]
                    parts = (pth, ptl)
                    for g, src in enumerate(parts):
                        nc.tensor.matmul(out[:, 0:4 * VW], src[0:3 * NI, p % 2, 3 * P:4 * P], vm[0:3 * NI, T.par, p, :, :],
                                         start=(g == 0), stop=False)
                    for t, (h, k) in enumerate(((2 * p, 1), (2 * p + 1, 1), (2 * p, 2))):
                        for g, src in enumerate(parts):
                            last = nc.tensor.matmul(out[:, t * VW:(t + k) * VW], src[:, p % 2, t * P:(t + 1) * P],
                                                    v3[:, T.par, 0, h:h + k, :], start=False, stop=(g == 1 and t == 2))
                    last.then_inc(s_O, 1)

                pe.wait_ge(s_const, 160)
                pe.wait_ge(s_init, 6)
                T0 = Turn(0, 0)
                for f in (xT_, q_, k_, v_):
                    f(T0)
                scores(T0, 0)
                for T, first, last in turns(pe):
                    for p in range(PAIRS):
                        if p < PAIRS - 1:
                            scores(T, p + 1)
                        elif not last:
                            scores(T.at(1), 0)
                        turn_probs(T, p)
                        if p > 0:
                            values(T, p - 1)
                        elif not first:
                            values(T.at(-1), PAIRS - 1)
                        if not last and 1 <= p < 5:
                            (xT_, q_, k_, v_)[p - 1](T.at(1))
                        if not first and p == 5:
                            oT_(T.at(-1), not last)
                        if not first and p == 6:
                            out_(T.at(-1), not last)
                T = Turn(BATCH // 2 - 1, 1)
                values(T, PAIRS - 1)
                oT_(T, False)
                out_(T, False)

            @block.scalar
            def _(act):
                def xT_(T):
                    act.wait_ge(s_xT_ps, T.b + 1)
                    wait(act, s_v_ps, T.b)
                    nc.scalar.activation(xT[:, :, 0:SEQ], ps_x[:, :].rearrange("p (c n) -> p c n", c=KC)[:, :, 0:SEQ], ACT.Copy)\
                        .then_inc(s_xT, 1)

                def k_(T):
                    act.wait_ge(s_k_ps, T.b + 1)
                    wait(act, s_S, T.pair(-8))
                    for m in range(KC):
                        last = nc.scalar.activation(ks[:, T.par, m, :], ps_x[:, m * SEQ:(m + 1) * SEQ], ACT.Identity,
                                                    bias=bk[:, m:m + 1])
                    last.then_inc(s_k, 1)

                def v1_(T):
                    act.wait_ge(s_vf, T.b + 1)
                    wait(act, s_O, T.pair(-8))
                    wait(act, s_vm[T.par], T.half * VM)
                    nc.scalar.activation(v3[:, T.par, :, :, 0:HD], vf[:, :, :, :], ACT.Copy).then_inc(s_v1, 1)

                def oT_(T):
                    act.wait_ge(s_oT_ps, T.b + 1)
                    wait(act, s_Y, T.b)
                    nc.scalar.activation(oT[:, :, :], ps_x[:, :].rearrange("p (c n) -> p c n", c=KC)[:, :, 0:SEQ], ACT.Copy)\
                        .then_inc(s_oT, 1)

                def exps(T, p):
                    act.wait_ge(s_shift, T.pair(p) + 1)
                    nc.scalar.activation(prob[:, p % 2, :], prob[:, p % 2, :], ACT.Exp).then_inc(s_P, 1)

                def high(T, p):
                    n = T.pair(p)
                    act.wait_ge(s_PT, n + 1)
                    wait(act, s_O, n - 1)
                    nc.scalar.activation(pth[:, p % 2, :], ps_t[p % 2][:, :], ACT.Copy).then_inc(s_Ph, 1)

                act.wait_ge(s_const, 160)
                act.wait_ge(s_init, 6)
                T0 = Turn(0, 0)
                for f in (xT_, k_, v1_):
                    f(T0)
                exps(T0, 0)
                for T, first, last in turns(act):
                    for p in range(PAIRS):
                        high(T, p)
                        if p < PAIRS - 1:
                            exps(T, p + 1)
                        elif not last:
                            exps(T.at(1), 0)
                        if not last and p in (1, 3, 4):
                            {1: xT_, 3: k_, 4: v1_}[p](T.at(1))
                        if not first and p == 5:
                            oT_(T.at(-1))
                oT_(Turn(BATCH // 2 - 1, 1))

            @block.vector
            def _(dve):
                v = nc.vector

                def q_(T):
                    dve.wait_ge(s_q_ps, T.b + 1)
                    if not isinstance(T.b, int) or T.b > 0:
                        L = T.at(-1)
                        dve.wait_ge(s_qm[L.par], (L.half + 1) * QM)
                    for m in range(KC):
                        last = v.tensor_scalar(qs[:, m, :], ps_y[:, m * SEQ:(m + 1) * SEQ], bq[:, m:m + 1], scale[:, 0:1],
                                               ALU.add, ALU.mult)
                    last.then_inc(s_q, 1)

                def v_(T):
                    dve.wait_ge(s_v_ps, T.b + 1)
                    wait(dve, s_v2, T.b)
                    v.tensor_tensor(vf[:, :, :, :].rearrange("p a h d -> p (a h d)"), ps_y[:, :], bv[:, :], ALU.add)\
                        .then_inc(s_vf, 1)

                def norm(T):
                    dve.wait_ge(s_Ored, T.pair(0) + 8)
                    wait(dve, s_oT_ps, T.b)
                    parts = (((0, P), 0, 0), ((0, NI), 1, 2), ((64, 64 + NI), 1, 3))
                    o_v = on[:, :, :].rearrange("p m (a h d) -> p m a h d", h=2, d=HD)
                    v.tensor_tensor(o_v[:, 0, :, :, :], osum[:, T.par, :, 0:2, :],
                                    rden[:, T.par, :, 0:2].unsqueeze(3).to_broadcast([P, PAIRS, 2, HD]), ALU.mult)
                    for h, lo in ((0, 0), (1, 64)):
                        last = v.tensor_tensor(o_v[0:NI, 1, :, h, :], osum[lo:lo + NI, T.par, :, 2 + h, :],
                                               rden[lo:lo + NI, T.par, :, 2 + h].unsqueeze(2).to_broadcast([NI, PAIRS, HD]),
                                               ALU.mult)
                    last.then_inc(s_On, 1)

                def h1_(T):
                    dve.wait_ge(s_Y, T.b + 1)
                    dve.wait_ge(s_rb, T.b + 1)
                    v.tensor_tensor(res[:, T.par, 0, :], ps_y[:, 0:DM], res[:, T.par, 0, :], ALU.add)
                    v.tensor_tensor(res[0:NI, T.par, 1, :], ps_y[0:NI, DM:2 * DM], res[0:NI, T.par, 1, :], ALU.add).then_inc(s_h1, 1)

                def biased(T, p):
                    n = T.pair(p)
                    dve.wait_ge(s_S, n + 1)
                    wait(dve, s_shift, n - 1)
                    v.tensor_tensor(score[:, p % 2, :, :].rearrange("p t n -> p (t n)"), ps_s[p % 2][:, 0:3 * SEQ],
                                    bias[:, p, :, :].rearrange("p t n -> p (t n)"), ALU.add).then_inc(s_Sb, 1)
                    dve.wait_ge(s_Sb, n + 1)
                    v.tensor_reduce(rmax[:, p % 2, :], score[:, p % 2, :, :], AX.X, ALU.max).then_inc(s_mx, 1)

                def low(T, p):
                    dve.wait_ge(s_Ph, T.pair(p) + 1)
                    v.tensor_tensor(ptl[:, p % 2, :], ps_t[p % 2][:, :], pth[:, p % 2, :], ALU.subtract).then_inc(s_Pl, 1)

                def sums(T, p):
                    n = T.pair(p)
                    dve.wait_ge(s_O, n + 1)
                    if p == 0:
                        wait(dve, s_On, T.b - 1)
                    o = ps_o[p % 2][:, 0:4 * VW].rearrange("p (h w) -> p h w", w=VW)
                    v.tensor_reduce(osum[:, T.par, p, :, :], o[:, :, 0:3 * HD].rearrange("p h (k d) -> p h d k", d=HD), AX.X, ALU.add)
                    v.reciprocal(rden[:, T.par, p, :], o[:, :, VW - 1]).then_inc(s_Ored, 1)

                for t in ps_t:
                    v.memset(t[:, :], 0.0).then_inc(s_init, 1)
                dve.wait_ge(s_const, 160)
                chain = sem("a_chain")
                v.tensor_scalar(scale[:, :], temp[:, :], 0.1, 10.0, ALU.max, ALU.min).then_inc(chain, 1)
                dve.wait_ge(chain, 1)
                v.tensor_scalar(scale[:, :], scale[:, :], float(DM) ** 0.5, None, ALU.mult).then_inc(chain, 1)
                dve.wait_ge(chain, 2)
                v.reciprocal(scale[:, :], scale[:, :]).then_inc(s_scale, 1)
                dve.wait_ge(s_scale, 1)
                for p in range(PAIRS):
                    v.tensor_scalar(bias[:, p, :, :], bias[:, p, :, :], scale[:, 0:1], None, ALU.mult).then_inc(s_bias, 1)
                dve.wait_ge(s_bias, PAIRS)
                T0 = Turn(0, 0)
                q_(T0)
                v_(T0)
                biased(T0, 0)
                for T, first, last in turns(dve):
                    for p in range(PAIRS):
                        if p < PAIRS - 1:
                            biased(T, p + 1)
                        elif not last:
                            biased(T.at(1), 0)
                        low(T, p)
                        if p > 0:
                            sums(T, p - 1)
                        elif not first:
                            sums(T.at(-1), PAIRS - 1)
                        if not last and p == 2:
                            q_(T.at(1))
                        if not last and p == 4:
                            v_(T.at(1))
                        if not first and p == 1:
                            norm(T.at(-1))
                        if not first and p == 6:
                            h1_(T.at(-1))
                T = Turn(BATCH // 2 - 1, 1)
                sums(T, PAIRS - 1)
                norm(T)
                h1_(T)



def experts(nc, A, G, stop):
    f32, i32, u32 = mybir.dt.float32, mybir.dt.int32, mybir.dt.uint32
    ALU, ACT, AX = mybir.AluOpType, mybir.ActivationFunctionType, mybir.AxisListType
    ident, h1_d, y_slots, o_slots = (G[k] for k in ("ident", "h1_d", "y_slots", "o_slots"))
    E = EXPERTS
    LIST = (TOK + FT - 1) // FT
    with ExitStack() as keep:
        sbk, _, semk = G["tools"](keep)
        res = sbk("res2", [P, TT, DM])
        slot = sbk("slot", [P, TT, 2], u32)
        wts = sbk("wts", [P, 2, TT])
        owner = sbk("owner", [P, ETILES], i32)

        with ExitStack() as ctx:
            sb, bank, sem = G["tools"](ctx)
            y = sb("y", [P, TT, DM])
            gate = sb("gate", [P, KC, E])
            rms = sb("rms", [P, DM])
            st, mv = sb("st", [P, TT, 6]), sb("mv", [P, TT, 2])
            r1, r2 = sb("r1", [P, TT]), sb("r2", [P, TT])
            va = sb("va", [P, TT])
            x1 = sb("x1", [P, 2, DM])
            yT = sb("yT", [P, 2, KC, P])
            logit = sb("logit", [P, TT, E])
            top = sb("top", [P, TT, 8])
            topi = sb("topi", [P, TT, 8], u32)
            topf = sb("topf", [P, TT, 2])
            ex = sb("ex", [P, TT])
            io_i = sb("io_i", [P, 64], i32)
            io = sb("io", [P, 64])
            pick = sb("pick", [P, 2, TT, E])
            both = sb("both", [P, TT, E])
            below, ones = sb("below", [P, P]), sb("ones", [P, P])
            tot, incl = sb("tot", [P, E, TT]), sb("incl", [P, E, TT])
            place = sb("place", [P, TT, E])
            over = sb("over", [P, E, LIST])
            tiles, ends, base = sb("tiles", [P, E]), sb("ends", [P, E]), sb("base", [P, E])
            work = sb("work", [P, 2, TT, E])
            slotf = sb("slotf", [P, 2, TT])
            owns = sb("owns", [P, ETILES, E])
            ownf = sb("ownf", [P, ETILES])
            pt = [bank(f"r_pt{i}") for i in range(2)]
            pl = [bank(f"r_pl{i}") for i in range(2)]
            pa, pb = bank("r_pa"), bank("r_pb")
            (s_h, s_c, s_st, s_mv, s_v, s_sd, s_r, s_x1, s_y, s_yT_ps, s_yT, s_l, s_lg, s_top, s_io, s_tri, s_both,
             s_cnt, s_d, s_ex, s_step, s_slot, s_sc, s_resid) = (
                sem(f"r{n}") for n in range(24))
            with nc.Block() as block:
                @block.sync
                def _(sp):
                    sp.dma_start(gate[:, :, :], A["gate"].rearrange("(c p) n -> p c n", p=P)).then_inc(s_c, 16)
                    sp.dma_start(rms[:, :], A["rms_w"]).then_inc(s_c, 16)
                    sp.dma_start(res[:, :, :], h1_d.rearrange("(t p) n -> p t n", p=P)).then_inc(s_h, 16)

                @block.gpsimd
                def _(pool):
                    pool.iota(io_i[:, :], pattern=[[1, 64]], base=0, channel_multiplier=0).then_inc(s_io, 1)
                    pool.memset(below[:, :], 1.0).then_inc(s_tri, 1)
                    pool.memset(ones[:, :], 1.0).then_inc(s_tri, 1)
                    pool.wait_ge(s_tri, 2)
                    pool.affine_select(out=below[:, :], in_=below[:, :], compare_op=ALU.is_gt, fill=0.0, base=0,
                                       pattern=[[1, P]], channel_multiplier=-1).then_inc(s_tri, 1)
                    pool.wait_ge(s_slot, 1)
                    for t in range(TT):
                        for k in range(2):
                            pool.indirect_dma_start(out=y_slots, out_offset=bass.IndirectOffsetOnAxis(ap=slot[:, t, k:k + 1], axis=0),
                                                    in_=y[:, t, :], in_offset=None).then_inc(s_sc, 16)
                    pool.wait_ge(s_sc, 2 * TT * 16)

                @block.scalar
                def _(act):
                    act.wait_ge(s_v, 1)
                    nc.scalar.activation(r1[:, :], r1[:, :], ACT.Sqrt).then_inc(s_sd, 1)
                    act.wait_ge(s_v, 2)
                    nc.scalar.activation(r2[:, :], r2[:, :], ACT.Sqrt).then_inc(s_sd, 1)
                    for t in range(TT):
                        act.wait_ge(s_yT_ps, t + 1)
                        if t >= 2:
                            act.wait_ge(s_l, t - 1)
                        nc.scalar.activation(yT[:, t % 2, :, :], pt[t % 2][:, 0:KC * P].rearrange("p (c n) -> p c n", c=KC), ACT.Copy)\
                            .then_inc(s_yT, 1)
                    act.wait_ge(s_d, 1)
                    nc.scalar.activation(ex[:, :], ex[:, :], ACT.Exp).then_inc(s_ex, 1)

                @block.tensor
                def _(pe):
                    pe.wait_ge(s_c, 32)
                    for t in range(TT + 1):
                        if t < TT:
                            pe.wait_ge(s_y, t + 1)
                            if t >= 2:
                                pe.wait_ge(s_yT, t - 1)
                            for c in range(KC):
                                last = nc.tensor.transpose(pt[t % 2][:, c * P:(c + 1) * P], y[:, t, c * P:(c + 1) * P], ident[:, :])
                            last.then_inc(s_yT_ps, 1)
                        if t >= 1:
                            u = t - 1
                            pe.wait_ge(s_yT, u + 1)
                            if u >= 2:
                                pe.wait_ge(s_lg, u - 1)
                            for c in range(KC):
                                last = nc.tensor.matmul(pl[u % 2][:, 0:E], yT[:, u % 2, c, :], gate[:, c, :],
                                                        start=(c == 0), stop=(c == KC - 1))
                            last.then_inc(s_l, 1)
                    pe.wait_ge(s_tri, 3)
                    pe.wait_ge(s_both, 1)
                    flat = both[:, :, :].rearrange("p t e -> p (t e)")
                    nc.tensor.matmul(pa[:, 0:TT * E], below[:, :], flat, start=True, stop=True)
                    nc.tensor.matmul(pb[:, 0:TT * E], ones[:, :], flat, start=True, stop=True).then_inc(s_cnt, 1)

                @block.vector
                def _(dve):
                    v = nc.vector
                    n = [0]

                    def step(ins):
                        n[0] += 1
                        ins.then_inc(s_step, 1)
                        dve.wait_ge(s_step, n[0])

                    dve.wait_ge(s_h, 16)
                    for t in range(TT):
                        v.bn_stats(st[:, t, :], res[:, t, :]).then_inc(s_st, 1)
                    for t in range(TT):
                        dve.wait_ge(s_st, t + 1)
                        v.bn_aggr(mv[:, t, :], st[:, t, :]).then_inc(s_mv, 1)
                    dve.wait_ge(s_mv, TT)
                    step(v.tensor_scalar(va[:, :], mv[:, :, 1], 1e-5, None, ALU.add))
                    v.tensor_copy(r1[:, :], va[:, :]).then_inc(s_v, 1)
                    step(v.reciprocal(va[:, :], va[:, :]))
                    step(v.tensor_tensor(va[:, :], va[:, :], mv[:, :, 1], ALU.mult))
                    v.tensor_scalar(r2[:, :], va[:, :], 1e-6, None, ALU.add).then_inc(s_v, 1)
                    dve.wait_ge(s_sd, 2)
                    step(v.reciprocal(r1[:, :], r1[:, :]))
                    step(v.reciprocal(r2[:, :], r2[:, :]))
                    dve.wait_ge(s_c, 32)
                    for t in range(TT):
                        if t >= 2:
                            dve.wait_ge(s_resid, t - 1)
                        v.tensor_scalar(x1[:, t % 2, :], res[:, t, :], mv[:, t, 0:1], r1[:, t:t + 1],
                                        ALU.subtract, ALU.mult).then_inc(s_x1, 1)
                        dve.wait_ge(s_x1, t + 1)
                        v.scalar_tensor_tensor(y[:, t, :], x1[:, t % 2, :], r2[:, t:t + 1], rms[:, :],
                                               ALU.mult, ALU.mult).then_inc(s_y, 1)
                        v.tensor_tensor(res[:, t, :], res[:, t, :], x1[:, t % 2, :], ALU.add).then_inc(s_resid, 1)
                    for t in range(TT):
                        dve.wait_ge(s_l, t + 1)
                        v.tensor_copy(logit[:, t, :], pl[t % 2][:, 0:E]).then_inc(s_lg, 1)
                        dve.wait_ge(s_lg, t + 1)
                        v.max(top[:, t, :], logit[:, t, :]).then_inc(s_top, 1)
                        dve.wait_ge(s_top, 2 * t + 1)
                        v.max_index(topi[:, t, :], top[:, t, :], logit[:, t, :]).then_inc(s_top, 1)
                    dve.wait_ge(s_top, 2 * TT)
                    v.tensor_tensor(ex[:, :], top[:, :, 1], top[:, :, 0], ALU.subtract).then_inc(s_d, 1)
                    dve.wait_ge(s_io, 1)
                    v.tensor_copy(topf[:, :, :], topi[:, :, 0:2])
                    step(v.tensor_copy(io[:, :], io_i[:, :]))
                    for k in range(2):
                        step(v.tensor_tensor(pick[:, k, :, :], io[:, 0:E].unsqueeze(1).to_broadcast([P, TT, E]),
                                             topf[:, :, k].unsqueeze(2).to_broadcast([P, TT, E]), ALU.is_equal))
                    v.tensor_tensor(both[:, :, :], pick[:, 0, :, :], pick[:, 1, :, :], ALU.add).then_inc(s_both, 1)
                    dve.wait_ge(s_ex, 1)
                    step(v.tensor_scalar(wts[:, 0, :], ex[:, :], 1.0, None, ALU.add))
                    step(v.reciprocal(wts[:, 0, :], wts[:, 0, :]))
                    step(v.tensor_tensor(wts[:, 1, :], ex[:, :], wts[:, 0, :], ALU.mult))
                    dve.wait_ge(s_cnt, 1)
                    step(v.tensor_copy(tot[:, :, :], pb[:, 0:TT * E].rearrange("p (t e) -> p e t", e=E)))
                    for e in range(E):
                        step(v.tensor_tensor_scan(incl[:, e, :], ones[:, 0:TT], tot[:, e, :], 0.0, ALU.mult, ALU.add))
                    step(v.tensor_scalar(ownf[:, 0:LIST], io[:, 0:LIST], float(FT), None, ALU.mult))
                    step(v.tensor_tensor(over[:, :, :], incl[:, :, TT - 1].unsqueeze(2).to_broadcast([P, E, LIST]),
                                         ownf[:, 0:LIST].unsqueeze(1).to_broadcast([P, E, LIST]), ALU.is_gt))
                    step(v.tensor_reduce(tiles[:, :], over[:, :, :], AX.X, ALU.add))
                    step(v.tensor_tensor_scan(ends[:, :], ones[:, 0:E], tiles[:, :], 0.0, ALU.mult, ALU.add))
                    step(v.tensor_tensor(base[:, :], ends[:, :], tiles[:, :], ALU.subtract))
                    step(v.tensor_scalar(base[:, :], base[:, :], float(FT), None, ALU.mult))
                    step(v.tensor_tensor(incl[:, :, :], incl[:, :, :], tot[:, :, :], ALU.subtract))
                    step(v.tensor_tensor(place[:, :, :], pa[:, 0:TT * E].rearrange("p (t e) -> p t e", e=E),
                                         incl[:, :, :].rearrange("p e t -> p t e"), ALU.add))
                    step(v.tensor_tensor(place[:, :, :], place[:, :, :], base[:, :].unsqueeze(1).to_broadcast([P, TT, E]), ALU.add))
                    for k in range(2):
                        step(v.tensor_tensor(work[:, k, :, :], pick[:, k, :, :], place[:, :, :], ALU.mult))
                        step(v.tensor_reduce(slotf[:, k, :], work[:, k, :, :], AX.X, ALU.add))
                    v.tensor_copy(slot[:, :, :], slotf[:, :, :].rearrange("p k t -> p t k")).then_inc(s_slot, 1)
                    step(v.tensor_tensor(owns[:, :, :], io[:, 0:ETILES].unsqueeze(2).to_broadcast([P, ETILES, E]),
                                         ends[:, :].unsqueeze(1).to_broadcast([P, ETILES, E]), ALU.is_ge))
                    step(v.tensor_reduce(ownf[:, :], owns[:, :, :], AX.X, ALU.add))
                    step(v.tensor_scalar(owner[:, :], ownf[:, :], float(E - 1), None, ALU.min))
        if stop < 4:
            return

        CT = FT // P
        with ExitStack() as ctx:
            sb, bank, sem = G["tools"](ctx)
            w12 = sb("w12", [P, 2, KC, 2 * DE])
            w3 = sb("w3", [P, 2, MC + 1, DM])
            yb = sb("yb", [P, 2, CT, DM])
            yT = sb("yT2", [P, KC, FT])
            act_up = sb("act_up", [P, 2, FT])
            hid = sb("hid", [P, 2, MC + 1, FT])
            ob = sb("ob", [P, 2, CT, DM])
            pT = [bank(f"e_pT{i}") for i in range(2)]
            pu = [bank(f"e_pu{i}") for i in range(2)]
            pg = [bank(f"e_pg{i}") for i in range(2)]
            pd = [bank(f"e_pd{i}") for i in range(2)]
            s_w, s_y, s_o = ([sem(f"e_{n}{i}") for i in range(2)] for n in "wyo")
            s_start = sem("e_start")
            s_T, s_yT, s_up, s_silu, s_hid, s_dn, s_ob = (sem(f"e_{n}") for n in ("T", "yT", "up", "silu", "hid", "dn", "ob"))
            UP = MC + 1
            DN = CT // 2

            def tiles_of(engine):
                with engine.Fori(0, ETILES // 2) as i:
                    for par in range(2):
                        yield i, par, 2 * i + par

            CU, CD, CUP, CO = 2 * UP, 2 * DN, 1, 16

            with nc.Block() as block:
                @block.sync
                def _(sp):
                    for i, par, j in tiles_of(sp):
                        sp.wait_ge(s_start, 1)
                        e = sp.value_load(owner[0:1, bass.ds(j, 1)], min_val=0, max_val=E - 1)
                        wait_alone(sp, s_dn, CD + DN * (j - 1), s_start)
                        sp.dma_start(yb[:, par, :, :], y_slots[bass.ds(j * FT, FT), :].rearrange("(c p) n -> p c n", p=P))\
                            .then_inc(s_y[par], 16)
                        sp.dma_start(w12[:, par, :, :], A["W12"][bass.ds(e, 1), :, :].rearrange("a (c p) n -> p (a c) n", p=P))\
                            .then_inc(s_w[par], 16)
                        sp.dma_start(w3[:, par, 0:MC, :], A["W3"][bass.ds(e, 1), 0:MC * P, :].rearrange("a (c p) n -> p (a c) n", p=P))\
                            .then_inc(s_w[par], 16)
                        sp.dma_start(w3[0:MR, par, MC, :], A["W3"][bass.ds(e, 1), MC * P:DE, :].rearrange("a p n -> (a p) n"))\
                            .then_inc(s_w[par], 16)

                @block.tensor
                def _(pe):
                    pe.sem_inc(s_dn, CD)
                    pe.sem_inc(s_up, CUP)
                    for i, par, j in tiles_of(pe):
                        pe.wait_ge(s_y[par], (i + 1) * 16)
                        pe.wait_ge(s_yT, 1 + j)
                        for c in range(KC):
                            for k in range(CT):
                                last = nc.tensor.transpose(pT[c][:, k * P:(k + 1) * P], yb[:, par, k, c * P:(c + 1) * P], ident[:, :])
                        last.then_inc(s_T, 1)
                        pe.wait_ge(s_yT, 2 + j)
                        pe.wait_ge(s_w[par], (i + 1) * 48)
                        for m in range(UP):
                            b = m % 2
                            pe.wait_ge(s_hid, CU + UP * j + m - 1)
                            outs = ((pu[b], m), (pg[b], MC + m)) if m < MC else ((pu[b], 2 * MC),)
                            for o, q in outs:
                                for c in range(KC):
                                    last = nc.tensor.matmul(o[:, 0:FT], w12[:, par, c, q * P:(q + 1) * P], yT[:, c, :],
                                                            start=(c == 0), stop=(c == KC - 1))
                            last.then_inc(s_up, 1)
                        for k in range(CT):
                            if k % 2 == 0:
                                pe.wait_ge(s_hid, CU + UP * (j + 1))
                                pe.wait_ge(s_ob, CD + DN * j + k // 2 - 1)
                            for m in range(MC + 1):
                                r = P if m < MC else MR
                                last = nc.tensor.matmul(pd[k // 2 % 2][:, (k % 2) * DM:(k % 2 + 1) * DM],
                                                        hid[0:r, par, m, k * P:(k + 1) * P], w3[0:r, par, m, :],
                                                        start=(m == 0), stop=(m == MC))
                            if k % 2:
                                last.then_inc(s_dn, 1)

                @block.scalar
                def _(act):
                    act.sem_inc(s_yT, 1)
                    act.sem_inc(s_start, 1)
                    for par in range(2):
                        act.sem_inc(s_o[par], CO)
                    act.sem_inc(s_ob, CD)
                    for i, par, j in tiles_of(act):
                        act.wait_ge(s_T, j + 1)
                        act.wait_ge(s_up, CUP + UP * j)
                        for c in range(KC):
                            last = nc.scalar.activation(yT[:, c, :], pT[c][:, 0:FT], ACT.Copy)
                        last.then_inc(s_yT, 1)
                        for m in range(UP):
                            act.wait_ge(s_up, CUP + UP * j + m + 1)
                            act.wait_ge(s_hid, CU + UP * j + m - 1)
                            r = P if m < MC else MR
                            nc.scalar.activation(act_up[0:r, m % 2, :], pu[m % 2][0:r, 0:FT], ACT.Silu).then_inc(s_silu, 1)
                        act.wait_ge(s_o[par], CO + i * 16)
                        for q in range(DN):
                            act.wait_ge(s_dn, CD + DN * j + q + 1)
                            nc.scalar.activation(ob[:, par, 2 * q:2 * q + 2, :], pd[q % 2][:, :].rearrange("p (k n) -> p k n", k=2),
                                                 ACT.Copy).then_inc(s_ob, 1)
                        wait_alone(act, s_ob, CD + DN * (j + 1), s_start)
                        act.dma_start(o_slots[bass.ds(j * FT, FT), :].rearrange("(c p) n -> p c n", p=P), ob[:, par, :, :])\
                            .then_inc(s_o[par], 16)
                    for par in range(2):
                        act.wait_ge(s_o[par], CO + ETILES // 2 * 16)

                @block.vector
                def _(dve):
                    dve.sem_inc(s_hid, CU)
                    for i, par, j in tiles_of(dve):
                        dve.wait_ge(s_dn, CD + DN * (j - 1))
                        for m in range(UP):
                            dve.wait_ge(s_silu, UP * j + m + 1)
                            r = P if m < MC else MR
                            g = pg[m % 2][:, 0:FT] if m < MC else pu[m % 2][MR:2 * MR, 0:FT]
                            nc.vector.tensor_tensor(hid[0:r, par, m, :], g, act_up[0:r, m % 2, :], ALU.mult).then_inc(s_hid, 1)
        if stop < 5:
            return

        with ExitStack() as ctx:
            sb, bank, sem = G["tools"](ctx)
            RING = 4
            got = sb("got", [P, RING, 2, DM])
            part = sb("part", [P, 2, DM])
            s_g = [sem(f"c_g{i}") for i in range(RING)]
            s_p, s_f, s_out = sem("c_p"), sem("c_f"), sem("c_out")
            out_rows = A["out"].rearrange("b t c -> (b t) c")
            with nc.Block() as block:
                @block.gpsimd
                def _(pool):
                    for t in range(TT):
                        if t >= RING:
                            pool.wait_ge(s_f, t - RING + 1)
                        for k in range(2):
                            pool.indirect_dma_start(out=got[:, t % RING, k, :], out_offset=None, in_=o_slots,
                                                    in_offset=bass.IndirectOffsetOnAxis(ap=slot[:, t, k:k + 1], axis=0))\
                                .then_inc(s_g[t % RING], 16)

                @block.vector
                def _(dve):
                    v = nc.vector
                    for t in range(TT):
                        dve.wait_ge(s_g[t % RING], 32 * (t // RING + 1))
                        if t >= 2:
                            dve.wait_ge(s_f, t - 1)
                        v.scalar_tensor_tensor(part[:, t % 2, :], got[:, t % RING, 0, :], wts[:, 0, t:t + 1], res[:, t, :],
                                               ALU.mult, ALU.add).then_inc(s_p, 1)
                        dve.wait_ge(s_p, t + 1)
                        v.scalar_tensor_tensor(res[:, t, :], got[:, t % RING, 1, :], wts[:, 1, t:t + 1], part[:, t % 2, :],
                                               ALU.mult, ALU.add).then_inc(s_f, 1)

                @block.sync
                def _(sp):
                    for t in range(TT):
                        sp.wait_ge(s_f, t + 1)
                        sp.dma_start(out_rows[t * P:(t + 1) * P, :], res[:, t, :]).then_inc(s_out, 16)
                    sp.wait_ge(s_out, TT * 16)



_F = ("patches", "txt", "ln1_w", "ln2_w", "tokW", "pos", "Wq", "Wk", "Wv", "Wp", "bq", "bk", "bv", "bp",
      "bias", "temp", "gate", "rms_w", "W12", "W3")


def layouts(i):
    g = {k: np.asarray(a) for k, a in i.items()}
    rows = lambda a, n=P: np.ascontiguousarray(np.broadcast_to(a[None, :], (n, a.shape[0])))
    x = g["x"].reshape(BATCH, CHANS, SIDE, PATCH, SIDE, PATCH).transpose(0, 2, 4, 1, 3, 5)
    yy, xx = np.meshgrid(np.arange(SIDE, dtype=np.float32), np.arange(SIDE, dtype=np.float32), indexing="ij")
    omega = np.arange(DM // 4, dtype=np.float32) / np.float32(DM // 4 - 1)
    omega = (np.float32(1.0) / np.float32(10000.0) ** omega).astype(np.float32)
    yy, xx = yy.reshape(-1)[:, None] * omega[None, :], xx.reshape(-1)[:, None] * omega[None, :]
    pos = np.concatenate([np.sin(xx), np.cos(xx), np.sin(yy), np.cos(yy)], axis=1).astype(np.float32)
    seq = np.concatenate([np.arange(NI, SEQ), np.arange(NI)])
    rel = np.clip(seq[:, None] - seq[None, :] + SEQ - 1, 0, TABLE - 1)
    by_head = g["L0_attn_bias_table"][rel].transpose(2, 0, 1)
    bias = np.zeros((P, PAIRS, 3, SEQ), np.float32)
    bias[:, :, 0] = by_head[0::2, :NT].transpose(1, 0, 2)
    bias[:, :, 1] = by_head[1::2, :NT].transpose(1, 0, 2)
    bias[0:NI, :, 2] = by_head[0::2, NT:].transpose(1, 0, 2)
    bias[64:64 + NI, :, 2] = by_head[1::2, NT:].transpose(1, 0, 2)
    w1, w2 = g["L0_ffn_W1"].transpose(0, 2, 1), g["L0_ffn_W2"].transpose(0, 2, 1)
    w12 = np.concatenate([w1[:, :, :MC * P], w2[:, :, :MC * P], w1[:, :, MC * P:], w2[:, :, MC * P:]], axis=2)
    return {
        "patches": np.ascontiguousarray(x.reshape(BATCH * NI, FEAT)),
        "txt": g["txt"],
        "ln1_w": np.ascontiguousarray(g["L0_tok_ln1_w"].reshape(FC, P).T),
        "ln2_w": rows(g["L0_tok_ln2_w"]),
        "tokW": np.ascontiguousarray(g["L0_tok_W"].T),
        "pos": np.ascontiguousarray(np.tile(pos, (BATCH, 1))),
        "Wq": g["L0_attn_Wq"], "Wk": g["L0_attn_Wk"], "Wv": g["L0_attn_Wv"], "Wp": g["L0_attn_Wp"],
        "bq": np.ascontiguousarray(g["L0_attn_bq"].reshape(KC, P).T),
        "bk": np.ascontiguousarray(g["L0_attn_bk"].reshape(KC, P).T),
        "bv": rows(np.concatenate([g["L0_attn_bv"]] * 2)),
        "bp": rows(g["L0_attn_bp"]),
        "bias": bias,
        "temp": rows(g["L0_attn_temperature"]),
        "gate": np.ascontiguousarray(g["L0_ffn_gate_w"].T),
        "rms_w": rows(g["L0_ffn_rms_w"]),
        "W12": np.ascontiguousarray(w12),
        "W3": np.ascontiguousarray(g["L0_ffn_W3"].transpose(0, 2, 1)),
    }


def kernel(**inputs):
    import concourse.bacc as bacc
    from concourse.bass_utils import run_bass_kernel_spmd as run

    nc = bacc.Bacc("TRN2", target_bir_lowering=False, num_devices=1)
    arrays, aps = {}, {}
    for name, a in layouts(inputs).items():
        arrays[f"in_{name}"] = np.ascontiguousarray(a)
        aps[name] = nc.dram_tensor(f"in_{name}", a.shape, mybir.dt.from_np(a.dtype), kind="ExternalInput").ap()
    aps["out"] = nc.dram_tensor("out_0", (BATCH, SEQ, DM), mybir.dt.float32, kind="ExternalOutput").ap()
    build(nc, aps)
    r = run(nc, [arrays], core_ids=[0])
    return r.results[0]["out_0"]
```

```python
import numpy as np
import concourse.bass as bass
from concourse import mybir
from contextlib import ExitStack

BATCH, CHANS, IMG, PATCH = 32, 3, 96, 16
SIDE = IMG // PATCH
NI = SIDE * SIDE
NT = 128
SEQ = NI + NT
TOK = BATCH * SEQ
DM = 256
FEAT = CHANS * PATCH * PATCH
HEADS, HD = 16, 16
PAIRS = HEADS // 2
P = 128
KC = DM // P
FC = FEAT // P
IT = BATCH * NI // P
TT = TOK // P
EXPERTS, DE = 8, 704
TABLE = 499
QW = 2 * NT + 64 + NI
VW = 3 * HD + 1

FT = 512
ETILES = (2 * TOK + EXPERTS * (FT - 1)) // FT
SLOTS = ETILES * FT
MC = DE // P
MR = DE - MC * P
UPC = 2 * MC + 1

ISLANDS = 4


def build(nc, A, stop=9):
    f32, bf16, fp16, i32 = mybir.dt.float32, mybir.dt.bfloat16, mybir.dt.float16, mybir.dt.int32
    ALU, ACT, AX = mybir.AluOpType, mybir.ActivationFunctionType, mybir.AxisListType

    outer = ExitStack()
    with outer:
        def dram(name, shape, dt=f32):
            return nc.dram_tensor(name, shape, dt, kind="Internal").ap()

        h0_img = dram("h0_img", (BATCH * NI, DM))
        xn_img = dram("xn_img", (BATCH * NI, DM))
        xn_txt = dram("xn_txt", (BATCH * NT, DM))
        h1_d = dram("h1_d", (TOK, DM))
        y_slots = dram("y_slots", (SLOTS, DM))
        o_slots = dram("o_slots", (SLOTS, DM))

        def tools(ctx):
            def sb(name, shape, dt=f32):
                return ctx.enter_context(nc.sbuf_tensor(name, shape, dt))

            def bank(name):
                return ctx.enter_context(nc.psum_tensor(name, [P, 512], f32))

            def sem(name):
                return ctx.enter_context(nc.semaphore(name))
            return sb, bank, sem

        sbo, _, semo = tools(outer)
        ident = sbo("ident", [P, P])

        tokenise(nc, A, locals())
        if stop < 2:
            return
        attention(nc, A, locals())
        if stop < 3:
            return
        experts(nc, A, locals(), stop)


def tokenise(nc, A, G):
    f32, ALU, ACT = mybir.dt.float32, mybir.AluOpType, mybir.ActivationFunctionType
    ident, h0_img, xn_img, xn_txt, y_slots = (G[k] for k in ("ident", "h0_img", "xn_img", "xn_txt", "y_slots"))
    eps = 1e-5
    with ExitStack() as ctx:
        sb, bank, sem = G["tools"](ctx)
        px = sb("px", [P, IT, FEAT])
        wt = sb("wt", [P, FC, DM])
        ln1 = sb("ln1", [P, FC])
        ln2 = sb("ln2", [P, DM])
        pe_t = sb("pe_t", [P, IT, DM])
        xT = sb("xT", [P, 2, FC, P])
        z = sb("z", [P, IT, DM])
        xo = sb("xo", [P, IT, DM])
        st1 = sb("st1", [P, IT, 2, 6])
        mv1 = sb("mv1", [P, IT, 2])
        st2 = sb("st2", [P, IT, 6])
        mv2 = sb("mv2", [P, IT, 2])
        st3 = sb("st3", [P, IT, 6])
        mv3 = sb("mv3", [P, IT, 2])
        rs = sb("rs", [P, 4, IT])
        tx = sb("tx", [P, 2, ISLANDS, DM])
        tst = sb("tst", [P, 2, ISLANDS, 6])
        tmv = sb("tmv", [P, 2, ISLANDS, 2])
        trs = sb("trs", [P, 2, 2, ISLANDS])
        zeros = sb("zeros", [P, 1024])
        bt = [bank(f"bt{i}") for i in range(4)]
        bz = [bank(f"bz{i}") for i in range(2)]

        s_zero, s_ident = sem("s_zero"), sem("s_ident")
        s_fill = sem("s_fill")
        s_px = [sem(f"s_px{t}") for t in range(IT)]
        s_w, s_wl = sem("s_w"), sem("s_wl")
        s_mv1, s_std1, s_rs1, s_n1 = sem("s_mv1"), sem("s_std1"), sem("s_rs1"), sem("s_n1")
        s_xTp, s_xTs, s_z = sem("s_xTp"), sem("s_xTs"), sem("s_z")
        s_zc, s_st = sem("s_zc"), sem("s_st")
        s_v2, s_std2, s_rs2, s_n2, s_n2b, s_h0 = (sem(x) for x in ("s_v2", "s_std2", "s_rs2", "s_n2", "s_n2b", "s_h0"))
        s_v3, s_std3, s_rs3, s_n3 = (sem(x) for x in ("s_v3", "s_std3", "s_rs3", "s_n3"))
        s_out = sem("s_out1")
        s_tx = [sem("s_tx0"), sem("s_tx1")]
        s_tst, s_tmv, s_tv, s_tstd, s_trs, s_tn = (sem(x) for x in ("s_tst", "s_tmv", "s_tv", "s_tstd", "s_trs", "s_tn"))
        s_tout = [sem("s_tout0"), sem("s_tout1")]
        s_t1, s_teps = sem("s_t1"), sem("s_teps")
        GROUPS = BATCH // ISLANDS
        x_txt = A["txt"].rearrange("b t c -> (b t) c")
        FILLS = SLOTS * DM // (P * 1024)
        fill_rows = y_slots.rearrange("(p r) c -> p (r c)", p=P)

        with nc.Block() as block:
            @block.sync
            def _(sp):
                for t in range(IT):
                    sp.dma_start(px[:, t, :], A["patches"][t * P:(t + 1) * P, :]).then_inc(s_px[t], 16)
                sp.dma_start(ln1[:, :], A["ln1_w"]).then_inc(s_w, 16)
                sp.dma_start(wt[:, :, :], A["tokW"].rearrange("(c p) n -> p c n", p=P)).then_inc(s_w, 16)
                sp.dma_start(ln2[:, :], A["ln2_w"]).then_inc(s_w, 16)
                sp.dma_start(pe_t[:, :, :], A["pos"].rearrange("(t p) n -> p t n", p=P)).then_inc(s_w, 16)
                for j in range(2):
                    sp.sem_inc(s_tout[j], 16)
                with sp.Fori(0, GROUPS // 2) as i:
                    for j in range(2):
                        rows = bass.ds((2 * i + j) * ISLANDS * P, ISLANDS * P)
                        wait_alone(sp, s_tout[j], 16 + i * 16, s_zero)
                        sp.dma_start(tx[:, j, :, :], x_txt[rows, :].rearrange("(t p) n -> p t n", p=P))\
                            .then_inc(s_tx[j], 16)
                    for j in range(2):
                        rows = bass.ds((2 * i + j) * ISLANDS * P, ISLANDS * P)
                        wait_alone(sp, s_tn, 2 * i + j + 1, s_zero)
                        sp.dma_start(xn_txt[rows, :].rearrange("(t p) n -> p t n", p=P), tx[:, j, :, :])\
                            .then_inc(s_tout[j], 16)
                sp.wait_ge(s_zero, 1)
                with sp.Fori(0, FILLS) as i:
                    sp.dma_start(fill_rows[:, bass.ds(i * 1024, 1024)], zeros[:, :]).then_inc(s_fill, 16)
                for t in range(IT):
                    sp.wait_ge(s_h0, t + 1)
                    sp.dma_start(h0_img[t * P:(t + 1) * P, :], z[:, t, :]).then_inc(s_out, 16)
                for t in range(IT):
                    sp.wait_ge(s_n3, t + 1)
                    sp.dma_start(xn_img[t * P:(t + 1) * P, :], xo[:, t, :]).then_inc(s_out, 16)
                sp.wait_ge(s_out, 2 * IT * 16)
                sp.wait_ge(s_fill, FILLS * 16)
                for j in range(2):
                    sp.wait_ge(s_tout[j], 16 + GROUPS // 2 * 16)

            @block.gpsimd
            def _(pool):
                pool.memset(ident[:, :], 0.0).then_inc(s_ident, 1)
                pool.memset(zeros[:, :], 0.0).then_inc(s_zero, 1)
                pool.wait_ge(s_ident, 1)
                pool.affine_select(out=ident[:, :], in_=ident[:, :], compare_op=ALU.not_equal, fill=1.0, base=0,
                                   pattern=[[-1, P]], channel_multiplier=1).then_inc(s_ident, 1)

            @block.scalar
            def _(act):
                with act.Fori(0, GROUPS // 2) as i:
                    for j in range(2):
                        act.wait_ge(s_tv, 2 * i + j + 1)
                        nc.scalar.activation(trs[:, j, 1, :], trs[:, j, 0, :], ACT.Sqrt).then_inc(s_tstd, 1)
                act.wait_ge(s_mv1, 1)
                nc.scalar.activation(rs[:, 0, :], rs[:, 3, :], ACT.Sqrt).then_inc(s_std1, 1)
                for t in range(IT):
                    act.wait_ge(s_xTp, t + 1)
                    if t >= 2:
                        act.wait_ge(s_z, t - 1)
                    nc.scalar.activation(xT[:, t % 2, 0:4, :], bt[2 * (t % 2)][:, 0:512].rearrange("p (c n) -> p c n", c=4), ACT.Copy)
                    nc.scalar.activation(xT[:, t % 2, 4:6, :], bt[2 * (t % 2) + 1][:, 0:256].rearrange("p (c n) -> p c n", c=2), ACT.Copy)\
                        .then_inc(s_xTs, 1)
                act.wait_ge(s_v2, 1)
                nc.scalar.activation(rs[:, 1, :], rs[:, 3, :], ACT.Sqrt).then_inc(s_std2, 1)
                act.wait_ge(s_v3, 1)
                nc.scalar.activation(rs[:, 2, :], rs[:, 3, :], ACT.Sqrt).then_inc(s_std3, 1)

            @block.tensor
            def _(pe):
                pe.wait_ge(s_ident, 2)
                for t in range(IT + 1):
                    if t < IT:
                        pe.wait_ge(s_n1, t + 1)
                        if t >= 2:
                            pe.wait_ge(s_xTs, t - 1)
                        for c in range(FC):
                            last = nc.tensor.transpose(bt[2 * (t % 2) + c // 4][:, (c % 4) * P:(c % 4 + 1) * P],
                                                       px[:, t, c * P:(c + 1) * P], ident[:, :])
                        last.then_inc(s_xTp, 1)
                    if t >= 1:
                        u = t - 1
                        pe.wait_ge(s_xTs, u + 1)
                        if u == 0:
                            pe.wait_ge(s_wl, 1)
                        if u >= 2:
                            pe.wait_ge(s_zc, u - 1)
                        for c in range(FC):
                            last = nc.tensor.matmul(bz[u % 2][:, 0:DM], xT[:, u % 2, c, :], wt[:, c, :],
                                                    start=(c == 0), stop=(c == FC - 1))
                        last.then_inc(s_z, 1)

            @block.vector
            def _(dve):
                v = nc.vector

                def variance(mv, s_mv_n, s_after):
                    v.tensor_scalar(rs[:, 3, :], mv[:, :, 1], eps, None, ALU.add).then_inc(s_after, 1)

                with dve.Fori(0, GROUPS // 2) as i:
                    for j in range(2):
                        g = 2 * i + j
                        dve.wait_ge(s_tx[j], (i + 1) * 16)
                        for t in range(ISLANDS):
                            v.bn_stats(tst[:, j, t, :], tx[:, j, t, :]).then_inc(s_tst, 1)
                        dve.wait_ge(s_tst, (g + 1) * ISLANDS)
                        v.memset(trs[:, j, 0, :], eps).then_inc(s_teps, 1)
                        for t in range(ISLANDS):
                            v.bn_aggr(tmv[:, j, t, :], tst[:, j, t, :]).then_inc(s_tmv, 1)
                        dve.wait_ge(s_teps, g + 1)
                        dve.wait_ge(s_tmv, (g + 1) * ISLANDS)
                        v.tensor_tensor(trs[:, j, 0, :], trs[:, j, 0, :], tmv[:, j, :, 1], ALU.add).then_inc(s_tv, 1)
                        dve.wait_ge(s_tstd, g + 1)
                        v.reciprocal(trs[:, j, 1, :], trs[:, j, 1, :]).then_inc(s_trs, 1)
                        dve.wait_ge(s_trs, g + 1)
                        for t in range(ISLANDS):
                            last = v.tensor_scalar(tx[:, j, t, :], tx[:, j, t, :], tmv[:, j, t, 0:1],
                                                   trs[:, j, 1, t:t + 1], ALU.subtract, ALU.mult)
                        last.then_inc(s_tn, 1)
                for t in range(IT):
                    dve.wait_ge(s_px[t], 16)
                    for k in range(2):
                        v.bn_stats(st1[:, t, k, :], px[:, t, k * 384:(k + 1) * 384]).then_inc(s_st, 1)
                    dve.wait_ge(s_st, 2 * (t + 1))
                    v.bn_aggr(mv1[:, t, :], st1[:, t, :, :]).then_inc(s_t1, 1)
                dve.wait_ge(s_t1, IT)
                variance(mv1, None, s_mv1)
                dve.wait_ge(s_w, 64)
                for c in range(FC):
                    last = v.tensor_scalar(wt[:, c, :], wt[:, c, :], ln1[:, c:c + 1], None, ALU.mult)
                last.then_inc(s_wl, 1)
                dve.wait_ge(s_std1, 1)
                v.reciprocal(rs[:, 0, :], rs[:, 0, :]).then_inc(s_rs1, 1)
                dve.wait_ge(s_rs1, 1)
                for t in range(IT):
                    v.tensor_scalar(px[:, t, :], px[:, t, :], mv1[:, t, 0:1], rs[:, 0, t:t + 1],
                                    ALU.subtract, ALU.mult).then_inc(s_n1, 1)
                for t in range(IT):
                    dve.wait_ge(s_z, t + 1)
                    v.bn_stats(st2[:, t, :], bz[t % 2][:, 0:DM]).then_inc(s_st, 1)
                    v.tensor_copy(z[:, t, :], bz[t % 2][:, 0:DM]).then_inc(s_zc, 1)
                    dve.wait_ge(s_st, 2 * IT + t + 1)
                    v.bn_aggr(mv2[:, t, :], st2[:, t, :]).then_inc(s_t1, 1)
                dve.wait_ge(s_t1, 2 * IT)
                dve.wait_ge(s_std1, 1)
                variance(mv2, None, s_v2)
                dve.wait_ge(s_std2, 1)
                v.reciprocal(rs[:, 1, :], rs[:, 1, :]).then_inc(s_rs2, 1)
                dve.wait_ge(s_rs2, 1)
                dve.wait_ge(s_zc, IT)
                for t in range(IT):
                    v.tensor_scalar(z[:, t, :], z[:, t, :], mv2[:, t, 0:1], rs[:, 1, t:t + 1],
                                    ALU.subtract, ALU.mult).then_inc(s_n2, 1)
                for t in range(IT):
                    dve.wait_ge(s_n2, t + 1)
                    v.tensor_tensor(z[:, t, :], z[:, t, :], ln2[:, :], ALU.mult).then_inc(s_n2b, 1)
                for t in range(IT):
                    dve.wait_ge(s_n2b, t + 1)
                    v.tensor_tensor(z[:, t, :], z[:, t, :], pe_t[:, t, :], ALU.add).then_inc(s_h0, 1)
                for t in range(IT):
                    dve.wait_ge(s_h0, t + 1)
                    v.bn_stats(st3[:, t, :], z[:, t, :]).then_inc(s_st, 1)
                for t in range(IT):
                    dve.wait_ge(s_st, 3 * IT + t + 1)
                    v.bn_aggr(mv3[:, t, :], st3[:, t, :]).then_inc(s_t1, 1)
                dve.wait_ge(s_t1, 3 * IT)
                variance(mv3, None, s_v3)
                dve.wait_ge(s_std3, 1)
                v.reciprocal(rs[:, 2, :], rs[:, 2, :]).then_inc(s_rs3, 1)
                dve.wait_ge(s_rs3, 1)
                for t in range(IT):
                    v.tensor_scalar(xo[:, t, :], z[:, t, :], mv3[:, t, 0:1], rs[:, 2, t:t + 1],
                                    ALU.subtract, ALU.mult).then_inc(s_n3, 1)


class Turn:

    def __init__(self, i, k):
        self.i, self.k = i, k
        self.b, self.par, self.half = 2 * i + k, k % 2, i + k // 2

    def at(self, d):
        return Turn(self.i, self.k + d)

    def pair(self, p):
        return 8 * self.i * 2 + (8 * self.k + p)


def turns(engine):
    yield Turn(0, 0), True, False
    yield Turn(0, 1), False, False
    with engine.Fori(1, BATCH // 2 - 1) as i:
        yield Turn(i, 0), False, False
        yield Turn(i, 1), False, False
    yield Turn(BATCH // 2 - 1, 0), False, False
    yield Turn(BATCH // 2 - 1, 1), False, True


LEAD = 3
LAG = 1
RING = 4


def ahead(T, p, d, first, last):
    k, q = divmod(p + d, PAIRS)
    if (k < 0 and first) or (k > 0 and last):
        return None
    return T.at(k), q


def last_two(T):
    return isinstance(T.i, int) and T.i == BATCH // 2 - 1


def wait(engine, sem, value):
    if not isinstance(value, int) or value > 0:
        engine.wait_ge(sem, value)


def wait_alone(engine, sem, value, ready):
    engine.wait_ge(ready, 1)
    wait(engine, sem, value)


def attention(nc, A, G):
    f32, bf16, fp16 = mybir.dt.float32, mybir.dt.bfloat16, mybir.dt.float16
    ALU, ACT, AX = mybir.AluOpType, mybir.ActivationFunctionType, mybir.AxisListType
    ident, h0_img, xn_img, xn_txt, h1_d = (G[k] for k in ("ident", "h0_img", "xn_img", "xn_txt", "h1_d"))
    txt_rows = A["txt"].rearrange("b t c -> (b t) c")
    with ExitStack() as ctx:
        sb, bank, sem = G["tools"](ctx)
        w_in = [sb(f"w_{n}", [P, KC, DM]) for n in "qkvp"]
        wq, wk, wv, wp = w_in
        bq, bk = sb("bq", [P, KC]), sb("bk", [P, KC])
        bqs = sb("bqs", [P, KC])
        bv, bp = sb("bv", [P, 2 * DM]), sb("bp", [P, DM])
        bias = sb("bias", [P, PAIRS, 3, SEQ])
        temp = sb("temp", [P, 1])
        scale = sb("scale", [P, 1])
        x_in = sb("x_in", [P, 2, 2, DM])
        xT = sb("xT_a", [P, KC, 2 * P])
        qs = sb("qs", [P, KC, NI + SEQ])
        qm = sb("qm", [P, 2, PAIRS, QW])
        ks = sb("ks", [P, 2, KC, SEQ])
        vf = sb("vf", [P, 2, HEADS, HD])
        vr = sb("vr", [P, 2, HEADS, HD])
        v3 = sb("v3", [P, 2, 2, HEADS, VW], bf16)
        vm = sb("vm", [P, 2, PAIRS, 4, VW], bf16)
        score = sb("score", [P, RING, 3, SEQ])
        prob = sb("prob", [P, RING, 3 * SEQ])
        rmax = sb("rmax", [P, RING, 3])
        pth = sb("pth", [P, RING, 512], fp16)
        ptl = sb("ptl", [P, RING, 512], fp16)
        osum = sb("osum", [P, 2, PAIRS, 4, HD])
        rden = sb("rden", [P, 2, PAIRS, 4])
        on = sb("on", [P, 2, DM])
        oT = sb("oT", [P, KC, SEQ])
        res = sb("res", [P, 2, 2, DM])
        ps_s = [bank(f"ps_s{i}") for i in range(2)]
        ps_t = [bank(f"ps_t{i}") for i in range(2)]
        ps_o = [bank(f"ps_o{i}") for i in range(2)]
        ps_x, ps_y = bank("ps_x"), bank("ps_y")

        s_const, s_init, s_scale, s_bias = sem("s_const"), sem("s_init"), sem("s_scale"), sem("s_bias")
        two = lambda n: [sem(f"{n}{i}") for i in range(2)]
        s_x, s_qm, s_vm, s_res, s_store = two("s_x"), two("s_qm"), two("s_vm"), two("s_res"), two("s_store")
        (s_xT_ps, s_xT, s_q_ps, s_q, s_k_ps, s_k, s_v_ps, s_vf, s_v1, s_vr, s_v2, s_v3) = (
            sem(n) for n in ("a_xT_ps", "a_xT", "a_q_ps", "a_q", "a_k_ps", "a_k", "a_v_ps", "a_vf", "a_v1",
                             "a_vr", "a_v2", "a_v3"))
        (s_S, s_Sb, s_mx, s_shift, s_P, s_PT, s_Ph, s_Pl, s_O, s_Ored) = (
            sem(n) for n in ("a_S", "a_Sb", "a_mx", "a_shift", "a_P", "a_PT", "a_Ph", "a_Pl", "a_O", "a_Ored"))
        s_On, s_On_b, s_oT_ps, s_oT, s_Y, s_rb, s_h1 = (sem(n) for n in ("a_On", "a_On_b", "a_oT_ps", "a_oT", "a_Y", "a_rb", "a_h1"))
        QM, VM = HEADS // KC * 16, 3 * 16

        def rows(T, part):
            return bass.ds(T.b * (NT if part == 0 else NI), NT if part == 0 else NI)

        with nc.Block() as block:
            @block.sync
            def _(sp):
                for w, name in zip(w_in, ("Wq", "Wk", "Wv", "Wp")):
                    sp.dma_start(w[:, :, :], A[name].rearrange("(c p) n -> p c n", p=P)).then_inc(s_const, 16)
                for t, name in ((temp, "temp"), (bq, "bq"), (bk, "bk"), (bv, "bv"), (bp, "bp")):
                    sp.dma_start(t[:, :], A[name]).then_inc(s_const, 16)
                sp.dma_start(bias[:, :, :, :], A["bias"]).then_inc(s_const, 16)

                def load_x(T):
                    wait_alone(sp, s_xT_ps, T.b - 1, s_scale)
                    sp.dma_start(x_in[:, T.par, 0, :], xn_txt[rows(T, 0), :]).then_inc(s_x[T.par], 16)
                    sp.dma_start(x_in[0:NI, T.par, 1, :], xn_img[rows(T, 1), :]).then_inc(s_x[T.par], 16)

                def spread_queries(T):
                    sp.wait_ge(s_q, T.b + 1)
                    for h in range(HEADS // KC):
                        r, q, o = h * HD, h // 2, h % 2
                        to = qm[r:r + HD, T.par, :, :].rearrange("p (c q) n -> p c q n", c=KC)[:, :, q, :]
                        lo, src = ((0, NI), (NT + 64, 0))[o]
                        sp.dma_start(to[:, :, lo:lo + SEQ], qs[r:r + HD, :, src:src + SEQ]).then_inc(s_qm[T.par], 16)

                def spread_values(T):
                    sp.wait_ge(s_v3, T.b + 1)
                    src = v3[0:NI, T.par, 1, :, :].rearrange("p (a b) w -> p a b w", b=2)
                    sp.dma_start(vm[0:NI, T.par, :, 0, :], src[:, :, 0, :]).then_inc(s_vm[T.par], 16)
                    sp.dma_start(vm[NI:2 * NI, T.par, :, 1, :], src[:, :, 1, :]).then_inc(s_vm[T.par], 16)
                    sp.dma_start(vm[2 * NI:3 * NI, T.par, :, 2:4, :], src).then_inc(s_vm[T.par], 16)

                def load_res(T):
                    wait_alone(sp, s_store[T.par], T.half * 32, s_scale)
                    sp.dma_start(res[:, T.par, 0, :], txt_rows[rows(T, 0), :]).then_inc(s_res[T.par], 16)
                    sp.dma_start(res[0:NI, T.par, 1, :], h0_img[rows(T, 1), :]).then_inc(s_res[T.par], 16)

                def store(T):
                    wait_alone(sp, s_h1, T.b + 1, s_scale)
                    sp.dma_start(h1_d[bass.ds(T.b * SEQ + NI, NT), :], res[:, T.par, 0, :]).then_inc(s_store[T.par], 16)
                    sp.dma_start(h1_d[bass.ds(T.b * SEQ, NI), :], res[0:NI, T.par, 1, :]).then_inc(s_store[T.par], 16)

                load_x(Turn(0, 0))
                load_x(Turn(0, 1))
                sp.wait_ge(s_init, 6)
                spread_queries(Turn(0, 0))
                spread_values(Turn(0, 0))
                for T, first, last in turns(sp):
                    if not last_two(T):
                        load_x(T.at(2))
                    load_res(T)
                    if not last:
                        spread_queries(T.at(1))
                    if not first:
                        store(T.at(-1))
                    if not last:
                        spread_values(T.at(1))
                store(Turn(BATCH // 2 - 1, 1))
                for j in range(2):
                    sp.wait_ge(s_store[j], BATCH * 16)

            @block.gpsimd
            def _(pool):
                pool.memset(qm[:, :, :, :], 0.0).then_inc(s_init, 1)
                pool.memset(vm[:, :, :, :, :], 0.0).then_inc(s_init, 1)
                pool.memset(v3[:, :, :, :, VW - 1:VW], 1.0).then_inc(s_init, 1)
                pool.memset(xT[:, :, :], 0.0).then_inc(s_init, 1)

                def rest(T):
                    pool.wait_ge(s_v1, T.b + 1)
                    wait(pool, s_v3, T.b)
                    pool.tensor_tensor(vr[:, :, :, :], vf[:, :, :, :], v3[:, T.par, :, :, 0:HD], ALU.subtract).then_inc(s_vr, 1)

                def second(T):
                    pool.tensor_tensor(v3[:, T.par, :, :, HD:2 * HD], vf[:, :, :, :], v3[:, T.par, :, :, 0:HD],
                                       ALU.subtract).then_inc(s_v2, 1)

                def third(T):
                    pool.wait_ge(s_v2, T.b + 1)
                    pool.tensor_tensor(v3[:, T.par, :, :, 2 * HD:3 * HD], vr[:, :, :, :], v3[:, T.par, :, :, HD:2 * HD],
                                       ALU.subtract).then_inc(s_v3, 1)

                def res_bias(T):
                    pool.wait_ge(s_res[T.par], (T.half + 1) * 32)
                    pool.tensor_tensor(res[:, T.par, 0, :], res[:, T.par, 0, :], bp[:, :], ALU.add)
                    pool.tensor_tensor(res[0:NI, T.par, 1, :], res[0:NI, T.par, 1, :], bp[0:NI, :], ALU.add).then_inc(s_rb, 1)

                def norm(T):
                    pool.wait_ge(s_Ored, T.pair(0) + 8)
                    wait(pool, s_oT_ps, T.b)
                    o_v = on[:, :, :].rearrange("p m (a h d) -> p m a h d", h=2, d=HD)
                    pool.tensor_tensor(o_v[:, 0, :, :, :], osum[:, T.par, :, 0:2, :],
                                       rden[:, T.par, :, 0:2].unsqueeze(3).to_broadcast([P, PAIRS, 2, HD]), ALU.mult)
                    pool.tensor_tensor(o_v[0:NI, 1, :, 0, :], osum[0:NI, T.par, :, 2, :],
                                       rden[0:NI, T.par, :, 2].unsqueeze(2).to_broadcast([NI, PAIRS, HD]), ALU.mult).then_inc(s_On, 1)

                def shift(T, p):
                    n = T.pair(p)
                    pool.wait_ge(s_mx, n + 1)
                    wait(pool, s_PT, n - RING + 1)
                    for lo, k, src in ((0, P, score[:, p % RING, :, 0:P]), (3 * P, NI, score[:, p % RING, :, P:SEQ])):
                        last = pool.tensor_tensor(prob[:, p % RING, lo:lo + 3 * k].rearrange("p (t n) -> p t n", t=3), src,
                                                  rmax[:, p % RING, :].unsqueeze(2).to_broadcast([P, 3, k]), ALU.subtract)
                    last.then_inc(s_shift, 1)

                for f in (rest, second, third):
                    f(Turn(0, 0))
                for p in range(LEAD):
                    shift(Turn(0, 0), p)
                pool.wait_ge(s_const, 160)
                for T, first, last in turns(pool):
                    for p in range(PAIRS):
                        if nxt := ahead(T, p, LEAD, first, last):
                            shift(*nxt)
                        if not first and p == 0:
                            norm(T.at(-1))
                        if p == 2:
                            res_bias(T)
                        if not last and p in (4, 5, 6):
                            (rest, second, third)[p - 4](T.at(1))
                norm(Turn(BATCH // 2 - 1, 1))

            @block.tensor
            def _(pe):
                def xT_(T):
                    pe.wait_ge(s_x[T.par], (T.half + 1) * 32)
                    if isinstance(T.b, int) and T.b == 1:
                        pe.wait_ge(s_k, 1)
                    wait(pe, s_oT, T.b - 2)
                    for c in range(KC):
                        nc.tensor.transpose(ps_x[:, c * 256:c * 256 + NT], x_in[:, T.par, 0, c * P:(c + 1) * P], ident[:, :])
                        last = nc.tensor.transpose(ps_x[:, c * 256 + NT:c * 256 + SEQ], x_in[0:NI, T.par, 1, c * P:(c + 1) * P],
                                                   ident[0:NI, 0:NI])
                    last.then_inc(s_xT_ps, 1)

                def project(out, w):
                    for m in range(KC):
                        for c in range(KC):
                            last = nc.tensor.matmul(out[:, m * SEQ:(m + 1) * SEQ], w[:, c, m * P:(m + 1) * P], xT[:, c, 0:SEQ],
                                                    start=(c == 0), stop=(c == KC - 1))
                    return last

                def q_(T):
                    pe.wait_ge(s_xT, T.b + 1)
                    wait(pe, s_h1, T.b - 2)
                    project(ps_y, wq).then_inc(s_q_ps, 1)

                def k_(T):
                    project(ps_x, wk).then_inc(s_k_ps, 1)

                def v_(T):
                    pe.wait_ge(s_q, T.b + 1)
                    for m in range(2):
                        for c in range(KC):
                            last = nc.tensor.matmul(ps_y[:, m * DM:(m + 1) * DM], xT[:, c, m * P:(m + 1) * P], wv[:, c, :],
                                                    start=(c == 0), stop=(c == KC - 1))
                    last.then_inc(s_v_ps, 1)

                def oT_(T, follows):
                    pe.wait_ge(s_On, T.b + 1)
                    pe.wait_ge(s_On_b, T.b + 1)
                    if follows:
                        pe.wait_ge(s_k, T.b + 3)
                    for c in range(KC):
                        nc.tensor.transpose(ps_x[:, c * 256:c * 256 + NT], on[:, 0, c * P:(c + 1) * P], ident[:, :])
                        last = nc.tensor.transpose(ps_x[:, c * 256 + NT:c * 256 + SEQ], on[0:NI, 1, c * P:(c + 1) * P],
                                                   ident[0:NI, 0:NI])
                    last.then_inc(s_oT_ps, 1)

                def out_(T, follows):
                    pe.wait_ge(s_oT, T.b + 1)
                    if follows:
                        pe.wait_ge(s_vf, T.b + 3)
                    for m, (lo, n) in enumerate(((0, NT), (NT, NI))):
                        for c in range(KC):
                            last = nc.tensor.matmul(ps_y[0:n, m * DM:(m + 1) * DM], oT[:, c, lo:lo + n], wp[:, c, :],
                                                    start=(c == 0), stop=(c == KC - 1))
                    last.then_inc(s_Y, 1)

                def scores(T, p):
                    n = T.pair(p)
                    if p == 0:
                        pe.wait_ge(s_qm[T.par], (T.half + 1) * QM)
                        pe.wait_ge(s_k, T.b + 1)
                    wait(pe, s_Sb, n - 1)
                    c = p // 4
                    out = ps_s[p % 2]
                    for t, lo in enumerate((0, QW - NT, NT)):
                        last = nc.tensor.matmul(out[:, t * SEQ:(t + 1) * SEQ], qm[:, T.par, p, lo:lo + P], ks[:, T.par, c, :], start=True, stop=True)
                    last.then_inc(s_S, 1)

                def turn_probs(T, p):
                    n = T.pair(p)
                    pe.wait_ge(s_P, n + 1)
                    wait(pe, s_Pl, n - 1)
                    out = ps_t[p % 2]
                    for t in range(3):
                        nc.tensor.transpose(out[:, t * P:(t + 1) * P], prob[:, p % RING, t * P:(t + 1) * P], ident[:, :])
                    nc.tensor.transpose(out[0:3 * NI, 3 * P:4 * P], prob[:, p % RING, 3 * P:3 * SEQ], ident[:, :]).then_inc(s_PT, 1)

                def values(T, p):
                    n = T.pair(p)
                    if p == 0:
                        pe.wait_ge(s_vm[T.par], (T.half + 1) * VM)
                    pe.wait_ge(s_Pl, n + 1)
                    wait(pe, s_Ored, n - 1)
                    out = ps_o[p % 2]
                    parts = (pth, ptl)
                    for g, src in enumerate(parts):
                        nc.tensor.matmul(out[:, 0:4 * VW], src[0:3 * NI, p % RING, 3 * P:4 * P], vm[0:3 * NI, T.par, p, :, :],
                                         start=(g == 0), stop=False)
                    for t, (h, k) in enumerate(((2 * p, 1), (2 * p + 1, 1), (2 * p, 2))):
                        for g, src in enumerate(parts):
                            last = nc.tensor.matmul(out[:, t * VW:(t + k) * VW], src[:, p % RING, t * P:(t + 1) * P],
                                                    v3[:, T.par, 0, h:h + k, :], start=False, stop=(g == 1 and t == 2))
                    last.then_inc(s_O, 1)

                pe.wait_ge(s_const, 160)
                pe.wait_ge(s_init, 6)
                T0 = Turn(0, 0)
                for f in (xT_, q_, k_, v_):
                    f(T0)
                xT_(T0.at(1))
                for p in range(LEAD):
                    scores(T0, p)
                for T, first, last in turns(pe):
                    for p in range(PAIRS):
                        if nxt := ahead(T, p, LEAD, first, last):
                            scores(*nxt)
                        turn_probs(T, p)
                        if not last_two(T) and p == PAIRS - 1:
                            xT_(T.at(2))
                        if prev := ahead(T, p, -LAG, first, last):
                            values(*prev)
                        if not last and p < 3:
                            (q_, k_, v_)[p](T.at(1))
                        if not first and p == 3:
                            oT_(T.at(-1), not last)
                        if not first and p == 4:
                            out_(T.at(-1), not last)
                T = Turn(BATCH // 2 - 1, 1)
                for p in range(PAIRS - LAG, PAIRS):
                    values(T, p)
                oT_(T, False)
                out_(T, False)

            @block.scalar
            def _(act):
                def xT_(T):
                    act.wait_ge(s_xT_ps, T.b + 1)
                    wait(act, s_v_ps, T.b)
                    nc.scalar.activation(xT[:, :, 0:SEQ], ps_x[:, :].rearrange("p (c n) -> p c n", c=KC)[:, :, 0:SEQ], ACT.Copy)\
                        .then_inc(s_xT, 1)

                def q_(T):
                    act.wait_ge(s_q_ps, T.b + 1)
                    if not isinstance(T.b, int) or T.b > 0:
                        L = T.at(-1)
                        act.wait_ge(s_qm[L.par], (L.half + 1) * QM)
                    for m in range(KC):
                        for lo, src, k in ((NI, 0, SEQ), (0, NT, NI)):
                            last = nc.scalar.activation(qs[:, m, lo:lo + k], ps_y[:, m * SEQ + src:m * SEQ + src + k], ACT.Identity,
                                                        bias=bqs[:, m:m + 1], scale=scale[:, 0:1])
                    last.then_inc(s_q, 1)

                def k_(T):
                    act.wait_ge(s_k_ps, T.b + 1)
                    wait(act, s_S, T.pair(-8))
                    for m in range(KC):
                        last = nc.scalar.activation(ks[:, T.par, m, :], ps_x[:, m * SEQ:(m + 1) * SEQ], ACT.Identity,
                                                    bias=bk[:, m:m + 1])
                    last.then_inc(s_k, 1)

                def v1_(T):
                    act.wait_ge(s_vf, T.b + 1)
                    wait(act, s_O, T.pair(-8))
                    wait(act, s_vm[T.par], T.half * VM)
                    nc.scalar.activation(v3[:, T.par, :, :, 0:HD], vf[:, :, :, :], ACT.Copy).then_inc(s_v1, 1)

                def oT_(T):
                    act.wait_ge(s_oT_ps, T.b + 1)
                    wait(act, s_Y, T.b)
                    nc.scalar.activation(oT[:, :, :], ps_x[:, :].rearrange("p (c n) -> p c n", c=KC)[:, :, 0:SEQ], ACT.Copy)\
                        .then_inc(s_oT, 1)

                def exps(T, p):
                    act.wait_ge(s_shift, T.pair(p) + 1)
                    nc.scalar.activation(prob[:, p % RING, :], prob[:, p % RING, :], ACT.Exp).then_inc(s_P, 1)

                def high(T, p):
                    n = T.pair(p)
                    act.wait_ge(s_PT, n + 1)
                    wait(act, s_O, n - RING + 1)
                    nc.scalar.activation(pth[:, p % RING, :], ps_t[p % 2][:, :], ACT.Copy).then_inc(s_Ph, 1)

                act.wait_ge(s_const, 160)
                act.wait_ge(s_init, 6)
                T0 = Turn(0, 0)
                act.wait_ge(s_bias, PAIRS + 1)
                for f in (xT_, q_, k_, v1_):
                    f(T0)
                xT_(T0.at(1))
                for p in range(LEAD):
                    exps(T0, p)
                for T, first, last in turns(act):
                    for p in range(PAIRS):
                        high(T, p)
                        if not last_two(T) and p == PAIRS - 1:
                            xT_(T.at(2))
                        if not last and p == 1:
                            k_(T.at(1))
                        if not first and p == 3:
                            oT_(T.at(-1))
                        if not last and p == 3:
                            v1_(T.at(1))
                        if nxt := ahead(T, p, LEAD, first, last):
                            exps(*nxt)
                        if not last and p == 0:
                            q_(T.at(1))
                oT_(Turn(BATCH // 2 - 1, 1))

            @block.vector
            def _(dve):
                v = nc.vector

                def v_(T):
                    dve.wait_ge(s_v_ps, T.b + 1)
                    wait(dve, s_v2, T.b)
                    v.tensor_tensor(vf[:, :, :, :].rearrange("p a h d -> p (a h d)"), ps_y[:, :], bv[:, :], ALU.add)\
                        .then_inc(s_vf, 1)

                def norm_b(T):
                    dve.wait_ge(s_Ored, T.pair(0) + 8)
                    wait(dve, s_oT_ps, T.b)
                    o_v = on[:, :, :].rearrange("p m (a h d) -> p m a h d", h=2, d=HD)
                    v.tensor_tensor(o_v[0:NI, 1, :, 1, :], osum[64:64 + NI, T.par, :, 3, :],
                                    rden[64:64 + NI, T.par, :, 3].unsqueeze(2).to_broadcast([NI, PAIRS, HD]),
                                    ALU.mult).then_inc(s_On_b, 1)

                def h1_(T):
                    dve.wait_ge(s_Y, T.b + 1)
                    dve.wait_ge(s_rb, T.b + 1)
                    v.tensor_tensor(res[:, T.par, 0, :], ps_y[:, 0:DM], res[:, T.par, 0, :], ALU.add)
                    v.tensor_tensor(res[0:NI, T.par, 1, :], ps_y[0:NI, DM:2 * DM], res[0:NI, T.par, 1, :], ALU.add).then_inc(s_h1, 1)

                def biased(T, p):
                    n = T.pair(p)
                    dve.wait_ge(s_S, n + 1)
                    wait(dve, s_shift, n - RING + 1)
                    v.tensor_tensor(score[:, p % RING, :, :].rearrange("p t n -> p (t n)"), ps_s[p % 2][:, 0:3 * SEQ],
                                    bias[:, p, :, :].rearrange("p t n -> p (t n)"), ALU.add).then_inc(s_Sb, 1)
                    dve.wait_ge(s_Sb, n + 1)
                    v.tensor_reduce(rmax[:, p % RING, :], score[:, p % RING, :, :], AX.X, ALU.max).then_inc(s_mx, 1)

                def low(T, p):
                    dve.wait_ge(s_Ph, T.pair(p) + 1)
                    v.tensor_tensor(ptl[:, p % RING, :], ps_t[p % 2][:, :], pth[:, p % RING, :], ALU.subtract).then_inc(s_Pl, 1)

                def sums(T, p):
                    n = T.pair(p)
                    dve.wait_ge(s_O, n + 1)
                    if p == 0:
                        wait(dve, s_On, T.b - 1)
                        wait(dve, s_On_b, T.b - 1)
                    o = ps_o[p % 2][:, 0:4 * VW].rearrange("p (h w) -> p h w", w=VW)
                    v.tensor_reduce(osum[:, T.par, p, :, :], o[:, :, 0:3 * HD].rearrange("p h (k d) -> p h d k", d=HD), AX.X, ALU.add)
                    v.reciprocal(rden[:, T.par, p, :], o[:, :, VW - 1]).then_inc(s_Ored, 1)

                for t in ps_t:
                    v.memset(t[:, :], 0.0).then_inc(s_init, 1)
                dve.wait_ge(s_const, 160)
                chain = sem("a_chain")
                v.tensor_scalar(scale[:, :], temp[:, :], 0.1, 10.0, ALU.max, ALU.min).then_inc(chain, 1)
                dve.wait_ge(chain, 1)
                v.tensor_scalar(scale[:, :], scale[:, :], float(DM) ** 0.5, None, ALU.mult).then_inc(chain, 1)
                dve.wait_ge(chain, 2)
                v.reciprocal(scale[:, :], scale[:, :]).then_inc(s_scale, 1)
                dve.wait_ge(s_scale, 1)
                for p in range(PAIRS):
                    v.tensor_scalar(bias[:, p, :, :], bias[:, p, :, :], scale[:, 0:1], None, ALU.mult).then_inc(s_bias, 1)
                v.tensor_scalar(bqs[:, :], bq[:, :], scale[:, 0:1], None, ALU.mult).then_inc(s_bias, 1)
                dve.wait_ge(s_bias, PAIRS + 1)
                T0 = Turn(0, 0)
                v_(T0)
                for p in range(LEAD):
                    biased(T0, p)
                for T, first, last in turns(dve):
                    for p in range(PAIRS):
                        if nxt := ahead(T, p, LEAD, first, last):
                            biased(*nxt)
                        low(T, p)
                        if prev := ahead(T, p, -LAG, first, last):
                            sums(*prev)
                        if not last and p == 2:
                            v_(T.at(1))
                        if not first and p == 1:
                            norm_b(T.at(-1))
                        if not first and p == 4:
                            h1_(T.at(-1))
                T = Turn(BATCH // 2 - 1, 1)
                for p in range(PAIRS - LAG, PAIRS):
                    sums(T, p)
                norm_b(T)
                h1_(T)



def experts(nc, A, G, stop):
    f32, i32, u32 = mybir.dt.float32, mybir.dt.int32, mybir.dt.uint32
    ALU, ACT, AX = mybir.AluOpType, mybir.ActivationFunctionType, mybir.AxisListType
    ident, h1_d, y_slots, o_slots = (G[k] for k in ("ident", "h1_d", "y_slots", "o_slots"))
    E = EXPERTS
    LIST = (TOK + FT - 1) // FT
    with ExitStack() as keep:
        sbk, _, semk = G["tools"](keep)
        res = sbk("res2", [P, TT, DM])
        slot = sbk("slot", [P, TT, 2], u32)
        wts = sbk("wts", [P, 2, TT])
        owner = sbk("owner", [P, ETILES], i32)

        with ExitStack() as ctx:
            sb, bank, sem = G["tools"](ctx)
            y = sb("y", [P, TT, DM])
            gate = sb("gate", [P, KC, E])
            rms = sb("rms", [P, DM])
            st, mv = sb("st", [P, TT, 6]), sb("mv", [P, TT, 2])
            r1, r2 = sb("r1", [P, TT]), sb("r2", [P, TT])
            va = sb("va", [P, TT])
            x1 = sb("x1", [P, 2, DM])
            yT = sb("yT", [P, 2, KC, P])
            logit = sb("logit", [P, TT, E])
            top = sb("top", [P, TT, 8])
            topi = sb("topi", [P, TT, 8], u32)
            topf = sb("topf", [P, TT, 2])
            ex = sb("ex", [P, TT])
            io_i = sb("io_i", [P, 64], i32)
            io = sb("io", [P, 64])
            pick = sb("pick", [P, 2, TT, E])
            both = sb("both", [P, TT, E])
            below, ones = sb("below", [P, P]), sb("ones", [P, P])
            tot, incl = sb("tot", [P, E, TT]), sb("incl", [P, E, TT])
            place = sb("place", [P, TT, E])
            over = sb("over", [P, E, LIST])
            tiles, ends, base = sb("tiles", [P, E]), sb("ends", [P, E]), sb("base", [P, E])
            work = sb("work", [P, 2, TT, E])
            slotf = sb("slotf", [P, 2, TT])
            owns = sb("owns", [P, ETILES, E])
            ownf = sb("ownf", [P, ETILES])
            pt = [bank(f"r_pt{i}") for i in range(2)]
            pl = [bank(f"r_pl{i}") for i in range(2)]
            pa, pb = bank("r_pa"), bank("r_pb")
            (s_h, s_c, s_st, s_mv, s_v, s_sd, s_r, s_x1, s_y, s_yT_ps, s_yT, s_l, s_lg, s_top, s_io, s_tri, s_both,
             s_cnt, s_d, s_ex, s_step, s_slot, s_sc, s_resid) = (
                sem(f"r{n}") for n in range(24))
            with nc.Block() as block:
                @block.sync
                def _(sp):
                    sp.dma_start(gate[:, :, :], A["gate"].rearrange("(c p) n -> p c n", p=P)).then_inc(s_c, 16)
                    sp.dma_start(rms[:, :], A["rms_w"]).then_inc(s_c, 16)
                    sp.dma_start(res[:, :, :], h1_d.rearrange("(t p) n -> p t n", p=P)).then_inc(s_h, 16)

                @block.gpsimd
                def _(pool):
                    pool.iota(io_i[:, :], pattern=[[1, 64]], base=0, channel_multiplier=0).then_inc(s_io, 1)
                    pool.memset(below[:, :], 1.0).then_inc(s_tri, 1)
                    pool.memset(ones[:, :], 1.0).then_inc(s_tri, 1)
                    pool.wait_ge(s_tri, 2)
                    pool.affine_select(out=below[:, :], in_=below[:, :], compare_op=ALU.is_gt, fill=0.0, base=0,
                                       pattern=[[1, P]], channel_multiplier=-1).then_inc(s_tri, 1)
                    pool.wait_ge(s_slot, 1)
                    for t in range(TT):
                        for k in range(2):
                            pool.indirect_dma_start(out=y_slots, out_offset=bass.IndirectOffsetOnAxis(ap=slot[:, t, k:k + 1], axis=0),
                                                    in_=y[:, t, :], in_offset=None).then_inc(s_sc, 16)
                    pool.wait_ge(s_sc, 2 * TT * 16)

                @block.scalar
                def _(act):
                    act.wait_ge(s_v, 1)
                    nc.scalar.activation(r1[:, :], r1[:, :], ACT.Sqrt).then_inc(s_sd, 1)
                    act.wait_ge(s_v, 2)
                    nc.scalar.activation(r2[:, :], r2[:, :], ACT.Sqrt).then_inc(s_sd, 1)
                    for t in range(TT):
                        act.wait_ge(s_yT_ps, t + 1)
                        if t >= 2:
                            act.wait_ge(s_l, t - 1)
                        nc.scalar.activation(yT[:, t % 2, :, :], pt[t % 2][:, 0:KC * P].rearrange("p (c n) -> p c n", c=KC), ACT.Copy)\
                            .then_inc(s_yT, 1)
                    act.wait_ge(s_d, 1)
                    nc.scalar.activation(ex[:, :], ex[:, :], ACT.Exp).then_inc(s_ex, 1)

                @block.tensor
                def _(pe):
                    pe.wait_ge(s_c, 32)
                    for t in range(TT + 1):
                        if t < TT:
                            pe.wait_ge(s_y, t + 1)
                            if t >= 2:
                                pe.wait_ge(s_yT, t - 1)
                            for c in range(KC):
                                last = nc.tensor.transpose(pt[t % 2][:, c * P:(c + 1) * P], y[:, t, c * P:(c + 1) * P], ident[:, :])
                            last.then_inc(s_yT_ps, 1)
                        if t >= 1:
                            u = t - 1
                            pe.wait_ge(s_yT, u + 1)
                            if u >= 2:
                                pe.wait_ge(s_lg, u - 1)
                            for c in range(KC):
                                last = nc.tensor.matmul(pl[u % 2][:, 0:E], yT[:, u % 2, c, :], gate[:, c, :],
                                                        start=(c == 0), stop=(c == KC - 1))
                            last.then_inc(s_l, 1)
                    pe.wait_ge(s_tri, 3)
                    pe.wait_ge(s_both, 1)
                    flat = both[:, :, :].rearrange("p t e -> p (t e)")
                    nc.tensor.matmul(pa[:, 0:TT * E], below[:, :], flat, start=True, stop=True)
                    nc.tensor.matmul(pb[:, 0:TT * E], ones[:, :], flat, start=True, stop=True).then_inc(s_cnt, 1)

                @block.vector
                def _(dve):
                    v = nc.vector
                    n = [0]

                    def step(ins):
                        n[0] += 1
                        ins.then_inc(s_step, 1)
                        dve.wait_ge(s_step, n[0])

                    dve.wait_ge(s_h, 16)
                    for t in range(TT):
                        v.bn_stats(st[:, t, :], res[:, t, :]).then_inc(s_st, 1)
                    for t in range(TT):
                        dve.wait_ge(s_st, t + 1)
                        v.bn_aggr(mv[:, t, :], st[:, t, :]).then_inc(s_mv, 1)
                    dve.wait_ge(s_mv, TT)
                    step(v.tensor_scalar(va[:, :], mv[:, :, 1], 1e-5, None, ALU.add))
                    v.tensor_copy(r1[:, :], va[:, :]).then_inc(s_v, 1)
                    step(v.reciprocal(va[:, :], va[:, :]))
                    step(v.tensor_tensor(va[:, :], va[:, :], mv[:, :, 1], ALU.mult))
                    v.tensor_scalar(r2[:, :], va[:, :], 1e-6, None, ALU.add).then_inc(s_v, 1)
                    dve.wait_ge(s_sd, 2)
                    step(v.reciprocal(r1[:, :], r1[:, :]))
                    step(v.reciprocal(r2[:, :], r2[:, :]))
                    dve.wait_ge(s_c, 32)
                    for t in range(TT):
                        if t >= 2:
                            dve.wait_ge(s_resid, t - 1)
                        v.tensor_scalar(x1[:, t % 2, :], res[:, t, :], mv[:, t, 0:1], r1[:, t:t + 1],
                                        ALU.subtract, ALU.mult).then_inc(s_x1, 1)
                        dve.wait_ge(s_x1, t + 1)
                        v.scalar_tensor_tensor(y[:, t, :], x1[:, t % 2, :], r2[:, t:t + 1], rms[:, :],
                                               ALU.mult, ALU.mult).then_inc(s_y, 1)
                        v.tensor_tensor(res[:, t, :], res[:, t, :], x1[:, t % 2, :], ALU.add).then_inc(s_resid, 1)
                    for t in range(TT):
                        dve.wait_ge(s_l, t + 1)
                        v.tensor_copy(logit[:, t, :], pl[t % 2][:, 0:E]).then_inc(s_lg, 1)
                        dve.wait_ge(s_lg, t + 1)
                        v.max(top[:, t, :], logit[:, t, :]).then_inc(s_top, 1)
                        dve.wait_ge(s_top, 2 * t + 1)
                        v.max_index(topi[:, t, :], top[:, t, :], logit[:, t, :]).then_inc(s_top, 1)
                    dve.wait_ge(s_top, 2 * TT)
                    v.tensor_tensor(ex[:, :], top[:, :, 1], top[:, :, 0], ALU.subtract).then_inc(s_d, 1)
                    dve.wait_ge(s_io, 1)
                    v.tensor_copy(topf[:, :, :], topi[:, :, 0:2])
                    step(v.tensor_copy(io[:, :], io_i[:, :]))
                    for k in range(2):
                        step(v.tensor_tensor(pick[:, k, :, :], io[:, 0:E].unsqueeze(1).to_broadcast([P, TT, E]),
                                             topf[:, :, k].unsqueeze(2).to_broadcast([P, TT, E]), ALU.is_equal))
                    v.tensor_tensor(both[:, :, :], pick[:, 0, :, :], pick[:, 1, :, :], ALU.add).then_inc(s_both, 1)
                    dve.wait_ge(s_ex, 1)
                    step(v.tensor_scalar(wts[:, 0, :], ex[:, :], 1.0, None, ALU.add))
                    step(v.reciprocal(wts[:, 0, :], wts[:, 0, :]))
                    step(v.tensor_tensor(wts[:, 1, :], ex[:, :], wts[:, 0, :], ALU.mult))
                    dve.wait_ge(s_cnt, 1)
                    step(v.tensor_copy(tot[:, :, :], pb[:, 0:TT * E].rearrange("p (t e) -> p e t", e=E)))
                    for e in range(E):
                        step(v.tensor_tensor_scan(incl[:, e, :], ones[:, 0:TT], tot[:, e, :], 0.0, ALU.mult, ALU.add))
                    step(v.tensor_scalar(ownf[:, 0:LIST], io[:, 0:LIST], float(FT), None, ALU.mult))
                    step(v.tensor_tensor(over[:, :, :], incl[:, :, TT - 1].unsqueeze(2).to_broadcast([P, E, LIST]),
                                         ownf[:, 0:LIST].unsqueeze(1).to_broadcast([P, E, LIST]), ALU.is_gt))
                    step(v.tensor_reduce(tiles[:, :], over[:, :, :], AX.X, ALU.add))
                    step(v.tensor_tensor_scan(ends[:, :], ones[:, 0:E], tiles[:, :], 0.0, ALU.mult, ALU.add))
                    step(v.tensor_tensor(base[:, :], ends[:, :], tiles[:, :], ALU.subtract))
                    step(v.tensor_scalar(base[:, :], base[:, :], float(FT), None, ALU.mult))
                    step(v.tensor_tensor(incl[:, :, :], incl[:, :, :], tot[:, :, :], ALU.subtract))
                    step(v.tensor_tensor(place[:, :, :], pa[:, 0:TT * E].rearrange("p (t e) -> p t e", e=E),
                                         incl[:, :, :].rearrange("p e t -> p t e"), ALU.add))
                    step(v.tensor_tensor(place[:, :, :], place[:, :, :], base[:, :].unsqueeze(1).to_broadcast([P, TT, E]), ALU.add))
                    for k in range(2):
                        step(v.tensor_tensor(work[:, k, :, :], pick[:, k, :, :], place[:, :, :], ALU.mult))
                        step(v.tensor_reduce(slotf[:, k, :], work[:, k, :, :], AX.X, ALU.add))
                    v.tensor_copy(slot[:, :, :], slotf[:, :, :].rearrange("p k t -> p t k")).then_inc(s_slot, 1)
                    step(v.tensor_tensor(owns[:, :, :], io[:, 0:ETILES].unsqueeze(2).to_broadcast([P, ETILES, E]),
                                         ends[:, :].unsqueeze(1).to_broadcast([P, ETILES, E]), ALU.is_ge))
                    step(v.tensor_reduce(ownf[:, :], owns[:, :, :], AX.X, ALU.add))
                    step(v.tensor_scalar(owner[:, :], ownf[:, :], float(E - 1), None, ALU.min))
        if stop < 4:
            return

        f32r = mybir.dt.float32r
        CT = FT // P
        with ExitStack() as ctx:
            sb, bank, sem = G["tools"](ctx)
            w12 = sb("w12", [P, KC, 2 * DE])
            w3 = sb("w3", [P, MC + 1, DM])
            w12h, w12l = sb("w12h", [P, 2, KC, 2 * DE], f32r), sb("w12l", [P, 2, KC, 2 * DE], f32r)
            w3h, w3l = sb("w3h", [P, 2, MC + 1, DM], f32r), sb("w3l", [P, 2, MC + 1, DM], f32r)
            yb = sb("yb", [P, 2, CT, DM])
            yh, yl = sb("yh", [P, KC, FT], f32r), sb("yl", [P, KC, FT], f32r)
            silu = sb("silu", [P, 2, FT])
            prod = sb("prod", [P, 2, FT])
            hh, hl = sb("hh", [P, MC + 1, FT], f32r), sb("hl", [P, MC + 1, FT], f32r)
            ob = sb("ob", [P, CT, DM])
            pT = [bank(f"e_pT{i}") for i in range(2)]
            pu = [bank(f"e_pu{i}") for i in range(2)]
            pg = [bank(f"e_pg{i}") for i in range(2)]
            pd = [bank(f"e_pd{i}") for i in range(2)]
            s_w, s_y = ([sem(f"e_{n}{i}") for i in range(2)] for n in "wy")
            s_start = sem("e_start")
            s_T, s_yh, s_yl, s_up, s_silu, s_prod, s_hh, s_hl, s_dn, s_ob, s_o, s_wh, s_wl = (
                sem(f"e_{n}") for n in ("T", "yh", "yl", "up", "silu", "prod", "hh", "hl", "dn", "ob", "o", "wh", "wl"))
            UP = MC + 1
            DN = CT // 2
            PARTS = KC + 1

            def weight_part(q, par):
                if q < KC:
                    return w12[:, q, :], w12h[:, par, q, :], w12l[:, par, q, :]
                return w3[:, :, :], w3h[:, par, :, :], w3l[:, par, :, :]

            class Tile:
                def __init__(self, i, k):
                    self.i, self.k, self.j, self.par, self.half = i, k, 2 * i + k, k % 2, i + k // 2

                def next(self):
                    return Tile(self.i, self.k + 1)

            def tiles_of(engine):
                with engine.Fori(0, ETILES // 2 - 1) as i:
                    yield Tile(i, 0), False
                    yield Tile(i, 1), False
                yield Tile(ETILES // 2 - 1, 0), False
                yield Tile(ETILES // 2 - 1, 1), True

            CH, CD, CU, CO, CY = 2 * UP, 2 * DN, 2 * UP, 16, 2

            with nc.Block() as block:
                @block.sync
                def _(sp):
                    def load(T):
                        e = sp.value_load(owner[0:1, bass.ds(T.j, 1)], min_val=0, max_val=E - 1)
                        wait_alone(sp, s_T, CY + T.j - 1, s_start)
                        sp.dma_start(yb[:, T.par, :, :], y_slots[bass.ds(T.j * FT, FT), :].rearrange("(c p) n -> p c n", p=P))\
                            .then_inc(s_y[T.par], 16)
                        wait_alone(sp, s_wl, PARTS + PARTS * T.j, s_start)
                        sp.dma_start(w12[:, :, :], A["W12"][bass.ds(e, 1), :, :].rearrange("a (c p) n -> p (a c) n", p=P))\
                            .then_inc(s_w[T.par], 16)
                        sp.dma_start(w3[:, 0:MC, :], A["W3"][bass.ds(e, 1), 0:MC * P, :].rearrange("a (c p) n -> p (a c) n", p=P))\
                            .then_inc(s_w[T.par], 16)
                        sp.dma_start(w3[0:MR, MC, :], A["W3"][bass.ds(e, 1), MC * P:DE, :].rearrange("a p n -> (a p) n"))\
                            .then_inc(s_w[T.par], 16)

                    sp.wait_ge(s_start, 1)
                    load(Tile(0, 0))
                    for T, last in tiles_of(sp):
                        if not last:
                            load(T.next())

                @block.gpsimd
                def _(pool):
                    pool.memset(w3[:, MC, :], 0.0).then_inc(s_start, 1)
                    pool.sem_inc(s_wl, PARTS)

                    def split(T):
                        for q in range(PARTS):
                            raw, high, low = weight_part(q, T.par)
                            pool.wait_ge(s_wh, PARTS * T.j + q + 1)
                            pool.tensor_tensor(low, raw, high.bitcast(f32), ALU.subtract).then_inc(s_wl, 1)

                    split(Tile(0, 0))
                    for T, last in tiles_of(pool):
                        if not last:
                            split(T.next())

                @block.tensor
                def _(pe):
                    pe.sem_inc(s_dn, CD)
                    pe.sem_inc(s_up, CU)
                    pe.sem_inc(s_T, CY)

                    def turn(T):
                        pe.wait_ge(s_y[T.par], (T.half + 1) * 16)
                        pe.wait_ge(s_yl, 1 + T.j)
                        for c in range(KC):
                            for k in range(CT):
                                last = nc.tensor.transpose(pT[c][:, k * P:(k + 1) * P], yb[:, T.par, k, c * P:(c + 1) * P],
                                                           ident[:, :])
                        last.then_inc(s_T, 1)

                    def passes(out, pairs):
                        n = len(pairs)
                        for g, (w, x) in enumerate(pairs):
                            last = nc.tensor.matmul(out, w, x, start=(g == 0), stop=(g == n - 1))
                        return last

                    turn(Tile(0, 0))
                    for T, is_last in tiles_of(pe):
                        par, j = T.par, T.j
                        pe.wait_ge(s_yl, 2 + j)
                        pe.wait_ge(s_wl, PARTS * (j + 2))
                        for m in range(UP):
                            b = m % 2
                            pe.wait_ge(s_prod, CH + UP * j + m - 1)
                            outs = ((pu[b], m), (pg[b], MC + m)) if m < MC else ((pu[b], 2 * MC),)
                            for o, q in outs:
                                cols = slice(q * P, (q + 1) * P)
                                last = passes(o[:, 0:FT], [x for c in range(KC) for x in (
                                    (w12h[:, par, c, cols], yh[:, c, :]), (w12h[:, par, c, cols], yl[:, c, :]),
                                    (w12l[:, par, c, cols], yh[:, c, :]))])
                            last.then_inc(s_up, 1)
                        if not is_last:
                            turn(T.next())
                        for k in range(CT):
                            if k == 0:
                                pe.wait_ge(s_hl, CH + UP * (j + 1))
                            if k % 2 == 0:
                                pe.wait_ge(s_ob, CD + DN * j + k // 2 - 1)
                            toks = slice(k * P, (k + 1) * P)
                            pairs = []
                            for m in range(MC + 1):
                                r = P if m < MC else MR
                                pairs += [(hh[0:r, m, toks], w3h[0:r, par, m, :]), (hh[0:r, m, toks], w3l[0:r, par, m, :]),
                                          (hl[0:r, m, toks], w3h[0:r, par, m, :])]
                            last = passes(pd[k // 2][:, (k % 2) * DM:(k % 2 + 1) * DM], pairs)
                            if k % 2:
                                last.then_inc(s_dn, 1)

                @block.scalar
                def _(act):
                    act.sem_inc(s_ob, CD)
                    act.sem_inc(s_o, CO)

                    def round_weights(T, q):
                        if q == 0:
                            act.wait_ge(s_w[T.par], (T.half + 1) * 48)
                        act.wait_ge(s_dn, CD + DN * (T.j - 1))
                        raw, high, low = weight_part(q, T.par)
                        nc.scalar.activation(high, raw, ACT.Copy).then_inc(s_wh, 1)

                    def round_rows(T):
                        act.wait_ge(s_T, CY + T.j + 1)
                        act.wait_ge(s_up, CU + UP * T.j)
                        for c in range(KC):
                            nc.scalar.activation(yh[:, c, :], pT[c][:, 0:FT], ACT.Copy).then_inc(s_yh, 1)

                    T0 = Tile(0, 0)
                    for q in range(PARTS):
                        round_weights(T0, q)
                    round_rows(T0)
                    for T, last in tiles_of(act):
                        j = T.j
                        for m in range(UP + 1):
                            if m < UP:
                                act.wait_ge(s_up, CU + UP * j + m + 1)
                                act.wait_ge(s_prod, CH + UP * j + m - 1)
                                r = P if m < MC else MR
                                nc.scalar.activation(silu[0:r, m % 2, :], pu[m % 2][0:r, 0:FT], ACT.Silu).then_inc(s_silu, 1)
                            if m >= 1:
                                u = m - 1
                                r = P if u < MC else MR
                                act.wait_ge(s_prod, CH + UP * j + u + 1)
                                if u == 0:
                                    act.wait_ge(s_dn, CD + DN * j)
                                nc.scalar.activation(hh[0:r, u, :], prod[0:r, u % 2, :], ACT.Copy).then_inc(s_hh, 1)
                            if not last and m in (1, 2, 3):
                                round_weights(T.next(), m - 1)
                        if not last:
                            round_rows(T.next())
                        act.wait_ge(s_o, CO + j * 16)
                        for q in range(DN):
                            act.wait_ge(s_dn, CD + DN * j + q + 1)
                            nc.scalar.activation(ob[:, 2 * q:2 * q + 2, :], pd[q][:, :].rearrange("p (k n) -> p k n", k=2),
                                                 ACT.Copy).then_inc(s_ob, 1)
                        wait_alone(act, s_ob, CD + DN * (j + 1), s_start)
                        act.dma_start(o_slots[bass.ds(j * FT, FT), :].rearrange("(c p) n -> p c n", p=P), ob[:, :, :])\
                            .then_inc(s_o, 16)
                    act.wait_ge(s_o, CO + ETILES * 16)

                @block.vector
                def _(dve):
                    v = nc.vector
                    dve.sem_inc(s_prod, CH)
                    dve.sem_inc(s_hl, CH)
                    dve.sem_inc(s_yl, 1)

                    def rest_rows(T):
                        for c in range(KC):
                            dve.wait_ge(s_yh, KC * T.j + c + 1)
                            last = v.tensor_tensor(yl[:, c, :], pT[c][:, 0:FT], yh[:, c, :].bitcast(f32), ALU.subtract)
                        last.then_inc(s_yl, 1)

                    rest_rows(Tile(0, 0))
                    for T, last in tiles_of(dve):
                        j = T.j
                        for m in range(UP + 1):
                            if m < UP:
                                dve.wait_ge(s_silu, UP * j + m + 1)
                                dve.wait_ge(s_hl, CH + UP * j + m - 1)
                                r = P if m < MC else MR
                                g = pg[m % 2][:, 0:FT] if m < MC else pu[m % 2][MR:2 * MR, 0:FT]
                                v.tensor_tensor(prod[0:r, m % 2, :], g, silu[0:r, m % 2, :], ALU.mult).then_inc(s_prod, 1)
                            if m >= 1:
                                u = m - 1
                                r = P if u < MC else MR
                                dve.wait_ge(s_hh, UP * j + u + 1)
                                v.tensor_tensor(hl[0:r, u, :], prod[0:r, u % 2, :], hh[0:r, u, :].bitcast(f32), ALU.subtract)\
                                    .then_inc(s_hl, 1)
                        if not last:
                            rest_rows(T.next())
        if stop < 5:
            return

        with ExitStack() as ctx:
            sb, bank, sem = G["tools"](ctx)
            DEPTH = 4
            got = sb("got", [P, DEPTH, 2, DM])
            part = sb("part", [P, 2, DM])
            s_g = [sem(f"c_g{i}") for i in range(DEPTH)]
            s_p, s_f, s_out = sem("c_p"), sem("c_f"), sem("c_out")
            out_rows = A["out"].rearrange("b t c -> (b t) c")
            with nc.Block() as block:
                @block.gpsimd
                def _(pool):
                    for t in range(TT):
                        if t >= DEPTH:
                            pool.wait_ge(s_f, t - DEPTH + 1)
                        for k in range(2):
                            pool.indirect_dma_start(out=got[:, t % DEPTH, k, :], out_offset=None, in_=o_slots,
                                                    in_offset=bass.IndirectOffsetOnAxis(ap=slot[:, t, k:k + 1], axis=0))\
                                .then_inc(s_g[t % DEPTH], 16)

                @block.vector
                def _(dve):
                    v = nc.vector
                    for t in range(TT):
                        dve.wait_ge(s_g[t % DEPTH], 32 * (t // DEPTH + 1))
                        if t >= 2:
                            dve.wait_ge(s_f, t - 1)
                        v.scalar_tensor_tensor(part[:, t % 2, :], got[:, t % DEPTH, 0, :], wts[:, 0, t:t + 1], res[:, t, :],
                                               ALU.mult, ALU.add).then_inc(s_p, 1)
                        dve.wait_ge(s_p, t + 1)
                        v.scalar_tensor_tensor(res[:, t, :], got[:, t % DEPTH, 1, :], wts[:, 1, t:t + 1], part[:, t % 2, :],
                                               ALU.mult, ALU.add).then_inc(s_f, 1)

                @block.sync
                def _(sp):
                    for t in range(TT):
                        sp.wait_ge(s_f, t + 1)
                        sp.dma_start(out_rows[t * P:(t + 1) * P, :], res[:, t, :]).then_inc(s_out, 16)
                    sp.wait_ge(s_out, TT * 16)



_F = ("patches", "txt", "ln1_w", "ln2_w", "tokW", "pos", "Wq", "Wk", "Wv", "Wp", "bq", "bk", "bv", "bp",
      "bias", "temp", "gate", "rms_w", "W12", "W3")


def layouts(i):
    g = {k: np.asarray(a) for k, a in i.items()}
    rows = lambda a, n=P: np.ascontiguousarray(np.broadcast_to(a[None, :], (n, a.shape[0])))
    x = g["x"].reshape(BATCH, CHANS, SIDE, PATCH, SIDE, PATCH).transpose(0, 2, 4, 1, 3, 5)
    yy, xx = np.meshgrid(np.arange(SIDE, dtype=np.float32), np.arange(SIDE, dtype=np.float32), indexing="ij")
    omega = np.arange(DM // 4, dtype=np.float32) / np.float32(DM // 4 - 1)
    omega = (np.float32(1.0) / np.float32(10000.0) ** omega).astype(np.float32)
    yy, xx = yy.reshape(-1)[:, None] * omega[None, :], xx.reshape(-1)[:, None] * omega[None, :]
    pos = np.concatenate([np.sin(xx), np.cos(xx), np.sin(yy), np.cos(yy)], axis=1).astype(np.float32)
    seq = np.concatenate([np.arange(NI, SEQ), np.arange(NI)])
    rel = np.clip(seq[:, None] - seq[None, :] + SEQ - 1, 0, TABLE - 1)
    by_head = g["L0_attn_bias_table"][rel].transpose(2, 0, 1)
    bias = np.zeros((P, PAIRS, 3, SEQ), np.float32)
    bias[:, :, 0] = by_head[0::2, :NT].transpose(1, 0, 2)
    bias[:, :, 1] = by_head[1::2, :NT].transpose(1, 0, 2)
    bias[0:NI, :, 2] = by_head[0::2, NT:].transpose(1, 0, 2)
    bias[64:64 + NI, :, 2] = by_head[1::2, NT:].transpose(1, 0, 2)
    w1, w2 = g["L0_ffn_W1"].transpose(0, 2, 1), g["L0_ffn_W2"].transpose(0, 2, 1)
    w12 = np.concatenate([w1[:, :, :MC * P], w2[:, :, :MC * P], w1[:, :, MC * P:], w2[:, :, MC * P:]], axis=2)
    return {
        "patches": np.ascontiguousarray(x.reshape(BATCH * NI, FEAT)),
        "txt": g["txt"],
        "ln1_w": np.ascontiguousarray(g["L0_tok_ln1_w"].reshape(FC, P).T),
        "ln2_w": rows(g["L0_tok_ln2_w"]),
        "tokW": np.ascontiguousarray(g["L0_tok_W"].T),
        "pos": np.ascontiguousarray(np.tile(pos, (BATCH, 1))),
        "Wq": g["L0_attn_Wq"], "Wk": g["L0_attn_Wk"], "Wv": g["L0_attn_Wv"], "Wp": g["L0_attn_Wp"],
        "bq": np.ascontiguousarray(g["L0_attn_bq"].reshape(KC, P).T),
        "bk": np.ascontiguousarray(g["L0_attn_bk"].reshape(KC, P).T),
        "bv": rows(np.concatenate([g["L0_attn_bv"]] * 2)),
        "bp": rows(g["L0_attn_bp"]),
        "bias": bias,
        "temp": rows(g["L0_attn_temperature"]),
        "gate": np.ascontiguousarray(g["L0_ffn_gate_w"].T),
        "rms_w": rows(g["L0_ffn_rms_w"]),
        "W12": np.ascontiguousarray(w12),
        "W3": np.ascontiguousarray(g["L0_ffn_W3"].transpose(0, 2, 1)),
    }


def kernel(**inputs):
    import concourse.bacc as bacc
    from concourse.bass_utils import run_bass_kernel_spmd as run

    nc = bacc.Bacc("TRN2", target_bir_lowering=False, num_devices=1)
    arrays, aps = {}, {}
    for name, a in layouts(inputs).items():
        arrays[f"in_{name}"] = np.ascontiguousarray(a)
        aps[name] = nc.dram_tensor(f"in_{name}", a.shape, mybir.dt.from_np(a.dtype), kind="ExternalInput").ap()
    aps["out"] = nc.dram_tensor("out_0", (BATCH, SEQ, DM), mybir.dt.float32, kind="ExternalOutput").ap()
    build(nc, aps)
    r = run(nc, [arrays], core_ids=[0])
    return r.results[0]["out_0"]
```

```python
import numpy as np
import concourse.bass as bass
from concourse import mybir
from contextlib import ExitStack

BATCH, CHANS, IMG, PATCH = 32, 3, 96, 16
SIDE = IMG // PATCH
NI = SIDE * SIDE
NT = 128
SEQ = NI + NT
TOK = BATCH * SEQ
DM = 256
FEAT = CHANS * PATCH * PATCH
HEADS, HD = 16, 16
PAIRS = HEADS // 2
P = 128
KC = DM // P
FC = FEAT // P
IT = BATCH * NI // P
TT = TOK // P
EXPERTS, DE = 8, 704
TABLE = 499
QW = 2 * NT + 64 + NI
VW = 3 * HD + 1

FT = 512
ETILES = (2 * TOK + EXPERTS * (FT - 1)) // FT
SLOTS = ETILES * FT
ST = SLOTS // P
MC = DE // P
MR = DE - MC * P

TGT = 4
TG = BATCH * NT // (TGT * P)


def build(nc, A):
    f32, bf16, fp16, i32 = mybir.dt.float32, mybir.dt.bfloat16, mybir.dt.float16, mybir.dt.int32
    ALU, ACT, AX = mybir.AluOpType, mybir.ActivationFunctionType, mybir.AxisListType

    outer = ExitStack()
    with outer:
        def dram(name, shape, dt=f32):
            return nc.dram_tensor(name, shape, dt, kind="Internal").ap()

        h0_img = dram("h0_img", (BATCH * NI, DM))
        xn_img = dram("xn_img", (BATCH * NI, DM))
        xn_txt = dram("xn_txt", (BATCH * NT, DM))
        h1_d = dram("h1_d", (TOK, DM))
        y_rows = dram("y_rows", (TOK, DM))
        o_rows = dram("o_rows", (2 * TOK + SLOTS, DM))

        def tools(ctx):
            def sb(name, shape, dt=f32):
                return ctx.enter_context(nc.sbuf_tensor(name, shape, dt))

            def bank(name):
                return ctx.enter_context(nc.psum_tensor(name, [P, 512], f32))

            def sem(name):
                return ctx.enter_context(nc.semaphore(name))
            return sb, bank, sem

        sbo, _, semo = tools(outer)
        ident = sbo("ident", [P, P])

        tokenise(nc, A, locals())
        attention(nc, A, locals())
        experts(nc, A, locals())


def tokenise(nc, A, G):
    f32, ALU, ACT = mybir.dt.float32, mybir.AluOpType, mybir.ActivationFunctionType
    ident, h0_img, xn_img, xn_txt = (G[k] for k in ("ident", "h0_img", "xn_img", "xn_txt"))
    eps = 1e-5
    with ExitStack() as ctx:
        sb, bank, sem = G["tools"](ctx)
        px = sb("px", [P, IT, FEAT])
        wt = sb("wt", [P, FC, DM])
        ln1 = sb("ln1", [P, FC])
        ln2 = sb("ln2", [P, DM])
        pe_t = sb("pe_t", [P, IT, DM])
        xT = sb("xT", [P, 2, FC, P])
        z = sb("z", [P, IT, DM])
        xo = sb("xo", [P, IT, DM])
        st1 = sb("st1", [P, IT, 2, 6])
        mv1 = sb("mv1", [P, IT, 2])
        st2 = sb("st2", [P, IT, 6])
        mv2 = sb("mv2", [P, IT, 2])
        st3 = sb("st3", [P, IT, 6])
        mv3 = sb("mv3", [P, IT, 2])
        rs = sb("rs", [P, 4, IT])
        tx = sb("tx", [P, TG, TGT, DM])
        tst = sb("tst", [P, TG, TGT, 6])
        tmv = sb("tmv", [P, TG, TGT, 2])
        trs = sb("trs", [P, TG, 2, TGT])
        bt = [bank(f"bt{i}") for i in range(4)]
        bz = [bank(f"bz{i}") for i in range(2)]

        s_ident = sem("s_ident")
        s_px = [sem(f"s_px{t}") for t in range(IT)]
        s_w, s_wl = sem("s_w"), sem("s_wl")
        s_mv1, s_std1, s_rs1, s_n1 = sem("s_mv1"), sem("s_std1"), sem("s_rs1"), sem("s_n1")
        s_xTp, s_xTs, s_z = sem("s_xTp"), sem("s_xTs"), sem("s_z")
        s_zc, s_st = sem("s_zc"), sem("s_st")
        s_v2, s_std2, s_rs2, s_n2, s_n2b, s_h0 = (sem(x) for x in ("s_v2", "s_std2", "s_rs2", "s_n2", "s_n2b", "s_h0"))
        s_v3, s_std3, s_rs3, s_n3 = (sem(x) for x in ("s_v3", "s_std3", "s_rs3", "s_n3"))
        s_out = sem("s_out1")
        s_tx = [sem(f"s_tx{g}") for g in range(TG)]
        s_tst, s_tmv, s_tv, s_tstd, s_trs, s_tn = (sem(x) for x in ("s_tst", "s_tmv", "s_tv", "s_tstd", "s_trs", "s_tn"))
        s_t1 = sem("s_t1")
        x_txt = A["txt"].rearrange("b t c -> (b t) c")

        def text_rows(rows, g):
            return rows[g * TGT * P:(g + 1) * TGT * P, :].rearrange("(t p) n -> p t n", p=P)

        with nc.Block() as block:
            @block.sync
            def _(sp):
                for t in range(IT):
                    sp.dma_start(px[:, t, :], A["patches"][t * P:(t + 1) * P, :]).then_inc(s_px[t], 16)
                sp.dma_start(ln1[:, :], A["ln1_w"]).then_inc(s_w, 16)
                sp.dma_start(wt[:, :, :], A["tokW"].rearrange("(c p) n -> p c n", p=P)).then_inc(s_w, 16)
                sp.dma_start(ln2[:, :], A["ln2_w"]).then_inc(s_w, 16)
                sp.dma_start(pe_t[:, :, :], A["pos"].rearrange("(t p) n -> p t n", p=P)).then_inc(s_w, 16)
                for g in range(TG):
                    sp.dma_start(tx[:, g, :, :], text_rows(x_txt, g)).then_inc(s_tx[g], 16)
                for g in range(TG):
                    sp.wait_ge(s_tn, g + 1)
                    sp.dma_start(text_rows(xn_txt, g), tx[:, g, :, :]).then_inc(s_out, 16)
                for t in range(IT):
                    sp.wait_ge(s_h0, t + 1)
                    sp.dma_start(h0_img[t * P:(t + 1) * P, :], z[:, t, :]).then_inc(s_out, 16)
                for t in range(IT):
                    sp.wait_ge(s_n3, t + 1)
                    sp.dma_start(xn_img[t * P:(t + 1) * P, :], xo[:, t, :]).then_inc(s_out, 16)
                sp.wait_ge(s_out, (TG + 2 * IT) * 16)

            @block.gpsimd
            def _(pool):
                pool.memset(ident[:, :], 0.0).then_inc(s_ident, 1)
                pool.wait_ge(s_ident, 1)
                pool.affine_select(out=ident[:, :], in_=ident[:, :], compare_op=ALU.not_equal, fill=1.0, base=0,
                                   pattern=[[-1, P]], channel_multiplier=1).then_inc(s_ident, 1)

            @block.scalar
            def _(act):
                act.wait_ge(s_mv1, 1)
                nc.scalar.activation(rs[:, 0, :], rs[:, 3, :], ACT.Sqrt).then_inc(s_std1, 1)
                for t in range(IT + 2):
                    if t < IT:
                        act.wait_ge(s_xTp, t + 1)
                        if t >= 2:
                            act.wait_ge(s_z, t - 1)
                        nc.scalar.activation(xT[:, t % 2, 0:4, :], bt[2 * (t % 2)][:, 0:512].rearrange("p (c n) -> p c n", c=4), ACT.Copy)
                        nc.scalar.activation(xT[:, t % 2, 4:6, :], bt[2 * (t % 2) + 1][:, 0:256].rearrange("p (c n) -> p c n", c=2), ACT.Copy)\
                            .then_inc(s_xTs, 1)
                    if 1 <= t <= IT:
                        act.wait_ge(s_z, t)
                        nc.scalar.activation(z[:, t - 1, :], bz[(t - 1) % 2][:, 0:DM], ACT.Copy).then_inc(s_zc, 1)
                    if t >= 3:
                        act.wait_ge(s_tv, t - 2)
                        nc.scalar.activation(trs[:, t - 3, 1, :], trs[:, t - 3, 0, :], ACT.Sqrt).then_inc(s_tstd, 1)
                act.wait_ge(s_v2, 1)
                nc.scalar.activation(rs[:, 1, :], rs[:, 3, :], ACT.Sqrt).then_inc(s_std2, 1)
                act.wait_ge(s_v3, 1)
                nc.scalar.activation(rs[:, 2, :], rs[:, 3, :], ACT.Sqrt).then_inc(s_std3, 1)

            @block.tensor
            def _(pe):
                pe.wait_ge(s_ident, 2)
                for t in range(IT + 1):
                    if t < IT:
                        pe.wait_ge(s_n1, t + 1)
                        if t >= 2:
                            pe.wait_ge(s_xTs, t - 1)
                        for c in range(FC):
                            last = nc.tensor.transpose(bt[2 * (t % 2) + c // 4][:, (c % 4) * P:(c % 4 + 1) * P],
                                                       px[:, t, c * P:(c + 1) * P], ident[:, :])
                        last.then_inc(s_xTp, 1)
                    if t >= 1:
                        u = t - 1
                        pe.wait_ge(s_xTs, u + 1)
                        if u == 0:
                            pe.wait_ge(s_wl, 1)
                        if u >= 2:
                            pe.wait_ge(s_zc, u - 1)
                        for c in range(FC):
                            last = nc.tensor.matmul(bz[u % 2][:, 0:DM], xT[:, u % 2, c, :], wt[:, c, :],
                                                    start=(c == 0), stop=(c == FC - 1))
                        last.then_inc(s_z, 1)

            @block.vector
            def _(dve):
                v = nc.vector

                def variance(mv, s_after):
                    v.tensor_scalar(rs[:, 3, :], mv[:, :, 1], eps, None, ALU.add).then_inc(s_after, 1)

                for t in range(IT):
                    dve.wait_ge(s_px[t], 16)
                    for k in range(2):
                        v.bn_stats(st1[:, t, k, :], px[:, t, k * 384:(k + 1) * 384]).then_inc(s_st, 1)
                    dve.wait_ge(s_st, 2 * (t + 1))
                    v.bn_aggr(mv1[:, t, :], st1[:, t, :, :]).then_inc(s_t1, 1)
                dve.wait_ge(s_t1, IT)
                variance(mv1, s_mv1)
                dve.wait_ge(s_w, 64)
                for c in range(FC):
                    last = v.tensor_scalar(wt[:, c, :], wt[:, c, :], ln1[:, c:c + 1], None, ALU.mult)
                last.then_inc(s_wl, 1)
                dve.wait_ge(s_std1, 1)
                v.reciprocal(rs[:, 0, :], rs[:, 0, :]).then_inc(s_rs1, 1)
                dve.wait_ge(s_rs1, 1)
                for t in range(IT):
                    v.tensor_scalar(px[:, t, :], px[:, t, :], mv1[:, t, 0:1], rs[:, 0, t:t + 1],
                                    ALU.subtract, ALU.mult).then_inc(s_n1, 1)
                for g in range(TG + 1):
                    if g < TG:
                        dve.wait_ge(s_tx[g], 16)
                        for t in range(TGT):
                            v.bn_stats(tst[:, g, t, :], tx[:, g, t, :]).then_inc(s_tst, 1)
                        dve.wait_ge(s_tst, (g + 1) * TGT)
                        for t in range(TGT):
                            v.bn_aggr(tmv[:, g, t, :], tst[:, g, t, :]).then_inc(s_tmv, 1)
                        dve.wait_ge(s_tmv, (g + 1) * TGT)
                        v.tensor_scalar(trs[:, g, 0, :], tmv[:, g, :, 1], eps, None, ALU.add).then_inc(s_tv, 1)
                    if g >= 1:
                        dve.wait_ge(s_tstd, g)
                        v.reciprocal(trs[:, g - 1, 1, :], trs[:, g - 1, 1, :]).then_inc(s_trs, 1)
                        dve.wait_ge(s_trs, g)
                        for t in range(TGT):
                            last = v.tensor_scalar(tx[:, g - 1, t, :], tx[:, g - 1, t, :], tmv[:, g - 1, t, 0:1],
                                                   trs[:, g - 1, 1, t:t + 1], ALU.subtract, ALU.mult)
                        last.then_inc(s_tn, 1)
                for t in range(IT):
                    dve.wait_ge(s_zc, t + 1)
                    v.bn_stats(st2[:, t, :], z[:, t, :]).then_inc(s_st, 1)
                    dve.wait_ge(s_st, 2 * IT + t + 1)
                    v.bn_aggr(mv2[:, t, :], st2[:, t, :]).then_inc(s_t1, 1)
                dve.wait_ge(s_t1, 2 * IT)
                dve.wait_ge(s_std1, 1)
                variance(mv2, s_v2)
                dve.wait_ge(s_std2, 1)
                v.reciprocal(rs[:, 1, :], rs[:, 1, :]).then_inc(s_rs2, 1)
                dve.wait_ge(s_rs2, 1)
                dve.wait_ge(s_zc, IT)
                for t in range(IT):
                    v.tensor_scalar(z[:, t, :], z[:, t, :], mv2[:, t, 0:1], rs[:, 1, t:t + 1],
                                    ALU.subtract, ALU.mult).then_inc(s_n2, 1)
                for t in range(IT):
                    dve.wait_ge(s_n2, t + 1)
                    v.tensor_tensor(z[:, t, :], z[:, t, :], ln2[:, :], ALU.mult).then_inc(s_n2b, 1)
                for t in range(IT):
                    dve.wait_ge(s_n2b, t + 1)
                    v.tensor_tensor(z[:, t, :], z[:, t, :], pe_t[:, t, :], ALU.add).then_inc(s_h0, 1)
                for t in range(IT):
                    dve.wait_ge(s_h0, t + 1)
                    v.bn_stats(st3[:, t, :], z[:, t, :]).then_inc(s_st, 1)
                for t in range(IT):
                    dve.wait_ge(s_st, 3 * IT + t + 1)
                    v.bn_aggr(mv3[:, t, :], st3[:, t, :]).then_inc(s_t1, 1)
                dve.wait_ge(s_t1, 3 * IT)
                variance(mv3, s_v3)
                dve.wait_ge(s_std3, 1)
                v.reciprocal(rs[:, 2, :], rs[:, 2, :]).then_inc(s_rs3, 1)
                dve.wait_ge(s_rs3, 1)
                for t in range(IT):
                    v.tensor_scalar(xo[:, t, :], z[:, t, :], mv3[:, t, 0:1], rs[:, 2, t:t + 1],
                                    ALU.subtract, ALU.mult).then_inc(s_n3, 1)


class Turn:

    def __init__(self, i, k):
        self.i, self.k = i, k
        self.b, self.par, self.half = 2 * i + k, k % 2, i + k // 2

    def at(self, d):
        return Turn(self.i, self.k + d)

    def pair(self, p):
        return 8 * self.i * 2 + (8 * self.k + p)


def turns(engine):
    yield Turn(0, 0), True, False
    yield Turn(0, 1), False, False
    with engine.Fori(1, BATCH // 2 - 1) as i:
        yield Turn(i, 0), False, False
        yield Turn(i, 1), False, False
    yield Turn(BATCH // 2 - 1, 0), False, False
    yield Turn(BATCH // 2 - 1, 1), False, True


LEAD = 3
LAG = 1
RING = 4


def ahead(T, p, d, first, last):
    k, q = divmod(p + d, PAIRS)
    if (k < 0 and first) or (k > 0 and last):
        return None
    return T.at(k), q


def last_two(T):
    return isinstance(T.i, int) and T.i == BATCH // 2 - 1


def wait(engine, sem, value):
    if not isinstance(value, int) or value > 0:
        engine.wait_ge(sem, value)


def wait_alone(engine, sem, value, ready):
    if not isinstance(value, int):
        engine.wait_ge(ready, 1)
    wait(engine, sem, value)


def attention(nc, A, G):
    f32, bf16, fp16 = mybir.dt.float32, mybir.dt.bfloat16, mybir.dt.float16
    ALU, ACT, AX = mybir.AluOpType, mybir.ActivationFunctionType, mybir.AxisListType
    ident, h0_img, xn_img, xn_txt, h1_d = (G[k] for k in ("ident", "h0_img", "xn_img", "xn_txt", "h1_d"))
    txt_rows = A["txt"].rearrange("b t c -> (b t) c")
    with ExitStack() as ctx:
        sb, bank, sem = G["tools"](ctx)
        w_in = [sb(f"w_{n}", [P, KC, DM]) for n in "qkvp"]
        wq, wk, wv, wp = w_in
        bq, bk = sb("bq", [P, KC]), sb("bk", [P, KC])
        bqs = sb("bqs", [P, KC])
        bv, bp = sb("bv", [P, 2 * DM]), sb("bp", [P, DM])
        bias = sb("bias", [P, PAIRS, 3, SEQ])
        temp = sb("temp", [P, 1])
        scale = sb("scale", [P, 1])
        x_in = sb("x_in", [P, 2, 2, DM])
        xT = sb("xT_a", [P, KC, 2 * P])
        qs = sb("qs", [P, KC, NI + SEQ])
        qm = sb("qm", [P, 2, PAIRS, QW])
        ks = sb("ks", [P, 2, KC, SEQ])
        vf = sb("vf", [P, 2, HEADS, HD])
        vr = sb("vr", [P, 2, HEADS, HD])
        v3 = sb("v3", [P, 2, 2, HEADS, VW], bf16)
        vm = sb("vm", [P, 2, PAIRS, 4, VW], bf16)
        score = sb("score", [P, RING, 3, SEQ])
        prob = sb("prob", [P, RING, 3 * SEQ])
        rmax = sb("rmax", [P, RING, 3])
        pth = sb("pth", [P, RING, 512], fp16)
        ptl = sb("ptl", [P, RING, 512], fp16)
        osum = sb("osum", [P, 2, PAIRS, 4, HD])
        rden = sb("rden", [P, 2, PAIRS, 4])
        on = sb("on", [P, 2, DM])
        oT = sb("oT", [P, KC, SEQ])
        res = sb("res", [P, 2, 2, DM])
        ps_s = [bank(f"ps_s{i}") for i in range(2)]
        ps_t = [bank(f"ps_t{i}") for i in range(2)]
        ps_o = [bank(f"ps_o{i}") for i in range(2)]
        ps_x, ps_y = bank("ps_x"), bank("ps_y")

        s_const, s_init, s_scale, s_bias = sem("s_const"), sem("s_init"), sem("s_scale"), sem("s_bias")
        s_table, s_bqs = sem("s_table"), sem("s_bqs")
        two = lambda n: [sem(f"{n}{i}") for i in range(2)]
        s_x, s_qm, s_vm, s_res, s_store = two("s_x"), two("s_qm"), two("s_vm"), two("s_res"), two("s_store")
        (s_xT_ps, s_xT, s_q_ps, s_q, s_k_ps, s_k, s_v_ps, s_vf, s_v1, s_vr, s_v2, s_v3) = (
            sem(n) for n in ("a_xT_ps", "a_xT", "a_q_ps", "a_q", "a_k_ps", "a_k", "a_v_ps", "a_vf", "a_v1",
                             "a_vr", "a_v2", "a_v3"))
        (s_S, s_Sb, s_mx, s_shift, s_P, s_PT, s_Ph, s_Pl, s_O, s_Ored) = (
            sem(n) for n in ("a_S", "a_Sb", "a_mx", "a_shift", "a_P", "a_PT", "a_Ph", "a_Pl", "a_O", "a_Ored"))
        s_On, s_On_b, s_oT_ps, s_oT, s_Y, s_rb, s_h1 = (sem(n) for n in ("a_On", "a_On_b", "a_oT_ps", "a_oT", "a_Y", "a_rb", "a_h1"))
        QM, VM = HEADS // KC * 16, 3 * 16

        def rows(T, part):
            return bass.ds(T.b * (NT if part == 0 else NI), NT if part == 0 else NI)

        with nc.Block() as block:
            @block.sync
            def _(sp):
                def load_x(T):
                    wait_alone(sp, s_xT_ps, T.b - 1, s_scale)
                    sp.dma_start(x_in[:, T.par, 0, :], xn_txt[rows(T, 0), :]).then_inc(s_x[T.par], 16)
                    sp.dma_start(x_in[0:NI, T.par, 1, :], xn_img[rows(T, 1), :]).then_inc(s_x[T.par], 16)

                def spread_queries(T):
                    sp.wait_ge(s_q, T.b + 1)
                    for h in range(HEADS // KC):
                        r, q, o = h * HD, h // 2, h % 2
                        to = qm[r:r + HD, T.par, :, :].rearrange("p (c q) n -> p c q n", c=KC)[:, :, q, :]
                        lo, src = ((0, NI), (NT + 64, 0))[o]
                        sp.dma_start(to[:, :, lo:lo + SEQ], qs[r:r + HD, :, src:src + SEQ]).then_inc(s_qm[T.par], 16)

                def spread_values(T):
                    sp.wait_ge(s_v3, T.b + 1)
                    src = v3[0:NI, T.par, 1, :, :].rearrange("p (a b) w -> p a b w", b=2)
                    sp.dma_start(vm[0:NI, T.par, :, 0, :], src[:, :, 0, :]).then_inc(s_vm[T.par], 16)
                    sp.dma_start(vm[NI:2 * NI, T.par, :, 1, :], src[:, :, 1, :]).then_inc(s_vm[T.par], 16)
                    sp.dma_start(vm[2 * NI:3 * NI, T.par, :, 2:4, :], src).then_inc(s_vm[T.par], 16)

                def load_res(T):
                    wait_alone(sp, s_store[T.par], T.half * 32, s_scale)
                    sp.dma_start(res[:, T.par, 0, :], txt_rows[rows(T, 0), :]).then_inc(s_res[T.par], 16)
                    sp.dma_start(res[0:NI, T.par, 1, :], h0_img[rows(T, 1), :]).then_inc(s_res[T.par], 16)

                def store(T):
                    wait_alone(sp, s_h1, T.b + 1, s_scale)
                    sp.dma_start(h1_d[bass.ds(T.b * SEQ + NI, NT), :], res[:, T.par, 0, :]).then_inc(s_store[T.par], 16)
                    sp.dma_start(h1_d[bass.ds(T.b * SEQ, NI), :], res[0:NI, T.par, 1, :]).then_inc(s_store[T.par], 16)

                load_x(Turn(0, 0))
                for t, name in ((temp, "temp"), (bq, "bq"), (bk, "bk"), (bv, "bv"), (bp, "bp")):
                    sp.dma_start(t[:, :], A[name]).then_inc(s_const, 16)
                for w, name in zip(w_in, ("Wq", "Wk", "Wv", "Wp")):
                    sp.dma_start(w[:, :, :], A[name].rearrange("(c p) n -> p c n", p=P)).then_inc(s_const, 16)
                sp.dma_start(bias[:, :, :, :], A["bias"]).then_inc(s_table, 16)
                load_x(Turn(0, 1))
                sp.wait_ge(s_init, 6)
                spread_queries(Turn(0, 0))
                spread_values(Turn(0, 0))
                for T, first, last in turns(sp):
                    if not last_two(T):
                        load_x(T.at(2))
                    load_res(T)
                    if not last:
                        spread_queries(T.at(1))
                    if not first:
                        store(T.at(-1))
                    if not last:
                        spread_values(T.at(1))
                store(Turn(BATCH // 2 - 1, 1))
                for j in range(2):
                    sp.wait_ge(s_store[j], BATCH * 16)

            @block.gpsimd
            def _(pool):
                pool.memset(qm[:, :, :, :], 0.0).then_inc(s_init, 1)
                pool.memset(vm[:, :, :, :, :], 0.0).then_inc(s_init, 1)
                pool.memset(v3[:, :, :, :, VW - 1:VW], 1.0).then_inc(s_init, 1)
                pool.memset(xT[:, :, :], 0.0).then_inc(s_init, 1)

                def rest(T):
                    pool.wait_ge(s_v1, T.b + 1)
                    wait(pool, s_v3, T.b)
                    pool.tensor_tensor(vr[:, :, :, :], vf[:, :, :, :], v3[:, T.par, :, :, 0:HD], ALU.subtract).then_inc(s_vr, 1)

                def second(T):
                    pool.tensor_tensor(v3[:, T.par, :, :, HD:2 * HD], vf[:, :, :, :], v3[:, T.par, :, :, 0:HD],
                                       ALU.subtract).then_inc(s_v2, 1)

                def third(T):
                    pool.wait_ge(s_v2, T.b + 1)
                    pool.tensor_tensor(v3[:, T.par, :, :, 2 * HD:3 * HD], vr[:, :, :, :], v3[:, T.par, :, :, HD:2 * HD],
                                       ALU.subtract).then_inc(s_v3, 1)

                def res_bias(T):
                    pool.wait_ge(s_res[T.par], (T.half + 1) * 32)
                    pool.tensor_tensor(res[:, T.par, 0, :], res[:, T.par, 0, :], bp[:, :], ALU.add)
                    pool.tensor_tensor(res[0:NI, T.par, 1, :], res[0:NI, T.par, 1, :], bp[0:NI, :], ALU.add).then_inc(s_rb, 1)

                def norm(T):
                    pool.wait_ge(s_Ored, T.pair(0) + 8)
                    wait(pool, s_oT_ps, T.b)
                    o_v = on[:, :, :].rearrange("p m (a h d) -> p m a h d", h=2, d=HD)
                    pool.tensor_tensor(o_v[:, 0, :, :, :], osum[:, T.par, :, 0:2, :],
                                       rden[:, T.par, :, 0:2].unsqueeze(3).to_broadcast([P, PAIRS, 2, HD]), ALU.mult)
                    pool.tensor_tensor(o_v[0:NI, 1, :, 0, :], osum[0:NI, T.par, :, 2, :],
                                       rden[0:NI, T.par, :, 2].unsqueeze(2).to_broadcast([NI, PAIRS, HD]), ALU.mult).then_inc(s_On, 1)

                def shift(T, p):
                    n = T.pair(p)
                    pool.wait_ge(s_mx, n + 1)
                    wait(pool, s_PT, n - RING + 1)
                    for lo, k, src in ((0, P, score[:, p % RING, :, 0:P]), (3 * P, NI, score[:, p % RING, :, P:SEQ])):
                        last = pool.tensor_tensor(prob[:, p % RING, lo:lo + 3 * k].rearrange("p (t n) -> p t n", t=3), src,
                                                  rmax[:, p % RING, :].unsqueeze(2).to_broadcast([P, 3, k]), ALU.subtract)
                    last.then_inc(s_shift, 1)

                for f in (rest, second, third):
                    f(Turn(0, 0))
                for p in range(LEAD):
                    shift(Turn(0, 0), p)
                pool.wait_ge(s_const, 144)
                for T, first, last in turns(pool):
                    for p in range(PAIRS):
                        if nxt := ahead(T, p, LEAD, first, last):
                            shift(*nxt)
                        if not first and p == 0:
                            norm(T.at(-1))
                        if p == 2:
                            res_bias(T)
                        if not last and p in (4, 5, 6):
                            (rest, second, third)[p - 4](T.at(1))
                norm(Turn(BATCH // 2 - 1, 1))

            @block.tensor
            def _(pe):
                def xT_(T):
                    pe.wait_ge(s_x[T.par], (T.half + 1) * 32)
                    if isinstance(T.b, int) and T.b == 1:
                        pe.wait_ge(s_k, 1)
                    wait(pe, s_oT, T.b - 2)
                    for c in range(KC):
                        nc.tensor.transpose(ps_x[:, c * 256:c * 256 + NT], x_in[:, T.par, 0, c * P:(c + 1) * P], ident[:, :])
                        last = nc.tensor.transpose(ps_x[:, c * 256 + NT:c * 256 + SEQ], x_in[0:NI, T.par, 1, c * P:(c + 1) * P],
                                                   ident[0:NI, 0:NI])
                    last.then_inc(s_xT_ps, 1)

                def project(out, w):
                    for m in range(KC):
                        for c in range(KC):
                            last = nc.tensor.matmul(out[:, m * SEQ:(m + 1) * SEQ], w[:, c, m * P:(m + 1) * P], xT[:, c, 0:SEQ],
                                                    start=(c == 0), stop=(c == KC - 1))
                    return last

                def q_(T):
                    pe.wait_ge(s_xT, T.b + 1)
                    wait(pe, s_h1, T.b - 2)
                    project(ps_y, wq).then_inc(s_q_ps, 1)

                def k_(T):
                    project(ps_x, wk).then_inc(s_k_ps, 1)

                def v_(T):
                    pe.wait_ge(s_q, T.b + 1)
                    for m in range(2):
                        for c in range(KC):
                            last = nc.tensor.matmul(ps_y[:, m * DM:(m + 1) * DM], xT[:, c, m * P:(m + 1) * P], wv[:, c, :],
                                                    start=(c == 0), stop=(c == KC - 1))
                    last.then_inc(s_v_ps, 1)

                def oT_(T, follows):
                    pe.wait_ge(s_On, T.b + 1)
                    pe.wait_ge(s_On_b, T.b + 1)
                    if follows:
                        pe.wait_ge(s_k, T.b + 3)
                    for c in range(KC):
                        nc.tensor.transpose(ps_x[:, c * 256:c * 256 + NT], on[:, 0, c * P:(c + 1) * P], ident[:, :])
                        last = nc.tensor.transpose(ps_x[:, c * 256 + NT:c * 256 + SEQ], on[0:NI, 1, c * P:(c + 1) * P],
                                                   ident[0:NI, 0:NI])
                    last.then_inc(s_oT_ps, 1)

                def out_(T, follows):
                    pe.wait_ge(s_oT, T.b + 1)
                    if follows:
                        pe.wait_ge(s_vf, T.b + 3)
                    for m, (lo, n) in enumerate(((0, NT), (NT, NI))):
                        for c in range(KC):
                            last = nc.tensor.matmul(ps_y[0:n, m * DM:(m + 1) * DM], oT[:, c, lo:lo + n], wp[:, c, :],
                                                    start=(c == 0), stop=(c == KC - 1))
                    last.then_inc(s_Y, 1)

                def scores(T, p):
                    n = T.pair(p)
                    if p == 0:
                        pe.wait_ge(s_qm[T.par], (T.half + 1) * QM)
                        pe.wait_ge(s_k, T.b + 1)
                    wait(pe, s_Sb, n - 1)
                    c = p // 4
                    out = ps_s[p % 2]
                    for t, lo in enumerate((0, QW - NT, NT)):
                        last = nc.tensor.matmul(out[:, t * SEQ:(t + 1) * SEQ], qm[:, T.par, p, lo:lo + P], ks[:, T.par, c, :], start=True, stop=True)
                    last.then_inc(s_S, 1)

                def turn_probs(T, p):
                    n = T.pair(p)
                    pe.wait_ge(s_P, n + 1)
                    wait(pe, s_Pl, n - 1)
                    out = ps_t[p % 2]
                    for t in range(3):
                        nc.tensor.transpose(out[:, t * P:(t + 1) * P], prob[:, p % RING, t * P:(t + 1) * P], ident[:, :])
                    nc.tensor.transpose(out[0:3 * NI, 3 * P:4 * P], prob[:, p % RING, 3 * P:3 * SEQ], ident[:, :]).then_inc(s_PT, 1)

                def values(T, p):
                    n = T.pair(p)
                    if p == 0:
                        pe.wait_ge(s_vm[T.par], (T.half + 1) * VM)
                    pe.wait_ge(s_Pl, n + 1)
                    wait(pe, s_Ored, n - 1)
                    out = ps_o[p % 2]
                    parts = (pth, ptl)
                    for g, src in enumerate(parts):
                        nc.tensor.matmul(out[:, 0:4 * VW], src[0:3 * NI, p % RING, 3 * P:4 * P], vm[0:3 * NI, T.par, p, :, :],
                                         start=(g == 0), stop=False)
                    for t, (h, k) in enumerate(((2 * p, 1), (2 * p + 1, 1), (2 * p, 2))):
                        for g, src in enumerate(parts):
                            last = nc.tensor.matmul(out[:, t * VW:(t + k) * VW], src[:, p % RING, t * P:(t + 1) * P],
                                                    v3[:, T.par, 0, h:h + k, :], start=False, stop=(g == 1 and t == 2))
                    last.then_inc(s_O, 1)

                pe.wait_ge(s_const, 144)
                pe.wait_ge(s_init, 6)
                T0 = Turn(0, 0)
                for f in (xT_, q_, k_, v_):
                    f(T0)
                xT_(T0.at(1))
                for p in range(LEAD):
                    scores(T0, p)
                for T, first, last in turns(pe):
                    for p in range(PAIRS):
                        if nxt := ahead(T, p, LEAD, first, last):
                            scores(*nxt)
                        turn_probs(T, p)
                        if not last_two(T) and p == PAIRS - 1:
                            xT_(T.at(2))
                        if prev := ahead(T, p, -LAG, first, last):
                            values(*prev)
                        if not last and p < 3:
                            (q_, k_, v_)[p](T.at(1))
                        if not first and p == 3:
                            oT_(T.at(-1), not last)
                        if not first and p == 4:
                            out_(T.at(-1), not last)
                T = Turn(BATCH // 2 - 1, 1)
                for p in range(PAIRS - LAG, PAIRS):
                    values(T, p)
                oT_(T, False)
                out_(T, False)

            @block.scalar
            def _(act):
                def xT_(T):
                    act.wait_ge(s_xT_ps, T.b + 1)
                    wait(act, s_v_ps, T.b)
                    nc.scalar.activation(xT[:, :, 0:SEQ], ps_x[:, :].rearrange("p (c n) -> p c n", c=KC)[:, :, 0:SEQ], ACT.Copy)\
                        .then_inc(s_xT, 1)

                def q_(T):
                    act.wait_ge(s_q_ps, T.b + 1)
                    if not isinstance(T.b, int) or T.b > 0:
                        L = T.at(-1)
                        act.wait_ge(s_qm[L.par], (L.half + 1) * QM)
                    for m in range(KC):
                        for lo, src, k in ((NI, 0, SEQ), (0, NT, NI)):
                            last = nc.scalar.activation(qs[:, m, lo:lo + k], ps_y[:, m * SEQ + src:m * SEQ + src + k], ACT.Identity,
                                                        bias=bqs[:, m:m + 1], scale=scale[:, 0:1])
                    last.then_inc(s_q, 1)

                def k_(T):
                    act.wait_ge(s_k_ps, T.b + 1)
                    wait(act, s_S, T.pair(-8))
                    for m in range(KC):
                        last = nc.scalar.activation(ks[:, T.par, m, :], ps_x[:, m * SEQ:(m + 1) * SEQ], ACT.Identity,
                                                    bias=bk[:, m:m + 1])
                    last.then_inc(s_k, 1)

                def v1_(T):
                    act.wait_ge(s_vf, T.b + 1)
                    wait(act, s_O, T.pair(-8))
                    wait(act, s_vm[T.par], T.half * VM)
                    nc.scalar.activation(v3[:, T.par, :, :, 0:HD], vf[:, :, :, :], ACT.Copy).then_inc(s_v1, 1)

                def oT_(T):
                    act.wait_ge(s_oT_ps, T.b + 1)
                    wait(act, s_Y, T.b)
                    nc.scalar.activation(oT[:, :, :], ps_x[:, :].rearrange("p (c n) -> p c n", c=KC)[:, :, 0:SEQ], ACT.Copy)\
                        .then_inc(s_oT, 1)

                def exps(T, p):
                    act.wait_ge(s_shift, T.pair(p) + 1)
                    nc.scalar.activation(prob[:, p % RING, :], prob[:, p % RING, :], ACT.Exp).then_inc(s_P, 1)

                def high(T, p):
                    n = T.pair(p)
                    act.wait_ge(s_PT, n + 1)
                    wait(act, s_O, n - RING + 1)
                    nc.scalar.activation(pth[:, p % RING, :], ps_t[p % 2][:, :], ACT.Copy).then_inc(s_Ph, 1)

                act.wait_ge(s_const, 144)
                act.wait_ge(s_init, 6)
                T0 = Turn(0, 0)
                act.wait_ge(s_bqs, 1)
                for f in (xT_, q_, k_, v1_):
                    f(T0)
                xT_(T0.at(1))
                for p in range(LEAD):
                    exps(T0, p)
                for T, first, last in turns(act):
                    for p in range(PAIRS):
                        high(T, p)
                        if not last_two(T) and p == PAIRS - 1:
                            xT_(T.at(2))
                        if not last and p == 1:
                            k_(T.at(1))
                        if not first and p == 3:
                            oT_(T.at(-1))
                        if not last and p == 3:
                            v1_(T.at(1))
                        if nxt := ahead(T, p, LEAD, first, last):
                            exps(*nxt)
                        if not last and p == 0:
                            q_(T.at(1))
                oT_(Turn(BATCH // 2 - 1, 1))

            @block.vector
            def _(dve):
                v = nc.vector

                def v_(T):
                    dve.wait_ge(s_v_ps, T.b + 1)
                    wait(dve, s_v2, T.b)
                    v.tensor_tensor(vf[:, :, :, :].rearrange("p a h d -> p (a h d)"), ps_y[:, :], bv[:, :], ALU.add)\
                        .then_inc(s_vf, 1)

                def norm_b(T):
                    dve.wait_ge(s_Ored, T.pair(0) + 8)
                    wait(dve, s_oT_ps, T.b)
                    o_v = on[:, :, :].rearrange("p m (a h d) -> p m a h d", h=2, d=HD)
                    v.tensor_tensor(o_v[0:NI, 1, :, 1, :], osum[64:64 + NI, T.par, :, 3, :],
                                    rden[64:64 + NI, T.par, :, 3].unsqueeze(2).to_broadcast([NI, PAIRS, HD]),
                                    ALU.mult).then_inc(s_On_b, 1)

                def h1_(T):
                    dve.wait_ge(s_Y, T.b + 1)
                    dve.wait_ge(s_rb, T.b + 1)
                    v.tensor_tensor(res[:, T.par, 0, :], ps_y[:, 0:DM], res[:, T.par, 0, :], ALU.add)
                    v.tensor_tensor(res[0:NI, T.par, 1, :], ps_y[0:NI, DM:2 * DM], res[0:NI, T.par, 1, :], ALU.add).then_inc(s_h1, 1)

                def biased(T, p):
                    n = T.pair(p)
                    dve.wait_ge(s_S, n + 1)
                    wait(dve, s_shift, n - RING + 1)
                    v.tensor_tensor(score[:, p % RING, :, :].rearrange("p t n -> p (t n)"), ps_s[p % 2][:, 0:3 * SEQ],
                                    bias[:, p, :, :].rearrange("p t n -> p (t n)"), ALU.add).then_inc(s_Sb, 1)
                    dve.wait_ge(s_Sb, n + 1)
                    v.tensor_reduce(rmax[:, p % RING, :], score[:, p % RING, :, :], AX.X, ALU.max).then_inc(s_mx, 1)

                def low(T, p):
                    dve.wait_ge(s_Ph, T.pair(p) + 1)
                    v.tensor_tensor(ptl[:, p % RING, :], ps_t[p % 2][:, :], pth[:, p % RING, :], ALU.subtract).then_inc(s_Pl, 1)

                def sums(T, p):
                    n = T.pair(p)
                    dve.wait_ge(s_O, n + 1)
                    if p == 0:
                        wait(dve, s_On, T.b - 1)
                        wait(dve, s_On_b, T.b - 1)
                    o = ps_o[p % 2][:, 0:4 * VW].rearrange("p (h w) -> p h w", w=VW)
                    v.tensor_reduce(osum[:, T.par, p, :, :], o[:, :, 0:3 * HD].rearrange("p h (k d) -> p h d k", d=HD), AX.X, ALU.add)
                    v.reciprocal(rden[:, T.par, p, :], o[:, :, VW - 1]).then_inc(s_Ored, 1)

                for t in ps_t:
                    v.memset(t[:, :], 0.0).then_inc(s_init, 1)
                dve.wait_ge(s_const, 144)
                chain = sem("a_chain")
                v.tensor_scalar(scale[:, :], temp[:, :], 0.1, 10.0, ALU.max, ALU.min).then_inc(chain, 1)
                dve.wait_ge(chain, 1)
                v.tensor_scalar(scale[:, :], scale[:, :], float(DM) ** 0.5, None, ALU.mult).then_inc(chain, 1)
                dve.wait_ge(chain, 2)
                v.reciprocal(scale[:, :], scale[:, :]).then_inc(s_scale, 1)
                dve.wait_ge(s_scale, 1)
                v.tensor_scalar(bqs[:, :], bq[:, :], scale[:, 0:1], None, ALU.mult).then_inc(s_bqs, 1)
                T0 = Turn(0, 0)
                v_(T0)
                dve.wait_ge(s_table, 16)
                for p in range(PAIRS):
                    v.tensor_scalar(bias[:, p, :, :], bias[:, p, :, :], scale[:, 0:1], None, ALU.mult).then_inc(s_bias, 1)
                dve.wait_ge(s_bias, PAIRS)
                for p in range(LEAD):
                    biased(T0, p)
                for T, first, last in turns(dve):
                    for p in range(PAIRS):
                        if nxt := ahead(T, p, LEAD, first, last):
                            biased(*nxt)
                        low(T, p)
                        if prev := ahead(T, p, -LAG, first, last):
                            sums(*prev)
                        if not last and p == 2:
                            v_(T.at(1))
                        if not first and p == 1:
                            norm_b(T.at(-1))
                        if not first and p == 4:
                            h1_(T.at(-1))
                T = Turn(BATCH // 2 - 1, 1)
                for p in range(PAIRS - LAG, PAIRS):
                    sums(T, p)
                norm_b(T)
                h1_(T)


def experts(nc, A, G):
    f32, i32, u32 = mybir.dt.float32, mybir.dt.int32, mybir.dt.uint32
    ALU, ACT, AX = mybir.AluOpType, mybir.ActivationFunctionType, mybir.AxisListType
    bf16 = mybir.dt.bfloat16
    ident, h1_d, y_rows, o_rows = (G[k] for k in ("ident", "h1_d", "y_rows", "o_rows"))
    E = EXPERTS
    LIST = (TOK + FT - 1) // FT
    with ExitStack() as keep:
        sbk, _, semk = G["tools"](keep)
        res = sbk("res2", [P, TT, DM])
        source = sbk("source", [P, ST], u32)
        target = sbk("target", [P, ST], u32)
        wts = sbk("wts", [P, 2, TT])
        owner = sbk("owner", [P, ETILES], i32)

        with ExitStack() as ctx:
            sb, bank, sem = G["tools"](ctx)
            y = sb("y", [P, TT, DM])
            gate = sb("gate", [P, KC, E])
            rms = sb("rms", [P, DM])
            RX = 4
            st, mv = sb("st", [P, TT, 6]), sb("mv", [P, TT, 2])
            r1, r2 = sb("r1", [P, TT]), sb("r2", [P, TT])
            va = sb("va", [P, TT])
            x1 = sb("x1", [P, RX, DM])
            shift = sb("shift", [P, TT])
            yT = sb("yT", [P, 2, KC, P])
            logit = sb("logit", [P, TT, E])
            top = sb("top", [P, TT, 8])
            topi = sb("topi", [P, TT, 8], u32)
            topf = sb("topf", [P, TT, 2])
            ex = sb("ex", [P, TT])
            io_i = sb("io_i", [P, 64], i32)
            io = sb("io", [P, 64])
            pick = sb("pick", [P, 2, TT, E])
            both = sb("both", [P, TT, E])
            below, ones = sb("below", [P, P]), sb("ones", [P, P])
            tot, incl = sb("tot", [P, E, TT]), sb("incl", [P, E, TT])
            place = sb("place", [P, TT, E])
            over = sb("over", [P, E, LIST])
            tiles, ends, base = sb("tiles", [P, E]), sb("ends", [P, E]), sb("base", [P, E])
            work = sb("work", [P, 2, TT, E])
            slotf = sb("slotf", [P, 2, TT])
            slot_i = sb("slot_i", [P, 2, TT], i32)
            s_row, s_col = sb("s_row", [P, 2, TT]), sb("s_col", [P, 2, TT])
            in_row = sb("in_row", [P, 2, TT, P], bf16)
            in_col = sb("in_col", [P, 2, TT, 3 * ST], bf16)
            num = sb("num", [P, 2, TT])
            seq_i = sb("seq_i", [P, 4, P], i32)
            seq = sb("seq", [P, 4, P])
            held, real, dump = sb("held", [P, ST]), sb("real", [P, ST]), sb("dump", [P, ST])
            owns = sb("owns", [P, ETILES, E])
            ownf = sb("ownf", [P, ETILES])
            pt = [bank(f"r_pt{i}") for i in range(2)]
            pl = bank("r_pl")
            pa, pb, pc = bank("r_pa"), bank("r_pb"), bank("r_pc")
            s_seq, s_in_row, s_in_col, s_in_tile, s_in_rows, s_held = (
                sem(f"r_{n}") for n in ("seq", "in_row", "in_col", "in_tile", "in_rows", "held"))
            (s_c, s_st, s_mv, s_v, s_sd, s_x1, s_y, s_yT_ps, s_yT, s_l, s_lg, s_top,
             s_io, s_tri, s_both, s_cnt, s_d, s_ex, s_step, s_sc, s_resid) = (
                sem(f"r_{n}") for n in ("weights", "stats", "mean_var", "variance", "root", "normed", "y", "yT_ps", "yT", "logits_ps",
                                       "logits", "top", "iota", "triangle", "both", "counts", "difference", "exp", "step", "stored", "residual"))
            GROUPS = [(lo, min(lo + 11, TT)) for lo in range(0, TT, 11)]
            s_h = [sem(f"r_h{i}") for i in range(len(GROUPS))]
            s_shiftc = sem("r_shift")
            with nc.Block() as block:
                @block.sync
                def _(sp):
                    sp.dma_start(gate[:, :, :], A["gate"].rearrange("(c p) n -> p c n", p=P)).then_inc(s_c, 16)
                    sp.dma_start(rms[:, :], A["rms_w"]).then_inc(s_c, 16)
                    for i, (lo, hi) in enumerate(GROUPS):
                        sp.dma_start(res[:, lo:hi, :], h1_d[lo * P:hi * P, :].rearrange("(t p) n -> p t n", p=P)).then_inc(s_h[i], 16)
                    sp.wait_ge(s_y, TT)
                    sp.dma_start(y_rows.rearrange("(t p) n -> p t n", p=P), y[:, :, :]).then_inc(s_sc, 16)
                    sp.wait_ge(s_sc, 16)

                @block.gpsimd
                def _(pool):
                    pool.iota(io_i[:, :], pattern=[[1, 64]], base=0, channel_multiplier=0).then_inc(s_io, 1)
                    pool.memset(below[:, :], 1.0).then_inc(s_tri, 1)
                    pool.memset(ones[:, :], 1.0).then_inc(s_tri, 1)
                    pool.wait_ge(s_tri, 2)
                    pool.affine_select(out=below[:, :], in_=below[:, :], compare_op=ALU.is_gt, fill=0.0, base=0,
                                       pattern=[[1, P]], channel_multiplier=-1).then_inc(s_tri, 1)
                    for t in range(TT):
                        pool.wait_ge(s_x1, t + 1)
                        pool.tensor_tensor(res[:, t, :], res[:, t, :], x1[:, t % RX, :], ALU.add).then_inc(s_resid, 1)
                    pool.iota(seq_i[:, 0, :], pattern=[[1, P]], base=0, channel_multiplier=0).then_inc(s_seq, 1)
                    pool.iota(seq_i[:, 1, :], pattern=[[P, P]], base=0, channel_multiplier=0).then_inc(s_seq, 1)
                    pool.iota(seq_i[:, 2, :], pattern=[[P, P]], base=2 * TOK, channel_multiplier=1).then_inc(s_seq, 1)
                    pool.iota(seq_i[:, 3, :], pattern=[[0, P]], base=0, channel_multiplier=1).then_inc(s_seq, 1)
                    for k in range(2):
                        pool.wait_ge(s_in_col, k + 1)
                        pool.tensor_tensor(in_col[:, k, :, ST:2 * ST], in_col[:, k, :, 0:ST],
                                           num[:, k, :].unsqueeze(2).to_broadcast([P, TT, ST]), ALU.mult).then_inc(s_in_tile, 1)

                @block.scalar
                def _(act):
                    act.wait_ge(s_v, 1)
                    nc.scalar.activation(r1[:, :], r1[:, :], ACT.Sqrt).then_inc(s_sd, 1)
                    act.wait_ge(s_v, 2)
                    nc.scalar.activation(r2[:, :], r2[:, :], ACT.Sqrt).then_inc(s_sd, 1)
                    act.wait_ge(s_shiftc, 1)
                    for t in range(TT + RX):
                        if t < TT:
                            if t >= RX:
                                act.wait_ge(s_y, t - RX + 1)
                                act.wait_ge(s_resid, t - RX + 1)
                            nc.scalar.activation(x1[:, t % RX, :], res[:, t, :], ACT.Identity, bias=shift[:, t:t + 1],
                                                 scale=r1[:, t:t + 1]).then_inc(s_x1, 1)
                        t -= RX
                        if t < 0:
                            continue
                        act.wait_ge(s_yT_ps, t + 1)
                        if t >= 2:
                            act.wait_ge(s_l, t - 1)
                        nc.scalar.activation(yT[:, t % 2, :, :], pt[t % 2][:, 0:KC * P].rearrange("p (c n) -> p c n", c=KC), ACT.Copy)\
                            .then_inc(s_yT, 1)
                    act.wait_ge(s_d, 1)
                    nc.scalar.activation(ex[:, :], ex[:, :], ACT.Exp).then_inc(s_ex, 1)
                    for k in range(2):
                        act.wait_ge(s_in_col, k + 1)
                        nc.scalar.activation(in_col[:, k, :, 2 * ST:3 * ST], in_col[:, k, :, 0:ST], ACT.Copy,
                                             scale=seq[:, 3, 0:1]).then_inc(s_in_rows, 1)

                @block.tensor
                def _(pe):
                    pe.wait_ge(s_c, 32)
                    for t in range(TT + 1):
                        if t < TT:
                            pe.wait_ge(s_y, t + 1)
                            if t >= 2:
                                pe.wait_ge(s_yT, t - 1)
                            for c in range(KC):
                                last = nc.tensor.transpose(pt[t % 2][:, c * P:(c + 1) * P], y[:, t, c * P:(c + 1) * P], ident[:, :])
                            last.then_inc(s_yT_ps, 1)
                        if t >= 1:
                            u = t - 1
                            pe.wait_ge(s_yT, u + 1)
                            for c in range(KC):
                                last = nc.tensor.matmul(pl[:, u * E:(u + 1) * E], yT[:, u % 2, c, :], gate[:, c, :],
                                                        start=(c == 0), stop=(c == KC - 1))
                            last.then_inc(s_l, 1)
                    pe.wait_ge(s_tri, 3)
                    pe.wait_ge(s_both, 1)
                    flat = both[:, :, :].rearrange("p t e -> p (t e)")
                    nc.tensor.matmul(pa[:, 0:TT * E], below[:, :], flat, start=True, stop=True)
                    nc.tensor.matmul(pb[:, 0:TT * E], ones[:, :], flat, start=True, stop=True).then_inc(s_cnt, 1)
                    for k in range(2):
                        pe.wait_ge(s_in_row, k + 1)
                        pe.wait_ge(s_in_tile, k + 1)
                        pe.wait_ge(s_in_rows, k + 1)
                        for t in range(TT):
                            last = nc.tensor.matmul(pc[:, 0:2 * ST], in_row[:, k, t, :], in_col[:, k, t, ST:3 * ST],
                                                    start=(k == 0 and t == 0), stop=(k == 1 and t == TT - 1))
                    last.then_inc(s_held, 1)

                @block.vector
                def _(dve):
                    v = nc.vector
                    n = [0]

                    def step(ins):
                        n[0] += 1
                        ins.then_inc(s_step, 1)
                        dve.wait_ge(s_step, n[0])

                    for t in range(TT):
                        if t % 11 == 0:
                            dve.wait_ge(s_h[t // 11], 16)
                        v.bn_stats(st[:, t, :], res[:, t, :]).then_inc(s_st, 1)
                    for t in range(TT):
                        dve.wait_ge(s_st, t + 1)
                        v.bn_aggr(mv[:, t, :], st[:, t, :]).then_inc(s_mv, 1)
                    dve.wait_ge(s_mv, TT)
                    step(v.tensor_scalar(va[:, :], mv[:, :, 1], 1e-5, None, ALU.add))
                    v.tensor_copy(r1[:, :], va[:, :]).then_inc(s_v, 1)
                    step(v.reciprocal(va[:, :], va[:, :]))
                    step(v.tensor_tensor(va[:, :], va[:, :], mv[:, :, 1], ALU.mult))
                    v.tensor_scalar(r2[:, :], va[:, :], 1e-6, None, ALU.add).then_inc(s_v, 1)
                    dve.wait_ge(s_sd, 2)
                    step(v.reciprocal(r1[:, :], r1[:, :]))
                    step(v.reciprocal(r2[:, :], r2[:, :]))
                    v.scalar_tensor_tensor(shift[:, :], mv[:, :, 0], -1.0, r1[:, :], ALU.mult, ALU.mult).then_inc(s_shiftc, 1)
                    dve.wait_ge(s_c, 32)
                    for t in range(TT):
                        dve.wait_ge(s_x1, t + 1)
                        v.scalar_tensor_tensor(y[:, t, :], x1[:, t % RX, :], r2[:, t:t + 1], rms[:, :],
                                               ALU.mult, ALU.mult).then_inc(s_y, 1)
                    dve.wait_ge(s_l, TT)
                    v.tensor_copy(logit[:, :, :].rearrange("p t e -> p (t e)"), pl[:, 0:TT * E]).then_inc(s_lg, 1)
                    dve.wait_ge(s_lg, 1)
                    for t in range(TT):
                        v.max(top[:, t, :], logit[:, t, :]).then_inc(s_top, 1)
                    for t in range(TT):
                        dve.wait_ge(s_top, t + 1)
                        v.max_index(topi[:, t, :], top[:, t, :], logit[:, t, :]).then_inc(s_top, 1)
                    dve.wait_ge(s_top, 2 * TT)
                    v.tensor_tensor(ex[:, :], top[:, :, 1], top[:, :, 0], ALU.subtract).then_inc(s_d, 1)
                    dve.wait_ge(s_io, 1)
                    v.tensor_copy(topf[:, :, :], topi[:, :, 0:2])
                    step(v.tensor_copy(io[:, :], io_i[:, :]))
                    for k in range(2):
                        step(v.tensor_tensor(pick[:, k, :, :], io[:, 0:E].unsqueeze(1).to_broadcast([P, TT, E]),
                                             topf[:, :, k].unsqueeze(2).to_broadcast([P, TT, E]), ALU.is_equal))
                    v.tensor_tensor(both[:, :, :], pick[:, 0, :, :], pick[:, 1, :, :], ALU.add).then_inc(s_both, 1)
                    dve.wait_ge(s_ex, 1)
                    step(v.tensor_scalar(wts[:, 0, :], ex[:, :], 1.0, None, ALU.add))
                    step(v.reciprocal(wts[:, 0, :], wts[:, 0, :]))
                    step(v.tensor_tensor(wts[:, 1, :], ex[:, :], wts[:, 0, :], ALU.mult))
                    dve.wait_ge(s_cnt, 1)
                    step(v.tensor_copy(tot[:, :, :], pb[:, 0:TT * E].rearrange("p (t e) -> p e t", e=E)))
                    for e in range(E):
                        step(v.tensor_tensor_scan(incl[:, e, :], ones[:, 0:TT], tot[:, e, :], 0.0, ALU.mult, ALU.add))
                    step(v.tensor_scalar(ownf[:, 0:LIST], io[:, 0:LIST], float(FT), None, ALU.mult))
                    step(v.tensor_tensor(over[:, :, :], incl[:, :, TT - 1].unsqueeze(2).to_broadcast([P, E, LIST]),
                                         ownf[:, 0:LIST].unsqueeze(1).to_broadcast([P, E, LIST]), ALU.is_gt))
                    step(v.tensor_reduce(tiles[:, :], over[:, :, :], AX.X, ALU.add))
                    step(v.tensor_tensor_scan(ends[:, :], ones[:, 0:E], tiles[:, :], 0.0, ALU.mult, ALU.add))
                    step(v.tensor_tensor(base[:, :], ends[:, :], tiles[:, :], ALU.subtract))
                    step(v.tensor_scalar(base[:, :], base[:, :], float(FT), None, ALU.mult))
                    step(v.tensor_tensor(incl[:, :, :], incl[:, :, :], tot[:, :, :], ALU.subtract))
                    step(v.tensor_tensor(place[:, :, :], pa[:, 0:TT * E].rearrange("p (t e) -> p t e", e=E),
                                         incl[:, :, :].rearrange("p e t -> p t e"), ALU.add))
                    step(v.tensor_tensor(place[:, :, :], place[:, :, :], base[:, :].unsqueeze(1).to_broadcast([P, TT, E]), ALU.add))
                    dve.wait_ge(s_seq, 4)
                    step(v.tensor_copy(seq[:, :, :], seq_i[:, :, :]))
                    for k in range(2):
                        step(v.tensor_scalar(num[:, k, :], seq[:, 0, 0:TT], 1.0 + k * TT, None, ALU.add))
                    for k in range(2):
                        step(v.tensor_tensor(work[:, k, :, :], pick[:, k, :, :], place[:, :, :], ALU.mult))
                        step(v.tensor_reduce(slotf[:, k, :], work[:, k, :, :], AX.X, ALU.add))
                        step(v.tensor_copy(slot_i[:, k, :], slotf[:, k, :]))
                        step(v.tensor_scalar(slot_i[:, k, :], slot_i[:, k, :], P - 1, None, ALU.bitwise_and))
                        step(v.tensor_copy(s_row[:, k, :], slot_i[:, k, :]))
                        step(v.tensor_tensor(s_col[:, k, :], slotf[:, k, :], s_row[:, k, :], ALU.subtract))
                        v.tensor_tensor(in_col[:, k, :, 0:ST], seq[:, 1, 0:ST].unsqueeze(1).to_broadcast([P, TT, ST]),
                                        s_col[:, k, :].unsqueeze(2).to_broadcast([P, TT, ST]), ALU.is_equal).then_inc(s_in_col, 1)
                        v.tensor_tensor(in_row[:, k, :, :], seq[:, 0, :].unsqueeze(1).to_broadcast([P, TT, P]),
                                        s_row[:, k, :].unsqueeze(2).to_broadcast([P, TT, P]), ALU.is_equal).then_inc(s_in_row, 1)
                    step(v.tensor_tensor(owns[:, :, :], io[:, 0:ETILES].unsqueeze(2).to_broadcast([P, ETILES, E]),
                                         ends[:, :].unsqueeze(1).to_broadcast([P, ETILES, E]), ALU.is_ge))
                    step(v.tensor_reduce(ownf[:, :], owns[:, :, :], AX.X, ALU.add))
                    step(v.tensor_scalar(owner[:, :], ownf[:, :], float(E - 1), None, ALU.min))
                    dve.wait_ge(s_held, 1)
                    step(v.tensor_scalar(held[:, :], pc[:, 0:ST], float(P), None, ALU.mult))
                    step(v.tensor_tensor(held[:, :], held[:, :], pc[:, ST:2 * ST], ALU.add))
                    step(v.tensor_scalar(real[:, :], held[:, :], float(P), None, ALU.is_lt))
                    step(v.tensor_scalar(held[:, :], held[:, :], -float(P), None, ALU.add))
                    step(v.tensor_scalar(dump[:, :], seq[:, 2, 0:ST], float(P), None, ALU.add))
                    step(v.tensor_tensor(dump[:, :], dump[:, :], real[:, :], ALU.mult))
                    step(v.tensor_tensor(target[:, :], held[:, :], dump[:, :], ALU.add))
                    step(v.tensor_scalar(real[:, :], held[:, :], float(TOK), -float(TOK), ALU.is_ge, ALU.mult))
                    step(v.tensor_tensor(held[:, :], held[:, :], real[:, :], ALU.add))
                    step(v.tensor_scalar(source[:, :], held[:, :], 0.0, None, ALU.max))

        f32r = mybir.dt.float32r
        CT = FT // P
        with ExitStack() as ctx:
            sb, bank, sem = G["tools"](ctx)
            w12 = sb("w12", [P, KC, 2 * DE])
            w3 = sb("w3", [P, MC + 1, DM])
            w12h, w12l = sb("w12h", [P, 2, KC, 2 * DE], f32r), sb("w12l", [P, 2, KC, 2 * DE], f32r)
            w3h, w3l = sb("w3h", [P, 2, MC + 1, DM], f32r), sb("w3l", [P, 2, MC + 1, DM], f32r)
            yb = sb("yb", [P, 2, CT, DM])
            yh, yl = sb("yh", [P, KC, FT], f32r), sb("yl", [P, KC, FT], f32r)
            silu = sb("silu", [P, 2, FT])
            prod = sb("prod", [P, 2, FT])
            hh, hl = sb("hh", [P, MC + 1, FT], f32r), sb("hl", [P, MC + 1, FT], f32r)
            ob = sb("ob", [P, CT, DM])
            source_now = sb("source_now", [P, 2, CT], u32)
            target_now = sb("target_now", [P, 2, CT], u32)
            pT = [bank(f"e_pT{i}") for i in range(2)]
            pu = [bank(f"e_pu{i}") for i in range(2)]
            pg = [bank(f"e_pg{i}") for i in range(2)]
            pd = [bank(f"e_pd{i}") for i in range(2)]
            s_w, s_y = ([sem(f"e_{n}{i}") for i in range(2)] for n in "wy")
            s_start, s_passed, s_out, s_source, s_target = sem("e_start"), sem("e_passed"), sem("e_out"), sem("e_source"), sem("e_target")
            s_T, s_yh, s_yl, s_up, s_silu, s_prod, s_hh, s_hl, s_dn, s_ob, s_o, s_wh, s_wl = (
                sem(f"e_{n}") for n in ("T", "yh", "yl", "up", "silu", "prod", "hh", "hl", "dn", "ob", "o", "wh", "wl"))
            UP = MC + 1
            DN = CT // 2
            PARTS = KC + 1

            def weight_part(q, par):
                if q < KC:
                    return w12[:, q, :], w12h[:, par, q, :], w12l[:, par, q, :]
                return w3[:, :, :], w3h[:, par, :, :], w3l[:, par, :, :]

            class Tile:
                def __init__(self, i, k):
                    self.i, self.k, self.j, self.par, self.half = i, k, 2 * i + k, k % 2, i + k // 2

                def next(self):
                    return Tile(self.i, self.k + 1)

            def tiles_of(engine):
                with engine.Fori(0, ETILES // 2 - 1) as i:
                    yield Tile(i, 0), False
                    yield Tile(i, 1), False
                yield Tile(ETILES // 2 - 1, 0), False
                yield Tile(ETILES // 2 - 1, 1), True

            CH, CD, CU, CO, CY = 2 * UP, 2 * DN, 2 * UP, 2, 2

            with nc.Block() as block:
                @block.sync
                def _(sp):
                    def load(T):
                        e = sp.value_load(owner[0:1, bass.ds(T.j, 1)], min_val=0, max_val=E - 1)
                        wait_alone(sp, s_wl, PARTS + PARTS * T.j, s_start)
                        sp.dma_start(w12[:, :, :], A["W12"][bass.ds(e, 1), :, :].rearrange("a (c p) n -> p (a c) n", p=P))\
                            .then_inc(s_w[T.par], 16)
                        sp.dma_start(w3[:, 0:MC, :], A["W3"][bass.ds(e, 1), 0:MC * P, :].rearrange("a (c p) n -> p (a c) n", p=P))\
                            .then_inc(s_w[T.par], 16)
                        sp.dma_start(w3[0:MR, MC, :], A["W3"][bass.ds(e, 1), MC * P:DE, :].rearrange("a p n -> (a p) n"))\
                            .then_inc(s_w[T.par], 16)

                    sp.wait_ge(s_start, 1)
                    load(Tile(0, 0))
                    for T, last in tiles_of(sp):
                        if not last:
                            load(T.next())

                @block.gpsimd
                def _(pool):
                    pool.memset(w3[:, MC, :], 0.0).then_inc(s_start, 1)
                    pool.sem_inc(s_wl, PARTS)
                    pool.sem_inc(s_out, CO)

                    def split(T):
                        for q in range(PARTS):
                            raw, high, low = weight_part(q, T.par)
                            pool.wait_ge(s_wh, PARTS * T.j + q + 1)
                            pool.tensor_tensor(low, raw, high.bitcast(f32), ALU.subtract).then_inc(s_wl, 1)

                    def gather(T):
                        pool.wait_ge(s_source, T.j + 1)
                        pool.wait_ge(s_T, CY + T.j - 1)
                        pool.sem_inc(s_passed, 1)
                        for c in range(CT):
                            pool.indirect_dma_start(out=yb[:, T.par, c, :], out_offset=None, in_=y_rows,
                                                    in_offset=bass.IndirectOffsetOnAxis(ap=source_now[:, T.par, c:c + 1], axis=0))\
                                .then_inc(s_y[T.par], 16)

                    def scatter(T):
                        pool.wait_ge(s_target, T.j + 1)
                        for q in range(DN):
                            pool.wait_ge(s_ob, CD + DN * T.j + q + 1)
                            pool.sem_inc(s_passed, 1)
                            for c in (2 * q, 2 * q + 1):
                                pool.indirect_dma_start(out=o_rows, in_=ob[:, c, :], in_offset=None,
                                                        out_offset=bass.IndirectOffsetOnAxis(ap=target_now[:, T.par, c:c + 1], axis=0))\
                                    .then_inc(s_o, 16)
                        pool.wait_ge(s_o, (T.j + 1) * CT * 16)
                        pool.sem_inc(s_out, 1)

                    pool.wait_ge(s_start, 1)
                    gather(Tile(0, 0))
                    split(Tile(0, 0))
                    for T, last in tiles_of(pool):
                        if not last:
                            gather(T.next())
                            split(T.next())
                        scatter(T)

                @block.tensor
                def _(pe):
                    pe.sem_inc(s_dn, CD)
                    pe.sem_inc(s_up, CU)
                    pe.sem_inc(s_T, CY)

                    def turn(T):
                        pe.wait_ge(s_y[T.par], (T.half + 1) * 16 * CT)
                        pe.wait_ge(s_yl, 1 + T.j)
                        for c in range(KC):
                            for k in range(CT):
                                last = nc.tensor.transpose(pT[c][:, k * P:(k + 1) * P], yb[:, T.par, k, c * P:(c + 1) * P],
                                                           ident[:, :])
                        last.then_inc(s_T, 1)

                    def passes(out, pairs):
                        n = len(pairs)
                        for g, (w, x) in enumerate(pairs):
                            last = nc.tensor.matmul(out, w, x, start=(g == 0), stop=(g == n - 1))
                        return last

                    turn(Tile(0, 0))
                    for T, is_last in tiles_of(pe):
                        par, j = T.par, T.j
                        pe.wait_ge(s_yl, 2 + j)
                        pe.wait_ge(s_wl, PARTS * (j + 2))
                        for m in range(UP):
                            b = m % 2
                            pe.wait_ge(s_prod, CH + UP * j + m - 1)
                            outs = ((pu[b], m), (pg[b], MC + m)) if m < MC else ((pu[b], 2 * MC),)
                            for o, q in outs:
                                cols = slice(q * P, (q + 1) * P)
                                last = passes(o[:, 0:FT], [x for c in range(KC) for x in (
                                    (w12h[:, par, c, cols], yh[:, c, :]), (w12h[:, par, c, cols], yl[:, c, :]),
                                    (w12l[:, par, c, cols], yh[:, c, :]))])
                            last.then_inc(s_up, 1)
                        if not is_last:
                            turn(T.next())
                        early, late, every = range(MC - 1), range(MC - 1, MC + 1), range(MC + 1)
                        for k, chunks in ((0, early), (2, early), (0, late), (1, every), (2, late), (3, every)):
                            if k % 2 == 0:
                                whole = chunks[0] == 0
                                pe.wait_ge(s_hl, CH + UP * (j + 1) - (2 if whole else 0))
                                if whole:
                                    pe.wait_ge(s_ob, CD + DN * j + k // 2 - 1)
                            toks = slice(k * P, (k + 1) * P)
                            for m in chunks:
                                r = P if m < MC else MR
                                for g, (h, w) in enumerate(((hh, w3h), (hh, w3l), (hl, w3h))):
                                    last = nc.tensor.matmul(pd[k // 2][:, (k % 2) * DM:(k % 2 + 1) * DM], h[0:r, m, toks],
                                                            w[0:r, par, m, :], start=(m == 0 and g == 0), stop=(m == MC and g == 2))
                            if k % 2:
                                last.then_inc(s_dn, 1)

                @block.scalar
                def _(act):
                    act.sem_inc(s_ob, CD)

                    def round_weights(T, q):
                        if q == 0:
                            act.wait_ge(s_w[T.par], (T.half + 1) * 48)
                        act.wait_ge(s_dn, CD + DN * (T.j - 1))
                        raw, high, low = weight_part(q, T.par)
                        nc.scalar.activation(high, raw, ACT.Copy).then_inc(s_wh, 1)

                    def round_rows(T):
                        act.wait_ge(s_T, CY + T.j + 1)
                        act.wait_ge(s_up, CU + UP * T.j)
                        for c in range(KC):
                            nc.scalar.activation(yh[:, c, :], pT[c][:, 0:FT], ACT.Copy).then_inc(s_yh, 1)

                    T0 = Tile(0, 0)
                    for q in range(PARTS):
                        round_weights(T0, q)
                    round_rows(T0)
                    for T, last in tiles_of(act):
                        j = T.j
                        for m in range(UP + 1):
                            if m < UP:
                                act.wait_ge(s_up, CU + UP * j + m + 1)
                                act.wait_ge(s_prod, CH + UP * j + m - 1)
                                r = P if m < MC else MR
                                nc.scalar.activation(silu[0:r, m % 2, :], pu[m % 2][0:r, 0:FT], ACT.Silu).then_inc(s_silu, 1)
                            if m >= 1:
                                u = m - 1
                                r = P if u < MC else MR
                                act.wait_ge(s_prod, CH + UP * j + u + 1)
                                if u == 0:
                                    act.wait_ge(s_dn, CD + DN * j)
                                nc.scalar.activation(hh[0:r, u, :], prod[0:r, u % 2, :], ACT.Copy).then_inc(s_hh, 1)
                            if not last and m in (1, 2, 3):
                                round_weights(T.next(), m - 1)
                        if not last:
                            round_rows(T.next())
                        act.wait_ge(s_out, CO + j)
                        for q in range(DN):
                            act.wait_ge(s_dn, CD + DN * j + q + 1)
                            nc.scalar.activation(ob[:, 2 * q:2 * q + 2, :], pd[q][:, :].rearrange("p (k n) -> p k n", k=2),
                                                 ACT.Copy).then_inc(s_ob, 1)

                @block.vector
                def _(dve):
                    v = nc.vector
                    dve.sem_inc(s_prod, CH)
                    dve.sem_inc(s_hl, CH)
                    dve.sem_inc(s_yl, 1)

                    def rest_rows(T):
                        for c in range(KC):
                            dve.wait_ge(s_yh, KC * T.j + c + 1)
                            last = v.tensor_tensor(yl[:, c, :], pT[c][:, 0:FT], yh[:, c, :].bitcast(f32), ALU.subtract)
                        last.then_inc(s_yl, 1)

                    def source_of(T):
                        dve.wait_ge(s_T, CY + T.j - 1)
                        v.tensor_copy(source_now[:, T.par, :], source[:, bass.ds(T.j * CT, CT)]).then_inc(s_source, 1)

                    def target_of(T):
                        dve.wait_ge(s_out, CO + T.j - 1)
                        v.tensor_copy(target_now[:, T.par, :], target[:, bass.ds(T.j * CT, CT)]).then_inc(s_target, 1)

                    source_of(Tile(0, 0))
                    rest_rows(Tile(0, 0))
                    for T, last in tiles_of(dve):
                        j = T.j
                        if not last:
                            source_of(T.next())
                        for m in range(UP + 1):
                            if m == 4:
                                target_of(T)
                            if m < UP:
                                dve.wait_ge(s_silu, UP * j + m + 1)
                                dve.wait_ge(s_hl, CH + UP * j + m - 1)
                                r = P if m < MC else MR
                                g = pg[m % 2][:, 0:FT] if m < MC else pu[m % 2][MR:2 * MR, 0:FT]
                                v.tensor_tensor(prod[0:r, m % 2, :], g, silu[0:r, m % 2, :], ALU.mult).then_inc(s_prod, 1)
                            if m >= 1:
                                u = m - 1
                                r = P if u < MC else MR
                                dve.wait_ge(s_hh, UP * j + u + 1)
                                v.tensor_tensor(hl[0:r, u, :], prod[0:r, u % 2, :], hh[0:r, u, :].bitcast(f32), ALU.subtract)\
                                    .then_inc(s_hl, 1)
                        if not last:
                            rest_rows(T.next())

        with ExitStack() as ctx:
            sb, _, sem = G["tools"](ctx)
            PART = 11
            PARTS = [(lo, min(lo + PART, TT)) for lo in range(0, TT, PART)]
            got = sb("got", [P, 2, TT, DM])
            s_g = [sem(f"c_g{i}") for i in range(len(PARTS))]
            s_first, s_sum, s_both, s_out = sem("c_first"), sem("c_sum"), sem("c_both"), sem("c_out")
            out_rows = A["out"].rearrange("b t c -> (b t) c").rearrange("(t p) n -> p t n", p=P)
            with nc.Block() as block:
                @block.sync
                def _(sp):
                    for i, (lo, hi) in enumerate(PARTS):
                        for k in range(2):
                            rows = o_rows[k * TOK + lo * P:k * TOK + hi * P, :]
                            sp.dma_start(got[:, k, lo:hi, :], rows.rearrange("(t p) n -> p t n", p=P)).then_inc(s_g[i], 16)
                    for lo, hi in PARTS:
                        sp.wait_ge(s_both, hi)
                        sp.dma_start(out_rows[:, lo:hi, :], res[:, lo:hi, :]).then_inc(s_out, 16)
                    sp.wait_ge(s_out, len(PARTS) * 16)

                @block.scalar
                def _(act):
                    for i, (lo, hi) in enumerate(PARTS):
                        act.wait_ge(s_g[i], 32)
                        for t in range(lo, hi):
                            nc.scalar.activation(got[:, 0, t, :], got[:, 0, t, :], ACT.Copy, scale=wts[:, 0, t:t + 1])\
                                .then_inc(s_first, 1)

                @block.gpsimd
                def _(pool):
                    for lo in range(0, TT, 2):
                        hi = min(lo + 2, TT)
                        pool.wait_ge(s_first, hi)
                        pool.tensor_tensor(res[:, lo:hi, :], res[:, lo:hi, :], got[:, 0, lo:hi, :], ALU.add).then_inc(s_sum, 1)

                @block.vector
                def _(dve):
                    for i, (lo, hi) in enumerate(PARTS):
                        dve.wait_ge(s_g[i], 32)
                        for t in range(lo, hi):
                            dve.wait_ge(s_sum, t // 2 + 1)
                            nc.vector.scalar_tensor_tensor(res[:, t, :], got[:, 1, t, :], wts[:, 1, t:t + 1], res[:, t, :],
                                                           ALU.mult, ALU.add).then_inc(s_both, 1)


def layouts(i):
    g = {k: np.asarray(a) for k, a in i.items()}
    rows = lambda a, n=P: np.ascontiguousarray(np.broadcast_to(a[None, :], (n, a.shape[0])))
    x = g["x"].reshape(BATCH, CHANS, SIDE, PATCH, SIDE, PATCH).transpose(0, 2, 4, 1, 3, 5)
    yy, xx = np.meshgrid(np.arange(SIDE, dtype=np.float32), np.arange(SIDE, dtype=np.float32), indexing="ij")
    omega = np.arange(DM // 4, dtype=np.float32) / np.float32(DM // 4 - 1)
    omega = (np.float32(1.0) / np.float32(10000.0) ** omega).astype(np.float32)
    yy, xx = yy.reshape(-1)[:, None] * omega[None, :], xx.reshape(-1)[:, None] * omega[None, :]
    pos = np.concatenate([np.sin(xx), np.cos(xx), np.sin(yy), np.cos(yy)], axis=1).astype(np.float32)
    seq = np.concatenate([np.arange(NI, SEQ), np.arange(NI)])
    rel = np.clip(seq[:, None] - seq[None, :] + SEQ - 1, 0, TABLE - 1)
    by_head = g["L0_attn_bias_table"][rel].transpose(2, 0, 1)
    bias = np.zeros((P, PAIRS, 3, SEQ), np.float32)
    bias[:, :, 0] = by_head[0::2, :NT].transpose(1, 0, 2)
    bias[:, :, 1] = by_head[1::2, :NT].transpose(1, 0, 2)
    bias[0:NI, :, 2] = by_head[0::2, NT:].transpose(1, 0, 2)
    bias[64:64 + NI, :, 2] = by_head[1::2, NT:].transpose(1, 0, 2)
    w1, w2 = g["L0_ffn_W1"].transpose(0, 2, 1), g["L0_ffn_W2"].transpose(0, 2, 1)
    w12 = np.concatenate([w1[:, :, :MC * P], w2[:, :, :MC * P], w1[:, :, MC * P:], w2[:, :, MC * P:]], axis=2)
    return {
        "patches": np.ascontiguousarray(x.reshape(BATCH * NI, FEAT)),
        "txt": g["txt"],
        "ln1_w": np.ascontiguousarray(g["L0_tok_ln1_w"].reshape(FC, P).T),
        "ln2_w": rows(g["L0_tok_ln2_w"]),
        "tokW": np.ascontiguousarray(g["L0_tok_W"].T),
        "pos": np.ascontiguousarray(np.tile(pos, (BATCH, 1))),
        "Wq": g["L0_attn_Wq"], "Wk": g["L0_attn_Wk"], "Wv": g["L0_attn_Wv"], "Wp": g["L0_attn_Wp"],
        "bq": np.ascontiguousarray(g["L0_attn_bq"].reshape(KC, P).T),
        "bk": np.ascontiguousarray(g["L0_attn_bk"].reshape(KC, P).T),
        "bv": rows(np.concatenate([g["L0_attn_bv"]] * 2)),
        "bp": rows(g["L0_attn_bp"]),
        "bias": bias,
        "temp": rows(g["L0_attn_temperature"]),
        "gate": np.ascontiguousarray(g["L0_ffn_gate_w"].T),
        "rms_w": rows(g["L0_ffn_rms_w"]),
        "W12": np.ascontiguousarray(w12),
        "W3": np.ascontiguousarray(g["L0_ffn_W3"].transpose(0, 2, 1)),
    }


def kernel(**inputs):
    import concourse.bacc as bacc
    from concourse.bass_utils import run_bass_kernel_spmd as run

    nc = bacc.Bacc("TRN2", target_bir_lowering=False, num_devices=1)
    arrays, aps = {}, {}
    for name, a in layouts(inputs).items():
        arrays[f"in_{name}"] = np.ascontiguousarray(a)
        aps[name] = nc.dram_tensor(f"in_{name}", a.shape, mybir.dt.from_np(a.dtype), kind="ExternalInput").ap()
    aps["out"] = nc.dram_tensor("out_0", (BATCH, SEQ, DM), mybir.dt.float32, kind="ExternalOutput").ap()
    build(nc, aps)
    r = run(nc, [arrays], core_ids=[0])
    return r.results[0]["out_0"]
```
